# Optimizing a Trainium2 kernel written in Bass

```python
import numpy as np
import jax
import jax.numpy as jnp

def _softmax(x, axis=-1):
    return jax.nn.softmax(x, axis=axis)

def _gelu(x):
    return jax.nn.gelu(x, approximate=True)

def _silu(x):
    return jax.nn.silu(x)

def _sigmoid(x):
    return jax.nn.sigmoid(x)

def _layernorm(x, axis=-1, eps=1e-05):
    m = jnp.mean(x, axis=axis, keepdims=True)
    v = jnp.var(x, axis=axis, keepdims=True)
    return (x - m) / jnp.sqrt(v + eps)

def _scatter_add(tgt, idx, src, axis=0):
    return tgt.at[idx].add(src)

def _segment_sum(src, seg, n):
    return jax.ops.segment_sum(src, seg, n)
kernel_name = 'mk_macaron_d2_jaxref_r8_3b9ef0'

def setup_inputs(seed: int=0):
    np.random.seed(seed)
    _w = jnp.asarray

    def _L0_attn_setup():
        import jax, jax.numpy as jnp
        import numpy as np
        N_EMBD = 256
        N_HEAD = 16
        D_HEAD = N_EMBD // N_HEAD
        B, T = (2, 256)
        ROPE_BASE = 10000.0

        def _rope_cos_sin(T, d, dtype):
            inv_freq = 1.0 / ROPE_BASE ** (jnp.arange(0, d, 2, dtype=jnp.float32) / d)
            ang = jnp.arange(T, dtype=jnp.float32)[:, None] * inv_freq[None, :]
            cos = jnp.concatenate([jnp.cos(ang), jnp.cos(ang)], axis=-1).astype(dtype)
            sin = jnp.concatenate([jnp.sin(ang), jnp.sin(ang)], axis=-1).astype(dtype)
            return (cos, sin)

        def _rotate_half(x):
            d = x.shape[-1] // 2
            return jnp.concatenate([-x[..., d:], x[..., :d]], axis=-1)
        key = jax.random.key(seed)
        k1, k2, k3 = jax.random.split(key, 3)
        x = jax.random.normal(k1, (B, T, N_EMBD), dtype=jnp.float32)
        w_qkv = jax.random.normal(k2, (3 * N_EMBD, N_EMBD), dtype=jnp.float32) * 0.02
        w_proj = jax.random.normal(k3, (N_EMBD, N_EMBD), dtype=jnp.float32) * 0.02
        return {'x': x, 'w_qkv': w_qkv, 'w_proj': w_proj}
    _L0_attn_in = _L0_attn_setup()

    def _L0_ffn_setup():
        import jax, jax.numpy as jnp
        import numpy as np
        E = 64
        K = 6
        CAP = 64
        SCALE = 1.0
        H = 256
        I = 96
        SI = I * 2
        B, S = (2, 128)

        def _moe(x, gate_w, gate_up_proj, down_proj, shared_gate_w, shared_up_w, shared_down_w):
            b, s, h = x.shape
            T = b * s
            xf = x.reshape(T, h)
            scores = jax.nn.softmax(xf @ gate_w.T, axis=-1)
            topk_w, topk_idx = jax.lax.top_k(scores, K)
            topk_w = topk_w * SCALE
            flat_e = topk_idx.reshape(-1)
            order = jnp.argsort(flat_e)
            sorted_e = flat_e[order]
            sorted_tok = (order // K).astype(jnp.int32)
            sorted_w = topk_w.reshape(-1)[order]
            counts = jnp.zeros((E,), jnp.int32).at[flat_e].add(1)
            offsets = jnp.cumsum(counts) - counts
            pos = jnp.arange(T * K, dtype=jnp.int32) - offsets[sorted_e]
            buf_tok = jnp.full((E, CAP), T, jnp.int32).at[sorted_e, pos].set(sorted_tok, mode='drop')
            buf_w = jnp.zeros((E, CAP), x.dtype).at[sorted_e, pos].set(sorted_w, mode='drop')
            xp = jnp.concatenate([xf, jnp.zeros((1, h), x.dtype)], axis=0)
            gx = xp[buf_tok]
            gu = jnp.einsum('ech,ehi->eci', gx, gate_up_proj)
            g, u = jnp.split(gu, 2, axis=-1)
            hid = jax.nn.silu(g) * u
            eo = jnp.einsum('eci,eih->ech', hid, down_proj) * buf_w[..., None]
            routed = jnp.zeros((T + 1, h), x.dtype).at[buf_tok.reshape(-1)].add(eo.reshape(-1, h))[:T]
            shared = jax.nn.silu(xf @ shared_gate_w.T) * (xf @ shared_up_w.T) @ shared_down_w.T
            return (routed + shared).reshape(b, s, h)
        key = jax.random.key(seed)
        ks = jax.random.split(key, 7)
        x = jax.random.normal(ks[0], (B, S, H), jnp.float32)
        gate_w = jax.random.normal(ks[1], (E, H), jnp.float32) * 0.02
        gate_up_proj = jax.random.normal(ks[2], (E, H, 2 * I), jnp.float32) * 0.02
        down_proj = jax.random.normal(ks[3], (E, I, H), jnp.float32) * 0.02
        shared_gate_w = jax.random.normal(ks[4], (SI, H), jnp.float32) * 0.02
        shared_up_w = jax.random.normal(ks[5], (SI, H), jnp.float32) * 0.02
        shared_down_w = jax.random.normal(ks[6], (H, SI), jnp.float32) * 0.02
        return dict(x=x, gate_w=gate_w, gate_up_proj=gate_up_proj, down_proj=down_proj, shared_gate_w=shared_gate_w, shared_up_w=shared_up_w, shared_down_w=shared_down_w)
    _L0_ffn_in = _L0_ffn_setup()

    def _L1_attn_setup():
        import jax, jax.numpy as jnp
        import numpy as np
        N_Q, N_KV = (16, 4)

        def _rope(x):
            d = x.shape[-1]
            T = x.shape[-2]
            inv_freq = 1.0 / 10000.0 ** (jnp.arange(d // 2, dtype=jnp.float32) * 2.0 / d)
            emb = jnp.arange(T, dtype=jnp.float32)[:, None] * inv_freq[None, :]
            cos, sin = (jnp.cos(emb), jnp.sin(emb))
            x1, x2 = (x[..., 0::2], x[..., 1::2])
            return jnp.concatenate([x1 * cos - x2 * sin, x1 * sin + x2 * cos], axis=-1)
        key = jax.random.key(seed)
        ks = jax.random.split(key, 5)
        B, T, C = (4, 256, 256)
        g = N_Q // N_KV
        Ckv = C // g
        s = 0.02
        return {'x': jax.random.normal(ks[0], (B, T, C), dtype=jnp.float32), 'Wq': jax.random.normal(ks[1], (C, C), dtype=jnp.float32) * s, 'bq': jnp.zeros((C,), dtype=jnp.float32), 'Wk': jax.random.normal(ks[2], (C, Ckv), dtype=jnp.float32) * s, 'bk': jnp.zeros((Ckv,), dtype=jnp.float32), 'Wv': jax.random.normal(ks[3], (C, Ckv), dtype=jnp.float32) * s, 'bv': jnp.zeros((Ckv,), dtype=jnp.float32), 'Wo': jax.random.normal(ks[4], (Ckv, C), dtype=jnp.float32) * s, 'bo': jnp.zeros((C,), dtype=jnp.float32)}
    _L1_attn_in = _L1_attn_setup()

    def _L1_ffn_setup():
        import jax, jax.numpy as jnp
        import numpy as np
        import math
        B, S, D = (2, 256, 256)
        P = 4
        PW = 2
        L = 2
        STD = 0.02
        EPS = 1e-05

        def _layer_norm(x, g, b):
            m = jnp.mean(x, axis=-1, keepdims=True)
            v = jnp.mean(jnp.square(x - m), axis=-1, keepdims=True)
            return (x - m) * jax.lax.rsqrt(v + EPS) * g + b
        key = jax.random.key(seed)
        ks = jax.random.split(key, 16)
        n = lambda k, shape: jax.random.normal(k, shape, dtype=jnp.float32) * STD
        inp = {'x': jax.random.normal(ks[0], (B, S, D), dtype=jnp.float32), 'amp_w': n(ks[1], (D, D)), 'amp_b': jnp.zeros((D,), jnp.float32), 'ph_w': n(ks[2], (D, D)), 'ph_b': jnp.zeros((D,), jnp.float32), 'ent_w': n(ks[3], (L, D, P * D)), 'ent_b': jnp.zeros((L, P * D), jnp.float32), 'ent_pw': n(ks[4], (L, P * D, D)), 'ent_pb': jnp.zeros((L, D), jnp.float32), 'path_w': n(ks[5], (L, PW, D, D)), 'path_b': jnp.zeros((L, PW, D), jnp.float32), 'phase': jax.random.normal(ks[6], (L, PW, D), dtype=jnp.float32), 'ln3_g': jnp.ones((L, D), jnp.float32), 'ln3_b': jnp.zeros((L, D), jnp.float32), 'ln4_g': jnp.ones((L, D), jnp.float32), 'ln4_b': jnp.zeros((L, D), jnp.float32)}
        return inp
    _L1_ffn_in = _L1_ffn_setup()
    _d = {'L0_attn_x': _L0_attn_in['x'], 'L0_attn_w_qkv': _L0_attn_in['w_qkv'], 'L0_attn_w_proj': _L0_attn_in['w_proj'], 'L0_ffn_gate_w': _L0_ffn_in['gate_w'], 'L0_ffn_gate_up_proj': _L0_ffn_in['gate_up_proj'], 'L0_ffn_down_proj': _L0_ffn_in['down_proj'], 'L0_ffn_shared_gate_w': _L0_ffn_in['shared_gate_w'], 'L0_ffn_shared_up_w': _L0_ffn_in['shared_up_w'], 'L0_ffn_shared_down_w': _L0_ffn_in['shared_down_w'], 'L1_attn_Wq': _L1_attn_in['Wq'], 'L1_attn_bq': _L1_attn_in['bq'], 'L1_attn_Wk': _L1_attn_in['Wk'], 'L1_attn_bk': _L1_attn_in['bk'], 'L1_attn_Wv': _L1_attn_in['Wv'], 'L1_attn_bv': _L1_attn_in['bv'], 'L1_attn_Wo': _L1_attn_in['Wo'], 'L1_attn_bo': _L1_attn_in['bo'], 'L1_ffn_amp_w': _L1_ffn_in['amp_w'], 'L1_ffn_amp_b': _L1_ffn_in['amp_b'], 'L1_ffn_ph_w': _L1_ffn_in['ph_w'], 'L1_ffn_ph_b': _L1_ffn_in['ph_b'], 'L1_ffn_ent_w': _L1_ffn_in['ent_w'], 'L1_ffn_ent_b': _L1_ffn_in['ent_b'], 'L1_ffn_ent_pw': _L1_ffn_in['ent_pw'], 'L1_ffn_ent_pb': _L1_ffn_in['ent_pb'], 'L1_ffn_path_w': _L1_ffn_in['path_w'], 'L1_ffn_path_b': _L1_ffn_in['path_b'], 'L1_ffn_phase': _L1_ffn_in['phase'], 'L1_ffn_ln3_g': _L1_ffn_in['ln3_g'], 'L1_ffn_ln3_b': _L1_ffn_in['ln3_b'], 'L1_ffn_ln4_g': _L1_ffn_in['ln4_g'], 'L1_ffn_ln4_b': _L1_ffn_in['ln4_b']}
    _x0 = _d['L0_attn_x']
    _d['L0_attn_x'] = jax.random.normal(jax.random.fold_in(jax.random.key(seed), 1), (4, 256, 256), dtype=_x0.dtype)
    del _x0
    return _d

def reference(L0_attn_x, L0_attn_w_qkv, L0_attn_w_proj, L0_ffn_gate_w, L0_ffn_gate_up_proj, L0_ffn_down_proj, L0_ffn_shared_gate_w, L0_ffn_shared_up_w, L0_ffn_shared_down_w, L1_attn_Wq, L1_attn_bq, L1_attn_Wk, L1_attn_bk, L1_attn_Wv, L1_attn_bv, L1_attn_Wo, L1_attn_bo, L1_ffn_amp_w, L1_ffn_amp_b, L1_ffn_ph_w, L1_ffn_ph_b, L1_ffn_ent_w, L1_ffn_ent_b, L1_ffn_ent_pw, L1_ffn_ent_pb, L1_ffn_path_w, L1_ffn_path_b, L1_ffn_phase, L1_ffn_ln3_g, L1_ffn_ln3_b, L1_ffn_ln4_g, L1_ffn_ln4_b):

    def _L0_attn_ref(x, w_qkv, w_proj):
        import jax, jax.numpy as jnp
        import numpy as np
        N_EMBD = 256
        N_HEAD = 16
        D_HEAD = N_EMBD // N_HEAD
        B, T = (2, 256)
        ROPE_BASE = 10000.0

        def _rope_cos_sin(T, d, dtype):
            inv_freq = 1.0 / ROPE_BASE ** (jnp.arange(0, d, 2, dtype=jnp.float32) / d)
            ang = jnp.arange(T, dtype=jnp.float32)[:, None] * inv_freq[None, :]
            cos = jnp.concatenate([jnp.cos(ang), jnp.cos(ang)], axis=-1).astype(dtype)
            sin = jnp.concatenate([jnp.sin(ang), jnp.sin(ang)], axis=-1).astype(dtype)
            return (cos, sin)

        def _rotate_half(x):
            d = x.shape[-1] // 2
            return jnp.concatenate([-x[..., d:], x[..., :d]], axis=-1)
        Bq, Tq, C = x.shape
        H, D = (N_HEAD, D_HEAD)
        qkv = jnp.einsum('btc,fc->btf', x, w_qkv).reshape(Bq, Tq, 3, H, D)
        q, k, v = (qkv[:, :, 0], qkv[:, :, 1], qkv[:, :, 2])
        q = jnp.transpose(q, (0, 2, 1, 3))
        k = jnp.transpose(k, (0, 2, 1, 3))
        v = jnp.transpose(v, (0, 2, 1, 3))
        cos, sin = _rope_cos_sin(Tq, D, x.dtype)
        q = q * cos[None, None] + _rotate_half(q) * sin[None, None]
        k = k * cos[None, None] + _rotate_half(k) * sin[None, None]
        scale = 1.0 / jnp.sqrt(jnp.asarray(D, x.dtype))
        scores = jnp.einsum('bhqd,bhkd->bhqk', q, k) * scale
        causal = jnp.tril(jnp.ones((Tq, Tq), dtype=bool))
        scores = jnp.where(causal[None, None], scores, jnp.asarray(-jnp.inf, x.dtype))
        attn = jax.nn.softmax(scores, axis=-1)
        y = jnp.einsum('bhqk,bhkd->bhqd', attn, v)
        y = jnp.transpose(y, (0, 2, 1, 3)).reshape(Bq, Tq, C)
        y = jnp.einsum('btc,fc->btf', y, w_proj)
        return y

    def _L0_ffn_ref(x, gate_w, gate_up_proj, down_proj, shared_gate_w, shared_up_w, shared_down_w):
        import jax, jax.numpy as jnp
        import numpy as np
        E = 64
        K = 6
        CAP = 64
        SCALE = 1.0
        H = 256
        I = 96
        SI = I * 2
        B, S = (2, 128)

        def _moe(x, gate_w, gate_up_proj, down_proj, shared_gate_w, shared_up_w, shared_down_w):
            b, s, h = x.shape
            T = b * s
            xf = x.reshape(T, h)
            scores = jax.nn.softmax(xf @ gate_w.T, axis=-1)
            topk_w, topk_idx = jax.lax.top_k(scores, K)
            topk_w = topk_w * SCALE
            flat_e = topk_idx.reshape(-1)
            order = jnp.argsort(flat_e)
            sorted_e = flat_e[order]
            sorted_tok = (order // K).astype(jnp.int32)
            sorted_w = topk_w.reshape(-1)[order]
            counts = jnp.zeros((E,), jnp.int32).at[flat_e].add(1)
            offsets = jnp.cumsum(counts) - counts
            pos = jnp.arange(T * K, dtype=jnp.int32) - offsets[sorted_e]
            buf_tok = jnp.full((E, CAP), T, jnp.int32).at[sorted_e, pos].set(sorted_tok, mode='drop')
            buf_w = jnp.zeros((E, CAP), x.dtype).at[sorted_e, pos].set(sorted_w, mode='drop')
            xp = jnp.concatenate([xf, jnp.zeros((1, h), x.dtype)], axis=0)
            gx = xp[buf_tok]
            gu = jnp.einsum('ech,ehi->eci', gx, gate_up_proj)
            g, u = jnp.split(gu, 2, axis=-1)
            hid = jax.nn.silu(g) * u
            eo = jnp.einsum('eci,eih->ech', hid, down_proj) * buf_w[..., None]
            routed = jnp.zeros((T + 1, h), x.dtype).at[buf_tok.reshape(-1)].add(eo.reshape(-1, h))[:T]
            shared = jax.nn.silu(xf @ shared_gate_w.T) * (xf @ shared_up_w.T) @ shared_down_w.T
            return (routed + shared).reshape(b, s, h)
        return _moe(x, gate_w, gate_up_proj, down_proj, shared_gate_w, shared_up_w, shared_down_w)

    def _L1_attn_ref(x, Wq, bq, Wk, bk, Wv, bv, Wo, bo):
        import jax, jax.numpy as jnp
        import numpy as np
        N_Q, N_KV = (16, 4)

        def _rope(x):
            d = x.shape[-1]
            T = x.shape[-2]
            inv_freq = 1.0 / 10000.0 ** (jnp.arange(d // 2, dtype=jnp.float32) * 2.0 / d)
            emb = jnp.arange(T, dtype=jnp.float32)[:, None] * inv_freq[None, :]
            cos, sin = (jnp.cos(emb), jnp.sin(emb))
            x1, x2 = (x[..., 0::2], x[..., 1::2])
            return jnp.concatenate([x1 * cos - x2 * sin, x1 * sin + x2 * cos], axis=-1)
        B, T, C = x.shape
        g = N_Q // N_KV
        d = C // N_Q
        q = (x @ Wq + bq).reshape(B, T, N_Q, d).transpose(0, 2, 1, 3)
        k = (x @ Wk + bk).reshape(B, T, N_KV, d).transpose(0, 2, 1, 3)
        v = (x @ Wv + bv).reshape(B, T, N_KV, d).transpose(0, 2, 1, 3)
        q = _rope(q)
        k = _rope(k)
        qg = q.reshape(B, N_KV, g, T, d)
        scores = jnp.einsum('bhgnd,bhsd->bhns', qg, k) * (1.0 / jnp.sqrt(jnp.float32(d)))
        mask = jnp.tril(jnp.ones((T, T), dtype=bool))
        att = jax.nn.softmax(jnp.where(mask, scores, -jnp.inf), axis=-1)
        y = jnp.einsum('bhns,bhsd->bhnd', att, v)
        y = y.transpose(0, 2, 1, 3).reshape(B, T, C // g)
        return y @ Wo + bo

    def _L1_ffn_ref(x, amp_w, amp_b, ph_w, ph_b, ent_w, ent_b, ent_pw, ent_pb, path_w, path_b, phase, ln3_g, ln3_b, ln4_g, ln4_b):
        import jax, jax.numpy as jnp
        import numpy as np
        import math
        B, S, D = (2, 256, 256)
        P = 4
        PW = 2
        L = 2
        STD = 0.02
        EPS = 1e-05

        def _layer_norm(x, g, b):
            m = jnp.mean(x, axis=-1, keepdims=True)
            v = jnp.mean(jnp.square(x - m), axis=-1, keepdims=True)
            return (x - m) * jax.lax.rsqrt(v + EPS) * g + b
        amp = jax.nn.sigmoid(x @ amp_w + amp_b)
        ph = jnp.tanh(x @ ph_w + ph_b) * math.pi
        h = (jnp.cos(ph) + jnp.sin(ph)) * amp
        for l in range(L):
            e = h @ ent_w[l] + ent_b[l]
            ent = e @ ent_pw[l] + ent_pb[l]
            h = _layer_norm(h + ent, ln3_g[l], ln3_b[l])
            t = jnp.einsum('bsd,pdf->pbsf', h, path_w[l]) + path_b[l][:, None, None, :]
            mod = jnp.cos(phase[l]) + jnp.sin(phase[l])
            interf = jnp.sum(t * mod[:, None, None, :], axis=0)
            h = _layer_norm(h + interf, ln4_g[l], ln4_b[l])
        return h
    x = L0_attn_x
    x = x + 0.5 * _L0_ffn_ref(_layernorm(x, axis=-1), L0_ffn_gate_w, L0_ffn_gate_up_proj, L0_ffn_down_proj, L0_ffn_shared_gate_w, L0_ffn_shared_up_w, L0_ffn_shared_down_w)
    x = x + _L0_attn_ref(_layernorm(x, axis=-1), L0_attn_w_qkv, L0_attn_w_proj)
    x = x + 0.5 * _L0_ffn_ref(_layernorm(x, axis=-1), L0_ffn_gate_w, L0_ffn_gate_up_proj, L0_ffn_down_proj, L0_ffn_shared_gate_w, L0_ffn_shared_up_w, L0_ffn_shared_down_w)
    x = x + 0.5 * _L1_ffn_ref(_layernorm(x, axis=-1), L1_ffn_amp_w, L1_ffn_amp_b, L1_ffn_ph_w, L1_ffn_ph_b, L1_ffn_ent_w, L1_ffn_ent_b, L1_ffn_ent_pw, L1_ffn_ent_pb, L1_ffn_path_w, L1_ffn_path_b, L1_ffn_phase, L1_ffn_ln3_g, L1_ffn_ln3_b, L1_ffn_ln4_g, L1_ffn_ln4_b)
    x = x + _L1_attn_ref(_layernorm(x, axis=-1), L1_attn_Wq, L1_attn_bq, L1_attn_Wk, L1_attn_bk, L1_attn_Wv, L1_attn_bv, L1_attn_Wo, L1_attn_bo)
    x = x + 0.5 * _L1_ffn_ref(_layernorm(x, axis=-1), L1_ffn_amp_w, L1_ffn_amp_b, L1_ffn_ph_w, L1_ffn_ph_b, L1_ffn_ent_w, L1_ffn_ent_b, L1_ffn_ent_pw, L1_ffn_ent_pb, L1_ffn_path_w, L1_ffn_path_b, L1_ffn_phase, L1_ffn_ln3_g, L1_ffn_ln3_b, L1_ffn_ln4_g, L1_ffn_ln4_b)
    return x

_drawn_inputs = setup_inputs


def setup_inputs(seed=0):
    import zlib

    import numpy as np

    out = dict(_drawn_inputs(seed))
    spreads = {'L1_attn_bq': (0.0, 0.8),
     'L1_attn_bk': (0.0, 0.8),
     'L1_attn_bv': (0.0, 0.606),
     'L1_attn_bo': (0.0, 0.1),
     'L1_ffn_amp_b': (0.0, 0.323),
     'L1_ffn_ph_b': (0.0, 0.1),
     'L1_ffn_ent_b': (0.0, 0.1),
     'L1_ffn_ent_pb': (0.0, 0.1),
     'L1_ffn_path_b': (0.0, 0.1),
     'L1_ffn_ln3_g': (1.0, 0.2),
     'L1_ffn_ln3_b': (0.0, 0.1),
     'L1_ffn_ln4_g': (1.0, 0.2),
     'L1_ffn_ln4_b': (0.0, 0.1)}
    factors = {'L0_attn_w_proj': 2.774,
     'L0_ffn_gate_w': 8.0,
     'L0_ffn_gate_up_proj': 8.0,
     'L0_ffn_down_proj': 8.0,
     'L0_ffn_shared_gate_w': 3.815,
     'L0_ffn_shared_up_w': 3.753,
     'L0_ffn_shared_down_w': 3.728,
     'L1_attn_Wq': 8.0,
     'L1_attn_Wk': 8.0,
     'L1_attn_Wv': 5.334,
     'L1_attn_Wo': 3.13}
    for name, (base, spread) in spreads.items():
        noise = np.random.default_rng([zlib.crc32(name.encode()), seed]).standard_normal(out[name].shape)
        drawn = base * np.exp(spread * noise) if base else spread * noise
        out[name] = jnp.asarray(drawn.astype(out[name].dtype))
    for name, factor in factors.items():
        out[name] = (out[name] * factor).astype(out[name].dtype)
    return out
```

```python
from contextlib import ExitStack

import numpy as np
import concourse.bass as bass
from concourse import mybir

F32 = mybir.dt.float32
BF16 = mybir.dt.bfloat16
U32 = mybir.dt.uint32
ALU = mybir.AluOpType
ACT = mybir.ActivationFunctionType
AX = mybir.AxisListType

P = 128
D = 256
KC = D // P
B, T = 4, 256
TOK = B * T
TILES = TOK // P
TB = T // P
NE, TOPK, CAP, HID, SHID = 64, 6, 64, 96, 192
PAIRS = NE // 2
SLOTS = NE * CAP
H, DH = 16, 16
HKV = 4
EPS = 1e-5
NL = 2
PW = 2
EW = 4 * D
MASKED = -1.0e30
PI = float(np.pi)


def flat(buf, first, shape):
    n = int(np.prod(shape))
    v = buf[:, first:first + n]
    if len(shape) == 2:
        return v.rearrange("p (a b) -> p a b", b=shape[1])
    if len(shape) == 3:
        return v.rearrange("p (a b c) -> p a b c", b=shape[1], c=shape[2])
    if len(shape) == 4:
        return v.rearrange("p (a b c d) -> p a b c d", b=shape[1], c=shape[2], d=shape[3])
    return v


class Chain:

    def __init__(self, engine, sem):
        self.engine, self.sem, self.links = engine, sem, 0
        engine.sem_clear(sem)

    def __call__(self, instruction):
        instruction.then_inc(self.sem, 1)
        self.links += 1
        self.engine.wait_ge(self.sem, self.links)

    def count(self, instruction):
        instruction.then_inc(self.sem, 1)
        self.links += 1


class Places:
    pass


def allocate(nc, ctx):
    m = Places()

    def sb(name, shape, dt=F32):
        return ctx.enter_context(nc.sbuf_tensor(name, shape, dt))

    m.w_gu = sb("w_gu", [P, NE * KC * SHID])
    m.w_dn = sb("w_dn", [P, NE * D])
    m.x = sb("x", [P, TILES, D])
    m.ident = sb("ident", [P, P])
    m.ident_b = sb("ident_b", [P, P], BF16)
    m.before_b = sb("before_b", [P, P], BF16)
    m.ones_b = sb("ones_b", [P, P], BF16)
    m.causal_b = sb("causal_b", [P, P], BF16)
    m.expert_no = sb("expert_no", [P, NE])
    m.rope = sb("rope", [P, TB, 2, 2, DH])
    m.w_router = sb("w_router", [P, KC, NE])
    m.w_sgu = sb("w_sgu", [P, KC, 2 * SHID])
    m.w_sdn = sb("w_sdn", [HID, 2, D])
    m.w_qkv = sb("w_qkv", [P, KC, 3 * D])
    m.w_proj = sb("w_proj", [P, KC, D])
    m.slots = sb("slots", [P, TILES, TOPK], U32)
    m.weights = sb("weights", [P, TILES, TOPK])
    m.taken = sb("taken", [P, NE], BF16)
    m.cur_slots = sb("cur_slots", [P, TB * TOPK], U32)
    m.cur_weights = sb("cur_weights", [P, TB, TOPK])
    m.stats = sb("stats", [P, 4, 6])
    m.mv = sb("mv", [P, 4, 2])
    m.var_eps = sb("var_eps", [P, 4])
    m.rstd = sb("rstd", [P, 4])
    m.minus_half = sb("minus_half", [P, 4])
    m.xn = sb("xn", [P, TB, D])
    m.work = sb("work", [P, 3840])
    m.banks = ctx.enter_context(nc.psum_tensor("banks", [P, 8, 512], F32))
    m.expert_in = nc.dram_tensor("expert_in", [SLOTS, D], F32, kind="Internal").ap()
    m.expert_out = nc.dram_tensor("expert_out", [SLOTS + P, D], F32, kind="Internal").ap()
    return m



class NormSems:
    def __init__(self, sem, name):
        self.var = sem(f"{name}_variance_ready")
        self.rstd = sem(f"{name}_rstd_ready")
        self.xn = sem(f"{name}_normed_ready")
        self.turned = sem(f"{name}_transposed")
        self.xnT = sem(f"{name}_normed_T_ready")


def norm_vector(nc, m, eng, chain, s, turn, x_tiles, xn, tiles=TB):
    for t in range(tiles):
        chain(nc.vector.bn_stats(m.stats[:, t, :], x_tiles[t]))
    for t in range(tiles):
        chain(nc.vector.bn_aggr(m.mv[:, t, :], m.stats[:, t, :]))
    nc.vector.tensor_scalar(m.var_eps[:, 0:tiles], m.mv[:, 0:tiles, 1], EPS, None, ALU.add).then_inc(s.var, 1)
    eng.wait_ge(s.rstd, turn + 1)
    for t in range(tiles):
        nc.vector.tensor_scalar(xn[:, t, :], x_tiles[t], m.mv[:, t, 0:1], m.rstd[:, t:t + 1],
                                ALU.subtract, ALU.mult).then_inc(s.xn, 1)


def norm_pool(nc, m, eng, s, turn, tiles=TB):
    eng.wait_ge(s.var, turn + 1)
    nc.gpsimd.tensor_tensor(m.rstd[:, 0:tiles], m.var_eps[:, 0:tiles], m.minus_half[:, 0:tiles],
                            ALU.pow).then_inc(s.rstd, 1)


def norm_tensor(nc, m, eng, s, turn, xn, out, tiles=TB):
    for t in range(tiles):
        eng.wait_ge(s.xn, turn * tiles + (t + 1))
        for c in range(KC):
            last = nc.tensor.transpose(out[:, c, t * P:(t + 1) * P], xn[:, t, c * P:(c + 1) * P], m.ident[:, :])
    last.then_inc(s.turned, 1)


def norm_scalar(nc, eng, s, turn, src, dst):
    eng.wait_ge(s.turned, turn + 1)
    nc.scalar.copy(dst, src).then_inc(s.xnT, 1)


class RouteSems:
    def __init__(self, sem, name):
        self.logits = sem(f"{name}_logits_ready")
        self.shared_in = sem(f"{name}_shared_gate_up_ready")
        self.neg_max = sem(f"{name}_neg_max_ready")
        self.exps = sem(f"{name}_exps_ready")
        self.mask = sem(f"{name}_choice_mask_ready")
        self.rank = sem(f"{name}_rank_ready")
        self.slots = sem(f"{name}_slots_ready")
        self.scattered = sem(f"{name}_rows_scattered")
        self.tanh = sem(f"{name}_shared_tanh_ready")
        self.hidden = sem(f"{name}_shared_hidden_ready")
        self.turned = sem(f"{name}_shared_hidden_turned")
        self.hiddenT = sem(f"{name}_shared_hidden_T_ready")
        self.shared_out = sem(f"{name}_shared_out_ready")


class RoutePlaces:

    def __init__(self, m):
        w = m.work
        self.xnT = flat(w, 0, (KC, T))
        self.logits = flat(w, 512, (TB, NE))
        self.top = flat(w, 640, (TB, 8))
        self.neg_max = flat(w, 656, (TB,))
        self.sum = flat(w, 658, (TB,))
        self.rsum = flat(w, 660, (TB,))
        self.top_exp = flat(w, 664, (TB, 8))
        self.index_f = flat(w, 680, (TB, 8))
        self.rank = flat(w, 696, (TB, TOPK))
        self.keep = flat(w, 708, (TB, TOPK))
        self.slot_f = flat(w, 720, (TB, TOPK))
        self.index = w[:, 732:748].bitcast(U32).rearrange("p (a b) -> p a b", b=8)
        self.exps = flat(w, 748, (TB, NE))
        self.mask = w[:, 876:940].bitcast(BF16).rearrange("p (a b) -> p a b", b=NE)
        self.onehot = flat(w, 940, (TB, TOPK, NE))
        self.product = flat(w, 1708, (TB, TOPK, NE))
        self.tanh = flat(w, 2476, (TB, SHID))
        self.hidden = flat(w, 2860, (TB, SHID))
        self.hiddenT = flat(w, 3244, (2, T))
        self.p_logits = m.banks[:, 6, 0:TB * NE].rearrange("p (a b) -> p a b", b=NE)
        self.p_rank = m.banks[:, 6, TB * NE:2 * TB * NE].rearrange("p (a b) -> p a b", b=NE)
        self.p_shared = m.banks[:, 0:TB, :]
        self.p_hiddenT = m.banks[:, 2, :].rearrange("p (a b) -> p a b", b=T)
        self.p_out = m.banks[:, 3, :].rearrange("p (a b) -> p a b", b=D)


def route_tensor(nc, m, r, eng, s, ready, turn):
    eng.wait_ge(*ready)
    for t in range(TB):
        for c in range(KC):
            last = nc.tensor.matmul(r.p_logits[:, t, :], r.xnT[:, c, t * P:(t + 1) * P], m.w_router[:, c, :],
                                    start=(c == 0), stop=(c == KC - 1))
    last.then_inc(s.logits, 1)
    for t in range(TB):
        for c in range(KC):
            last = nc.tensor.matmul(r.p_shared[:, t, 0:2 * SHID], r.xnT[:, c, t * P:(t + 1) * P],
                                    m.w_sgu[:, c, :], start=(c == 0), stop=(c == KC - 1))
        last.then_inc(s.shared_in, 1)
    eng.wait_ge(s.mask, turn + 1)
    for t in range(TB):
        nc.tensor.matmul(r.p_rank[:, t, :], m.before_b[:, :], r.mask[:, t, :], start=True, stop=False)
        last = nc.tensor.matmul(r.p_rank[:, t, :], m.ones_b[:, :], m.taken[:, :], start=False, stop=(t == 0))
        if t == 1:
            last = nc.tensor.matmul(r.p_rank[:, t, :], m.ones_b[:, :], r.mask[:, 0, :], start=False, stop=True)
    last.then_inc(s.rank, 1)
    for t in range(TB):
        eng.wait_ge(s.hidden, turn * TB + (t + 1))
        for j in range(2):
            last = nc.tensor.transpose(r.p_hiddenT[0:HID, j, t * P:(t + 1) * P],
                                       r.hidden[:, t, j * HID:(j + 1) * HID], m.ident[:, :])
    last.then_inc(s.turned, 1)
    eng.wait_ge(s.hiddenT, turn + 1)
    for t in range(TB):
        for j in range(2):
            last = nc.tensor.matmul(r.p_out[:, t, :], r.hiddenT[0:HID, j, t * P:(t + 1) * P], m.w_sdn[:, j, :],
                                    start=(j == 0), stop=(j == 1))
    last.then_inc(s.shared_out, 1)


def route_scalar(nc, r, eng, s, turn):
    eng.wait_ge(s.neg_max, turn + 1)
    for t in range(TB):
        nc.scalar.activation(r.exps[:, t, :], r.logits[:, t, :], ACT.Exp, bias=r.neg_max[:, t:t + 1],
                             accum_out=r.sum[:, t:t + 1])
        last = nc.scalar.activation(r.top_exp[:, t, :], r.top[:, t, :], ACT.Exp, bias=r.neg_max[:, t:t + 1])
    last.then_inc(s.exps, 1)
    for t in range(TB):
        eng.wait_ge(s.shared_in, turn * TB + (t + 1))
        nc.scalar.activation(r.tanh[:, t, :], r.p_shared[:, t, 0:SHID], ACT.Tanh, scale=0.5).then_inc(s.tanh, 1)
    eng.wait_ge(s.turned, turn + 1)
    nc.scalar.copy(r.hiddenT[0:HID, :, :], r.p_hiddenT[0:HID, :, :]).then_inc(s.hiddenT, 1)


def route_vector(nc, m, r, eng, chain, s, turn, sequence, x_tiles):
    eng.wait_ge(s.logits, turn + 1)
    chain(nc.vector.tensor_copy(r.logits[:, :, :], r.p_logits))
    for t in range(TB):
        last = nc.vector.max(r.top[:, t, :], r.logits[:, t, :])
        if t == 0:
            chain.count(last)
    chain(last)
    nc.vector.tensor_scalar(r.neg_max, r.top[:, :, 0], -1.0, None, ALU.mult).then_inc(s.neg_max, 1)
    for t in range(TB):
        chain(nc.vector.max_index(r.index[:, t, :], r.top[:, t, :], r.logits[:, t, :]))
    chain(nc.vector.tensor_copy(r.index_f, r.index))
    numbers = m.expert_no[:, :].unsqueeze(1).broadcast_to([P, TOPK, NE])
    for t in range(TB):
        chosen = r.index_f[:, t, 0:TOPK].unsqueeze(2).broadcast_to([P, TOPK, NE])
        chain(nc.vector.tensor_tensor(r.onehot[:, t], numbers, chosen, ALU.is_equal))
    for t in range(TB):
        with nc.allow_low_precision(reason="sums of zeros and a one"):
            last = nc.vector.tensor_reduce(r.mask[:, t, :], r.onehot[:, t].rearrange("p k e -> p e k"), AX.X,
                                           ALU.add)
        if t == 0:
            chain(last)
    last.then_inc(s.mask, 1)
    for t in range(TB):
        eng.wait_ge(s.tanh, turn * TB + (t + 1))
        chain(nc.vector.scalar_tensor_tensor(out=r.tanh[:, t, :], in0=r.tanh[:, t, :], scalar=1.0,
                                             in1=r.p_shared[:, t, 0:SHID], op0=ALU.add, op1=ALU.mult))
        nc.vector.tensor_tensor(r.hidden[:, t, :], r.tanh[:, t, :], r.p_shared[:, t, SHID:2 * SHID],
                                ALU.mult).then_inc(s.hidden, 1)
    eng.wait_ge(s.rank, turn + 1)
    for t in range(TB):
        ranks = r.p_rank[:, t, :].unsqueeze(1).broadcast_to([P, TOPK, NE])
        chain(nc.vector.tensor_tensor(r.product[:, t], r.onehot[:, t], ranks, ALU.mult))
    chain(nc.vector.tensor_reduce(r.rank, r.product, AX.X, ALU.add))
    chain(nc.vector.tensor_scalar(r.keep, r.rank, float(CAP), None, ALU.is_lt))
    chain(nc.vector.scalar_tensor_tensor(out=r.slot_f, in0=r.index_f[:, :, 0:TOPK], scalar=float(CAP),
                                         in1=r.rank, op0=ALU.mult, op1=ALU.add))
    chain(nc.vector.scalar_tensor_tensor(out=r.slot_f, in0=r.slot_f, scalar=-float(SLOTS), in1=r.keep,
                                         op0=ALU.add, op1=ALU.mult))
    chain(nc.vector.tensor_scalar(m.cur_slots[:, :].rearrange("p (a b) -> p a b", b=TOPK), r.slot_f,
                                  float(SLOTS), None, ALU.add))
    nc.vector.tensor_copy(m.slots[:, bass.ds(sequence * TB, TB), :],
                          m.cur_slots[:, :].rearrange("p (a b) -> p a b", b=TOPK)).then_inc(s.slots, 1)
    chain(nc.vector.tensor_tensor(m.taken[:, :], m.taken[:, :], r.mask[:, 0, :], ALU.add))
    chain(nc.vector.tensor_tensor(m.taken[:, :], m.taken[:, :], r.mask[:, 1, :], ALU.add))
    eng.wait_ge(s.exps, turn + 1)
    chain(nc.vector.reciprocal(r.rsum, r.sum))
    for t in range(TB):
        chain(nc.vector.tensor_scalar(r.top_exp[:, t, 0:TOPK], r.top_exp[:, t, 0:TOPK], r.rsum[:, t:t + 1], 0.25,
                                      ALU.mult, ALU.mult))
    chain(nc.vector.tensor_tensor(m.weights[:, bass.ds(sequence * TB, TB), :], r.top_exp[:, :, 0:TOPK], r.keep,
                                  ALU.mult))
    eng.wait_ge(s.shared_out, turn + 1)
    for t in range(TB):
        chain(nc.vector.scalar_tensor_tensor(out=x_tiles[t], in0=r.p_out[:, t, :], scalar=0.25, in1=x_tiles[t],
                                             op0=ALU.mult, op1=ALU.add))


def route_pool(nc, m, eng, s, turn, last_slot):
    eng.wait_ge(s.slots, 1)
    eng.sem_clear(s.slots)
    for t in range(TB):
        for k in range(TOPK):
            at = t * TOPK + k
            nc.gpsimd.indirect_dma_start(
                out=m.expert_in, out_offset=bass.IndirectOffsetOnAxis(m.cur_slots[:, at:at + 1], 0),
                in_=m.xn[:, t, :], in_offset=None, bounds_check=last_slot, oob_is_err=False
            ).then_inc(s.scattered, 16)
    eng.wait_ge(s.scattered, turn * (16 * TB * TOPK) + 16 * TB * TOPK)



def first_phase(nc, m, a, sem):
    s_const = sem("constants_loaded")
    s_x = sem("x_loaded")
    s_w = sem("small_weights_loaded")
    s_exp = sem("expert_weights_loaded")
    s_made = m.made = sem("constants_made")
    s_zero = sem("zeros_made")
    s_zeroed = sem("scratch_zeroed")
    v_chain = sem("first_vector_chain")
    norm, s = m.norm, m.route
    r = RoutePlaces(m)
    consts = m.w_dn[:, 0:512]
    zeros = m.work[:, 0:2048]
    m.s_expert_weights, m.s_attn_weights = s_exp, sem("attention_weights_loaded")

    with nc.Block() as block:
        @block.sync
        def _(sp):
            sp.dma_start(m.x[:, :, :], a["x"].rearrange("(t p) c -> p t c", p=P)).then_inc(s_x, 16)
            sp.dma_start(m.w_router[:, :, :], a["router"].rearrange("(c p) n -> p c n", p=P)).then_inc(s_w, 16)
            sp.dma_start(m.w_sgu[:, :, 0:SHID], a["shared_gate"].rearrange("(c p) n -> p c n", p=P)).then_inc(s_w, 16)
            sp.dma_start(m.w_sgu[:, :, SHID:2 * SHID],
                         a["shared_up"].rearrange("(c p) n -> p c n", p=P)).then_inc(s_w, 16)
            sp.dma_start(m.w_sdn[:, :, :], a["shared_down"].rearrange("(j p) n -> p j n", p=HID)).then_inc(s_w, 16)
            for g in range(8):
                n = NE // 8 * KC * SHID
                sp.dma_start(m.w_gu[:, g * n:(g + 1) * n], a["gate_up"][:, g * n:(g + 1) * n]).then_inc(s_exp, 16)
            sp.dma_start(m.w_qkv[:, :, :], a["qkv"].rearrange("(c p) n -> p c n", p=P)).then_inc(m.s_attn_weights, 16)
            sp.dma_start(m.w_proj[:, :, :], a["proj"].rearrange("(c p) n -> p c n", p=P)).then_inc(m.s_attn_weights, 16)

        @block.scalar
        def _(act):
            act.dma_start(consts[:, 0:448], a["consts"][:, 0:448]).then_inc(s_const, 16)
            act.dma_start(m.rope[:, :, :, :, :], a["rope"].rearrange("p (a b c d) -> p a b c d", b=2, c=2, d=DH)
                          ).then_inc(s_const, 16)
            act.wait_ge(s_zero, 1)
            for g in range(4):
                act.dma_start(m.expert_in[g * 1024:(g + 1) * 1024, :].rearrange("(p n) d -> p (n d)", p=P),
                              zeros).then_inc(s_zeroed, 16)
            act.dma_start(m.expert_out[SLOTS:SLOTS + P, :], zeros[:, 0:D]).then_inc(s_zeroed, 16)
            act.wait_ge(s_made, 5)
            for g in range(4):
                n = NE // 4 * D
                act.dma_start(m.w_dn[0:HID, g * n:(g + 1) * n], a["down"][:, g * n:(g + 1) * n]).then_inc(s_exp, 16)
            with act.Fori(0, B) as i:
                norm_scalar(nc, act, norm, i, m.banks[:, 7, :], m.work[:, 0:512])
                route_scalar(nc, r, act, s, i)

        @block.vector
        def _(dve):
            nc.vector.memset(zeros, 0.0).then_inc(s_zero, 1)
            nc.vector.memset(m.minus_half[:, :], -0.5)
            nc.vector.memset(m.taken[:, :], 0.0)
            nc.vector.memset(m.ones_b[:, :], 1.0)
            dve.wait_ge(s_const, 32)
            nc.vector.tensor_copy(m.ident[:, :], consts[:, 0:P]).then_inc(s_made, 1)
            nc.vector.tensor_copy(m.ident_b[:, :], consts[:, 0:P]).then_inc(s_made, 1)
            nc.vector.tensor_copy(m.before_b[:, :], consts[:, P:2 * P]).then_inc(s_made, 1)
            nc.vector.tensor_scalar(m.causal_b[:, :], consts[:, 2 * P:3 * P], MASKED, None, ALU.mult).then_inc(s_made, 1)
            nc.vector.tensor_copy(m.expert_no[:, :], consts[:, 3 * P:3 * P + NE]).then_inc(s_made, 1)
            dve.wait_ge(s_made, 5)
            dve.wait_ge(s_x, 16)
            dve.wait_ge(s_zeroed, 80)
            with dve.Fori(0, B) as i:
                chain = Chain(dve, v_chain)
                x_tiles = [m.x[:, i * TB + t, :] for t in range(TB)]
                norm_vector(nc, m, dve, chain, norm, i, x_tiles, m.xn)
                route_vector(nc, m, r, dve, chain, s, i, i, x_tiles)
                dve.wait_ge(s.scattered, i * (16 * TB * TOPK) + 16 * TB * TOPK)

        @block.tensor
        def _(pe):
            pe.wait_ge(s_made, 5)
            pe.wait_ge(s_w, 64)
            with pe.Fori(0, B) as i:
                norm_tensor(nc, m, pe, norm, i, m.xn, m.banks[:, 7, :].rearrange("p (a b) -> p a b", b=T))
                route_tensor(nc, m, r, pe, s, (norm.xnT, i + 1), i)

        @block.gpsimd
        def _(pool):
            pool.wait_ge(s_zeroed, 80)
            last_slot = pool.to_reg(SLOTS - 1)
            with pool.Fori(0, B) as i:
                norm_pool(nc, m, pool, norm, i)
                route_pool(nc, m, pool, s, i, last_slot)



RING = 4


class ExpertSems:
    def __init__(self, sem):
        self.rows = [sem(f"expert_rows_loaded{b}") for b in range(RING)]
        self.rows_turned = sem("expert_rows_turned")
        self.rowsT = sem("expert_rows_T_ready")
        self.gate_up = sem("expert_gate_up_ready")
        self.tanh = sem("expert_tanh_ready")
        self.gated = sem("expert_gated_ready")
        self.hidden = sem("expert_hidden_ready")
        self.hidden_turned = sem("expert_hidden_turned")
        self.hiddenT = sem("expert_hidden_T_ready")
        self.out = sem("expert_out_ready")
        self.copied = sem("expert_out_copied")
        self.stored = [sem(f"expert_out_stored{b}") for b in range(RING)]
        self.down = sem("expert_down_reloaded")


def in_steps(engine, stages):
    longest = max(lag for lag, _ in stages)
    turns = (PAIRS - longest) // RING

    def peeled(p):
        for lag, stage in stages:
            if 0 <= p - lag < PAIRS:
                stage(p - lag, (p - lag) % RING)

    for p in range(longest):
        peeled(p)
    with engine.Fori(0, turns) as i:
        for u in range(RING):
            for lag, stage in stages:
                stage(i * RING + (longest + u - lag), (longest + u - lag) % RING)
    for p in range(longest + turns * RING, PAIRS + longest):
        peeled(p)


def experts_phase(nc, m, a, call):
    x, w = m.experts, m.work
    rows = [flat(w, 256 * b, (D,)) for b in range(RING)]
    rowsT = [flat(w, 1024 + 256 * b, (KC, P)) for b in range(2)]
    tanh = [flat(w, 1536 + 192 * b, (2, HID)) for b in range(2)]
    hidden = [flat(w, 1920 + 192 * b, (2, HID)) for b in range(2)]
    hiddenT = [flat(w, 2304 + 128 * b, (2, CAP)) for b in range(2)]
    out = [flat(w, 2560 + 512 * b, (2, D)) for b in range(2)]
    p_rowsT = [m.banks[:, b, 0:D].rearrange("p (c t) -> p c t", t=P) for b in range(2)]
    p_gu = [m.banks[0:CAP, 2 + b, 0:2 * SHID].rearrange("p (e n) -> p e n", n=SHID) for b in range(2)]
    p_hiddenT = [m.banks[0:HID, 4 + b, 0:2 * CAP].rearrange("p (e n) -> p e n", n=CAP) for b in range(2)]
    p_out = [m.banks[0:CAP, 6 + b, :].rearrange("p (e n) -> p e n", n=D) for b in range(2)]
    w_gu = m.w_gu[:, :].rearrange("p (e c n) -> p e c n", c=KC, n=SHID)
    w_dn = m.w_dn[0:HID, :].rearrange("p (e n) -> p e n", n=D)
    before = call * PAIRS

    def rows_loaded(pair, b):
        return pair * (16 // RING) + (16 + (before - b) * 16 // RING)

    def out_stored(pair, b):
        return pair * (32 // RING) + (64 + (before - b) * 32 // RING)

    with nc.Block() as block:
        @block.sync
        def _(sp):
            if call == 0:
                sp.sem_inc(x.rows_turned, RING)

            def load(pair, b):
                sp.wait_ge(x.rows_turned, pair + (before + 1))
                sp.dma_start(rows[b], m.expert_in[bass.ds(pair * P, P), :]).then_inc(x.rows[b], 16)

            in_steps(sp, [(0, load)])

        @block.scalar
        def _(act):
            if call == 1:
                half = NE // 2 * D
                act.dma_start(m.w_dn[0:HID, half:], a["down"][:, half:]).then_inc(x.down, 16)
            else:
                act.sem_inc(x.copied, 2)
                for b in range(RING):
                    act.sem_inc(x.stored[b], 32)

            def copy_rows(pair, b):
                act.wait_ge(x.rows_turned, pair + (before + RING + 1))
                nc.scalar.copy(rowsT[b % 2], p_rowsT[b % 2]).then_inc(x.rowsT, 1)

            def gate(pair, b):
                act.wait_ge(x.gate_up, pair + (before + 1))
                nc.scalar.activation(tanh[b % 2][0:CAP], p_gu[b % 2][:, :, 0:HID], ACT.Tanh,
                                     scale=0.5).then_inc(x.tanh, 1)

            def store(pair, b):
                act.wait_ge(x.out, pair + (before + 1))
                act.wait_ge(x.stored[(b + 2) % RING], out_stored(pair - 2, (b + 2) % RING))
                nc.scalar.copy(out[b % 2][0:CAP], p_out[b % 2]).then_inc(x.copied, 1)
                act.wait_ge(x.copied, pair + (before + 3))
                for e in range(2):
                    act.dma_start(m.expert_out[bass.ds(pair * P + e * CAP, CAP), :],
                                  out[b % 2][0:CAP, e, :]).then_inc(x.stored[b], 16)

            in_steps(act, [(0, copy_rows), (1, gate), (3, store)])
            for b in range(RING):
                act.wait_ge(x.stored[b], out_stored(PAIRS - RING + b, b))

        @block.vector
        def _(dve):
            def gated(pair, b):
                dve.wait_ge(x.tanh, pair + (before + 1))
                nc.vector.scalar_tensor_tensor(out=tanh[b % 2][0:CAP], in0=tanh[b % 2][0:CAP], scalar=1.0,
                                               in1=p_gu[b % 2][:, :, 0:HID], op0=ALU.add,
                                               op1=ALU.mult).then_inc(x.gated, 1)
                dve.wait_ge(x.gated, pair + (before + 1))
                nc.vector.tensor_tensor(hidden[b % 2][0:CAP], tanh[b % 2][0:CAP], p_gu[b % 2][:, :, HID:2 * HID],
                                        ALU.mult).then_inc(x.hidden, 1)

            def copy_hidden(pair, b):
                dve.wait_ge(x.hidden_turned, pair + (before + 1))
                nc.vector.tensor_copy(hiddenT[b % 2][0:HID], p_hiddenT[b % 2]).then_inc(x.hiddenT, 1)

            in_steps(dve, [(1, gated), (2, copy_hidden)])

        @block.tensor
        def _(pe):
            if call == 0:
                pe.wait_ge(m.s_expert_weights, 16 * 12)
            else:
                pe.wait_ge(x.down, 16)

            def turn_rows(pair, b):
                pe.wait_ge(x.rows[b], rows_loaded(pair, b))
                for c in range(KC):
                    last = nc.tensor.transpose(p_rowsT[b % 2][:, c, :], rows[b][:, c * P:(c + 1) * P], m.ident[:, :])
                last.then_inc(x.rows_turned, 1)

            def gate_up(pair, b):
                pe.wait_ge(x.rowsT, pair + (before + 1))
                for e in range(2):
                    for c in range(KC):
                        last = nc.tensor.matmul(p_gu[b % 2][:, e, :], rowsT[b % 2][:, c, e * CAP:(e + 1) * CAP],
                                                w_gu[:, pair * 2 + e, c, :], start=(c == 0), stop=(c == KC - 1))
                last.then_inc(x.gate_up, 1)

            def turn_hidden(pair, b):
                pe.wait_ge(x.hidden, pair + (before + 1))
                for e in range(2):
                    last = nc.tensor.matmul(p_hiddenT[b % 2][:, e, :], hidden[b % 2][0:CAP, e, :],
                                            m.ident[0:CAP, 0:CAP], start=True, stop=True)
                last.then_inc(x.hidden_turned, 1)

            def down(pair, b):
                pe.wait_ge(x.hiddenT, pair + (before + 1))
                pe.wait_ge(x.copied, pair + (before + 1))
                for e in range(2):
                    last = nc.tensor.matmul(p_out[b % 2][:, e, :], hiddenT[b % 2][0:HID, e, :],
                                            w_dn[:, pair * 2 + e, :], start=True, stop=True)
                last.then_inc(x.out, 1)

            in_steps(pe, [(0, turn_rows), (1, gate_up), (2, turn_hidden), (3, down)])



class AttnSems:
    def __init__(self, sem, name):
        self.qkv = sem(f"{name}_qkv_ready")
        self.v = sem(f"{name}_v_ready")
        self.rope = sem(f"{name}_rope_ready")
        self.turned = sem(f"{name}_qk_turned")
        self.qkT = sem(f"{name}_qk_T_ready")
        self.scores = sem(f"{name}_scores_ready")
        self.neg_max = sem(f"{name}_neg_max_ready")
        self.probs = sem(f"{name}_probs_ready")
        self.probs_turned = sem(f"{name}_probs_turned")
        self.probsT = sem(f"{name}_probs_T_ready")
        self.pv = sem(f"{name}_pv_ready")
        self.y = sem(f"{name}_y_ready")
        self.y_turned = sem(f"{name}_y_turned")
        self.yT = sem(f"{name}_y_T_ready")
        self.proj = sem(f"{name}_proj_ready")


class AttnPlaces:

    def __init__(self, m, heads, area, work, w_qkv, w_proj, bias=None, proj_bias=None):
        self.heads, self.pairs, self.groups, self.width = heads, heads // 2, heads // 4, heads * DH
        self.w_qkv, self.w_proj, self.bias, self.proj_bias = w_qkv, w_proj, bias, proj_bias
        n = self.width
        self.qk = flat(area, 0, (TB, 2 * heads, 32))
        self.qkT = flat(area, 2048, (2 * self.groups, T))
        self.v = flat(area, 4096, (TB, n))
        self.p = [flat(area, 4608 + 768 * b, (2, 3 * P)) for b in range(2)]
        self.pT = [flat(area, 6144 + 768 * b, (2, 3, P)) for b in range(2)]
        self.neg_max = [flat(area, 7680 + 4 * b, (2, TB)) for b in range(2)]
        self.sum = flat(area, 7688, (TB, heads))
        self.rsum = flat(area, 7720, (TB, heads))
        self.y = flat(work, 512, (TB, n))
        self.yT = flat(work, 1024, (max(1, n // P), T))
        self.tmp = flat(work, 1536, (TB, 2 * n))
        self.qkv_sb = flat(work, 2560, (TB, 3 * n)) if bias is not None else None
        self.y_rows = min(n, P)
        self.xnT = flat(work, 0, (KC, T))
        self.p_scores = [[m.banks[:, 2 * b + j, 0:3 * P] for j in range(2)] for b in range(2)]
        self.p_pairs = [m.banks[:, 2 * b:2 * b + 2, 0:3 * P] for b in range(2)]
        self.p_probsT = m.banks[:, 4:6, 0:3 * P]
        self.p_y = m.banks[:, 6, 0:TB * n].rearrange("p (t n) -> p t n", n=n)
        self.p_yT = m.banks[:, 7, 0:max(1, n // P) * T].rearrange("p (c t) -> p c t", t=T)
        self.p_proj = m.banks[:, 5, :].rearrange("p (t n) -> p t n", n=D)
        self.split = 3 * n > 512


def attn_tensor(nc, m, s, a, eng, ready, turn):
    n, pairs = a.width, a.pairs
    eng.wait_ge(*ready)
    for t in range(TB):
        for first, last_col in ([(0, 2 * n), (2 * n, 3 * n)] if a.split else [(0, 3 * n)]):
            bank = 2 * t + (1 if first else 0)
            for c in range(KC):
                last = nc.tensor.matmul(m.banks[:, bank, 0:last_col - first], a.xnT[:, c, t * P:(t + 1) * P],
                                        a.w_qkv[:, c, first:last_col], start=(c == 0), stop=(c == KC - 1))
        last.then_inc(s.qkv, 1)
    for t in range(TB):
        eng.wait_ge(s.rope, turn * TB + (t + 1))
        for g in range(2 * a.groups):
            last = nc.tensor.transpose(m.banks[:, 4 + g // 2, (g % 2) * T + t * P:(g % 2) * T + (t + 1) * P],
                                       a.qk[:, t, 4 * g:4 * g + 4, :].rearrange("p h d -> p (h d)"), m.ident[:, :])
    last.then_inc(s.turned, 1)
    copies = 2 if a.groups > 1 else 1
    eng.wait_ge(s.qkT, turn * copies + copies)
    eng.wait_ge(s.v, turn * TB + TB)

    def scores(pair):
        if pair >= 2:
            eng.wait_ge(s.probs, turn * pairs + (pair - 1))
        for j in range(2):
            h = 2 * pair + j
            row = slice(32 * (h % 4), 32 * (h % 4) + DH)
            q, k, out = a.qkT[row, h // 4, :], a.qkT[row, a.groups + h // 4, :], a.p_scores[pair % 2][j]
            nc.tensor.matmul(out[:, 0:P], q[:, 0:P], k[:, 0:P], start=True, stop=False)
            nc.tensor.matmul(out[:, 0:P], m.ident_b[:, :], m.causal_b[:, :], start=False, stop=True)
            nc.tensor.matmul(out[:, P:3 * P], q[:, P:T], k[:, 0:T], start=True, stop=False)
            last = nc.tensor.matmul(out[:, 2 * P:3 * P], m.ident_b[:, :], m.causal_b[:, :], start=False, stop=True)
        last.then_inc(s.scores, 1)

    scores(0)
    scores(1)
    for pair in range(pairs):
        eng.wait_ge(s.probs, turn * pairs + (pair + 1))
        for j in range(2):
            for block in range(3):
                last = nc.tensor.transpose(a.p_probsT[:, j, block * P:(block + 1) * P],
                                           a.p[pair % 2][:, j, block * P:(block + 1) * P], m.ident[:, :])
        last.then_inc(s.probs_turned, 1)
        if pair + 2 < pairs:
            scores(pair + 2)
        eng.wait_ge(s.probsT, turn * pairs + (pair + 1))
        for j in range(2):
            h = 2 * pair + j
            cols = slice(h * DH, (h + 1) * DH)
            nc.tensor.matmul(a.p_y[:, 0, cols], a.pT[pair % 2][:, j, 0, :], a.v[:, 0, cols], start=True, stop=True)
            nc.tensor.matmul(a.p_y[:, 1, cols], a.pT[pair % 2][:, j, 1, :], a.v[:, 0, cols], start=True, stop=False)
            last = nc.tensor.matmul(a.p_y[:, 1, cols], a.pT[pair % 2][:, j, 2, :], a.v[:, 1, cols],
                                    start=False, stop=True)
    last.then_inc(s.pv, 1)
    eng.wait_ge(s.y, turn + 1)
    rows = a.y_rows
    for t in range(TB):
        for c in range(n // rows):
            last = nc.tensor.matmul(a.p_yT[0:rows, c, t * P:(t + 1) * P], a.y[:, t, c * rows:(c + 1) * rows],
                                    m.ident[:, :], start=True, stop=True)
    last.then_inc(s.y_turned, 1)
    eng.wait_ge(s.yT, turn + 1)
    for t in range(TB):
        for c in range(n // rows):
            last = nc.tensor.matmul(a.p_proj[:, t, :], a.yT[0:rows, c, t * P:(t + 1) * P], a.w_proj[0:rows, c, :],
                                    start=(c == 0), stop=(c == n // rows - 1))
    last.then_inc(s.proj, 1)


def attn_scalar(nc, m, s, a, eng, turn):
    n, pairs = a.width, a.pairs
    if a.bias is None:
        for t in range(TB):
            eng.wait_ge(s.qkv, turn * TB + (t + 1))
            nc.scalar.copy(a.v[:, t, :], m.banks[:, 2 * t + 1, 0:n]).then_inc(s.v, 1)
    if a.groups > 1:
        eng.wait_ge(s.turned, turn + 1)
        nc.scalar.copy(a.qkT[:, 0:a.groups, :], m.banks[:, 4:6, :].rearrange("p b (g t) -> p (b g) t", t=T)
                       ).then_inc(s.qkT, 1)
    for pair in range(pairs):
        eng.wait_ge(s.neg_max, turn * (2 * pairs) + (2 * pair + 2))
        for j in range(2):
            for t, cols in enumerate((slice(0, P), slice(P, 3 * P))):
                h = 2 * pair + j
                last = nc.scalar.activation(a.p[pair % 2][:, j, cols], a.p_scores[pair % 2][j][:, cols], ACT.Exp,
                                            bias=a.neg_max[pair % 2][:, j, t:t + 1],
                                            accum_out=a.sum[:, t, h:h + 1])
        last.then_inc(s.probs, 1)
    eng.wait_ge(s.y_turned, turn + 1)
    nc.scalar.copy(a.yT[0:a.y_rows], a.p_yT[0:a.y_rows]).then_inc(s.yT, 1)


def attn_vector(nc, m, s, a, eng, chain, turn, x_tiles):
    n, pairs, heads = a.width, a.pairs, a.heads
    for t in range(TB):
        eng.wait_ge(s.qkv, turn * TB + (t + 1))
        if a.bias is None:
            qk = m.banks[:, 2 * t, 0:2 * n]
        else:
            chain(nc.vector.tensor_tensor(a.qkv_sb[:, t, :], m.banks[:, 2 * t, 0:3 * n], a.bias, ALU.add))
            nc.vector.tensor_copy(a.v[:, t, :], a.qkv_sb[:, t, 2 * n:3 * n]).then_inc(s.v, 1)
            qk = a.qkv_sb[:, t, 0:2 * n]
        z = qk.rearrange("p (s h d) -> p s h d", s=2, d=DH)
        out = a.qk[:, t, :, :].rearrange("p (s h) d -> p s h d", s=2)
        tmp = a.tmp[:, t, :].rearrange("p (s h d) -> p s h d", s=2, d=DH)

        def table(which, first, end):
            v = m.rope[:, t, which, :, first:end]
            return v.unsqueeze(2).broadcast_to([P, 2, heads, end - first])

        half = DH // 2
        chain.count(nc.vector.tensor_tensor(tmp, z, table(0, 0, DH), ALU.mult))
        chain.count(nc.vector.tensor_tensor(out[:, :, :, 0:half], z[:, :, :, half:DH], table(1, 0, half), ALU.mult))
        chain(nc.vector.tensor_tensor(out[:, :, :, half:DH], z[:, :, :, 0:half], table(1, half, DH), ALU.mult))
        nc.vector.tensor_tensor(out[:, :, :, 0:DH], out[:, :, :, 0:DH], tmp, ALU.add).then_inc(s.rope, 1)
    eng.wait_ge(s.turned, turn + 1)
    if a.groups > 1:
        nc.vector.tensor_copy(a.qkT[:, a.groups:, :], m.banks[:, 6:8, :].rearrange("p b (g t) -> p (b g) t", t=T)
                              ).then_inc(s.qkT, 1)
    else:
        nc.vector.tensor_copy(a.qkT[:, 0:2, :], m.banks[:, 4, :].rearrange("p (g t) -> p g t", t=T)
                              ).then_inc(s.qkT, 1)

    def row_max(pair):
        eng.wait_ge(s.scores, turn * pairs + (pair + 1))
        for t, cols in enumerate((slice(0, P), slice(P, 3 * P))):
            nc.vector.tensor_reduce(a.neg_max[pair % 2][:, :, t], a.p_pairs[pair % 2][:, :, cols], AX.X, ALU.max,
                                    negate=True).then_inc(s.neg_max, 1)

    row_max(0)
    row_max(1)
    for pair in range(pairs):
        eng.wait_ge(s.probs_turned, turn * pairs + (pair + 1))
        nc.vector.tensor_copy(a.pT[pair % 2].rearrange("p j b q -> p j (b q)"), a.p_probsT).then_inc(s.probsT, 1)
        if pair + 2 < pairs:
            row_max(pair + 2)
    eng.wait_ge(s.pv, turn + 1)
    chain(nc.vector.reciprocal(a.rsum, a.sum))
    nc.vector.tensor_tensor(a.y.rearrange("p t (h d) -> p (t h) d", d=DH),
                            a.p_y.rearrange("p t (h d) -> p (t h) d", d=DH),
                            a.rsum.rearrange("p t h -> p (t h)").unsqueeze(2).broadcast_to([P, TB * heads, DH]),
                            ALU.mult).then_inc(s.y, 1)
    eng.wait_ge(s.proj, turn + 1)
    for t in range(TB):
        chain(nc.vector.tensor_tensor(x_tiles[t], x_tiles[t], a.p_proj[:, t, :], ALU.add))
        if a.proj_bias is not None:
            chain(nc.vector.tensor_tensor(x_tiles[t], x_tiles[t], a.proj_bias, ALU.add))



class CombineSems:
    def __init__(self, sem, name):
        self.slots = sem(f"{name}_slots_ready")
        self.gathered = [sem(f"{name}_rows_gathered{t}") for t in range(TB)]


def combine_pool(nc, m, rows, eng, s, turn, last_row):
    eng.wait_ge(s.slots, 1)
    eng.sem_clear(s.slots)
    for t in range(TB):
        for k in range(TOPK):
            at = t * TOPK + k
            nc.gpsimd.indirect_dma_start(
                out=rows[:, at, :], out_offset=None, in_=m.expert_out,
                in_offset=bass.IndirectOffsetOnAxis(m.cur_slots[:, at:at + 1], 0),
                bounds_check=last_row, oob_is_err=False).then_inc(s.gathered[t], 16)


def combine_vector(nc, m, rows, eng, chain, s, turn, sequence, x_tiles):
    nc.vector.tensor_copy(m.cur_slots[:, :].rearrange("p (a b) -> p a b", b=TOPK),
                          m.slots[:, bass.ds(sequence * TB, TB), :]).then_inc(s.slots, 1)
    chain(nc.vector.tensor_copy(m.cur_weights[:, :, :], m.weights[:, bass.ds(sequence * TB, TB), :]))
    for t in range(TB):
        eng.wait_ge(s.gathered[t], turn * (16 * TOPK) + 16 * TOPK)
        for k in range(TOPK):
            chain(nc.vector.scalar_tensor_tensor(out=x_tiles[t], in0=rows[:, t * TOPK + k, :],
                                                 scalar=m.cur_weights[:, t, k:k + 1], in1=x_tiles[t],
                                                 op0=ALU.mult, op1=ALU.add))



def middle_phase(nc, m, sem):
    v_chain = sem("middle_vector_chain")
    comb, norm, sr = m.combine, m.norm, m.route
    sa = AttnSems(sem, "attn1")
    s_pad = sem("padding_cleared")
    area = m.w_dn[:, NE // 2 * D:]
    rows = flat(m.work, 0, (TB * TOPK, D))
    a = AttnPlaces(m, H, area, m.work, m.w_qkv, m.w_proj)
    r = RoutePlaces(m)
    p_norm = m.banks[:, 7, :].rearrange("p (a b) -> p a b", b=T)

    with nc.Block() as block:
        @block.scalar
        def _(act):
            with act.Fori(0, B) as i:
                norm_scalar(nc, act, norm, 2 * i + B, m.banks[:, 7, :], m.work[:, 0:512])
                attn_scalar(nc, m, sa, a, act, i)
                norm_scalar(nc, act, norm, 2 * i + (B + 1), m.banks[:, 7, :], m.work[:, 0:512])
                route_scalar(nc, r, act, sr, i + B)

        @block.vector
        def _(dve):
            nc.vector.memset(a.qk, 0.0).then_inc(s_pad, 1)
            nc.vector.memset(m.taken[:, :], 0.0).then_inc(s_pad, 1)
            dve.wait_ge(s_pad, 2)
            with dve.Fori(0, B) as i:
                chain = Chain(dve, v_chain)
                x_tiles = [m.x[:, i * TB + t, :] for t in range(TB)]
                combine_vector(nc, m, rows, dve, chain, comb, i, i, x_tiles)
                norm_vector(nc, m, dve, chain, norm, 2 * i + B, x_tiles, m.xn)
                attn_vector(nc, m, sa, a, dve, chain, i, x_tiles)
                norm_vector(nc, m, dve, chain, norm, 2 * i + (B + 1), x_tiles, m.xn)
                route_vector(nc, m, r, dve, chain, sr, i + B, i, x_tiles)
                dve.wait_ge(sr.scattered, (i + B) * (16 * TB * TOPK) + 16 * TB * TOPK)

        @block.tensor
        def _(pe):
            pe.wait_ge(m.s_attn_weights, 32)
            with pe.Fori(0, B) as i:
                norm_tensor(nc, m, pe, norm, 2 * i + B, m.xn, p_norm)
                attn_tensor(nc, m, sa, a, pe, (norm.xnT, 2 * i + (B + 1)), i)
                norm_tensor(nc, m, pe, norm, 2 * i + (B + 1), m.xn, p_norm)
                route_tensor(nc, m, r, pe, sr, (norm.xnT, 2 * i + (B + 2)), i + B)

        @block.gpsimd
        def _(pool):
            last_slot, last_row = pool.to_reg(SLOTS - 1), pool.to_reg(SLOTS + P - 1)
            with pool.Fori(0, B) as i:
                combine_pool(nc, m, rows, pool, comb, i, last_row)
                norm_pool(nc, m, pool, norm, 2 * i + B)
                norm_pool(nc, m, pool, norm, 2 * i + (B + 1))
                route_pool(nc, m, pool, sr, i + B, last_slot)



HALF = TILES // 2
ROW_NAMES = ["amp_b", "ph_b", "ent_pb0", "ent_pb1", "path_b00", "path_b01", "path_b10", "path_b11",
             "phase00", "phase01", "phase10", "phase11", "ln3_g0", "ln3_g1", "ln3_b0", "ln3_b1",
             "ln4_g0", "ln4_g1", "ln4_b0", "ln4_b1", "bo", "bq"]
TURN_PI = float(np.nextafter(np.float32(np.pi), np.float32(0)))


def last_weights(m):
    w, g = Places(), m.w_gu
    w.ent_wT = flat(g, 0, (NL, EW // P, D))
    w.ent_pw = flat(g, 4096, (NL, EW // P, D))
    w.path = flat(g, 8192, (NL * PW, KC, D))
    w.amp_ph = flat(g, 10240, (KC, 2 * D))
    w.rows = flat(g, 11264, (len(ROW_NAMES), D))
    w.kv_b = flat(g, 16896, (2 * HKV * DH,))
    w.ent_b = flat(g, 17024, (NL, EW // P))
    w.ent = flat(g, 17040, (NL, KC, D))
    w.wave = flat(g, 18064, (NL, KC, D))
    w.ent_bias = flat(g, 19088, (NL, D))
    w.wave_bias = flat(g, 19600, (NL, D))
    w.wq = flat(g, 20112, (KC, D))
    w.qkv2 = flat(g, 20624, (KC, 3 * HKV * DH))
    w.qkv2_b = flat(g, 21008, (3 * HKV * DH,))
    w.wo = flat(g, 21200, (1, D))
    w.scaled = flat(g, 21456, (KC, D))
    w.ent_b_wide = flat(m.w_dn, 0, (EW // P, P))
    w.phase_turns = flat(m.w_dn, 1024, (NL * PW, D))
    w.phase_sin = flat(m.w_dn, 2048, (NL * PW, D))
    w.phase_cos = flat(m.w_dn, 3072, (NL * PW, D))
    w.mod = flat(m.w_dn, 4096, (NL * PW, D))
    w.half_pi = flat(m.w_dn, 5120, (1,))
    return w


def row(w, name):
    return w.rows[:, ROW_NAMES.index(name), :]


def fold_phase(nc, m, a, sem):
    w = last_weights(m)
    s_ent, s_rest = sem("entangling_weights_loaded"), sem("wave_weights_loaded")
    s_wide, s_used = sem("ent_bias_spread"), sem("ent_bias_products_copied")
    s_prod = sem("ent_product_ready")
    s_sin, s_half = sem("phase_sines_ready"), sem("phase_reduced")
    v_chain = sem("fold_vector_chain")

    with nc.Block() as block:
        @block.sync
        def _(sp):
            for l in range(NL):
                sp.dma_start(w.ent_b[:, l, :], a["ent_b"][:, l * 8:(l + 1) * 8]).then_inc(s_ent, 16)
                sp.dma_start(w.ent_wT[:, l], a["ent_wT"][l].rearrange("(c p) d -> p c d", p=P)).then_inc(s_ent, 16)
                sp.dma_start(w.ent_pw[:, l], a["ent_pw"][l].rearrange("(c p) d -> p c d", p=P)).then_inc(s_ent, 16)

        @block.scalar
        def _(act):
            n = len(ROW_NAMES) * D
            act.dma_start(w.rows.rearrange("p a b -> p (a b)"), a["rows"].broadcast_to([P, n])).then_inc(s_rest, 16)
            act.dma_start(w.kv_b, a["kv_b"].broadcast_to([P, 2 * HKV * DH])).then_inc(s_rest, 16)
            for q in range(NL * PW):
                act.dma_start(w.path[:, q], a["path_w"][q].rearrange("(c p) d -> p c d", p=P)).then_inc(s_rest, 16)
            act.dma_start(w.amp_ph[:, :, 0:D], a["amp_w"].rearrange("(c p) n -> p c n", p=P)).then_inc(s_rest, 16)
            act.dma_start(w.amp_ph[:, :, D:2 * D], a["ph_w"].rearrange("(c p) n -> p c n", p=P)).then_inc(s_rest, 16)
            act.dma_start(w.wq, a["Wq"].rearrange("(c p) n -> p c n", p=P)).then_inc(s_rest, 16)
            act.dma_start(w.qkv2[:, :, 64:128], a["Wk"].rearrange("(c p) n -> p c n", p=P)).then_inc(s_rest, 16)
            act.dma_start(w.qkv2[:, :, 128:192], a["Wv"].rearrange("(c p) n -> p c n", p=P)).then_inc(s_rest, 16)
            act.dma_start(w.wo[0:64, 0, :], a["Wo"]).then_inc(s_rest, 16)
            act.wait_ge(s_half, 1)
            nc.scalar.activation(w.phase_sin, w.phase_turns, ACT.Sin).then_inc(s_sin, 1)
            act.wait_ge(s_half, 2)
            nc.scalar.activation(w.phase_cos, w.phase_cos, ACT.Sin, scale=-1.0, bias=w.half_pi).then_inc(s_sin, 1)

        @block.vector
        def _(dve):
            chain = Chain(dve, v_chain)
            chain(nc.vector.memset(w.half_pi, PI / 2))
            dve.wait_ge(s_rest, 12 * 16)
            phase = w.rows[:, ROW_NAMES.index("phase00"):ROW_NAMES.index("phase00") + NL * PW, :]
            big = 12582912.0
            chain(nc.vector.tensor_scalar(w.phase_turns, phase, 0.5 / PI, big, ALU.mult, ALU.add))
            chain(nc.vector.tensor_scalar(w.phase_sin, w.phase_turns, -big, None, ALU.add))
            c1 = 6.28125
            c2 = float(np.float32(2 * np.pi - c1))
            chain(nc.vector.scalar_tensor_tensor(out=w.phase_turns, in0=w.phase_sin, scalar=-c1, in1=phase,
                                                 op0=ALU.mult, op1=ALU.add))
            chain(nc.vector.scalar_tensor_tensor(out=w.phase_turns, in0=w.phase_sin, scalar=-c2, in1=w.phase_turns,
                                                 op0=ALU.mult, op1=ALU.add))
            nc.vector.tensor_scalar(w.phase_turns, w.phase_turns, TURN_PI, -TURN_PI, ALU.min, ALU.max).then_inc(s_half, 1)
            dve.wait_ge(s_half, 1)
            nc.vector.scalar_tensor_tensor(out=w.phase_cos, in0=w.phase_turns, scalar=-1.0, in1=w.phase_turns,
                                           op0=ALU.mult, op1=ALU.max).then_inc(s_half, 1)
            dve.wait_ge(s_sin, 2)
            chain(nc.vector.tensor_tensor(w.mod, w.phase_sin, w.phase_cos, ALU.add))
            for l in range(NL):
                for q in range(PW):
                    mod = w.mod[:, l * PW + q, :].unsqueeze(1).broadcast_to([P, KC, D])
                    target = w.wave[:, l] if q == 0 else w.scaled
                    chain(nc.vector.tensor_tensor(target, w.path[:, l * PW + q], mod, ALU.mult))
                chain(nc.vector.tensor_tensor(w.wave[:, l], w.wave[:, l], w.scaled, ALU.add))
                for c in range(KC):
                    part = w.wave[:, l, c, c * P:(c + 1) * P]
                    chain(nc.vector.tensor_tensor(part, part, m.ident[:, :], ALU.add))
                chain(nc.vector.tensor_tensor(w.wave_bias[:, l, :], row(w, f"path_b{l}0"), w.mod[:, l * PW, :], ALU.mult))
                chain(nc.vector.tensor_tensor(w.scaled[:, 0, :], row(w, f"path_b{l}1"), w.mod[:, l * PW + 1, :],
                                              ALU.mult))
                chain(nc.vector.tensor_tensor(w.wave_bias[:, l, :], w.wave_bias[:, l, :], w.scaled[:, 0, :], ALU.add))
            chain(nc.vector.tensor_scalar(w.amp_ph[:, :, 0:D], w.amp_ph[:, :, 0:D], 0.5, None, ALU.mult))
            chain(nc.vector.tensor_scalar(row(w, "amp_b"), row(w, "amp_b"), 0.5, None, ALU.mult))
            for c in range(KC):
                chain(nc.vector.tensor_reduce(w.qkv2[:, c, 0:64].rearrange("p (h d) -> p h d", d=DH),
                                              w.wq[:, c, :].rearrange("p (h g d) -> p h d g", g=4, d=DH),
                                              AX.X, ALU.add))
            chain(nc.vector.tensor_reduce(w.qkv2_b[:, 0:64].rearrange("p (h d) -> p h d", d=DH),
                                          row(w, "bq").rearrange("p (h g d) -> p h d g", g=4, d=DH), AX.X, ALU.add))
            chain(nc.vector.tensor_copy(w.qkv2_b[:, 64:192], w.kv_b))
            dve.wait_ge(s_ent, 16 * 3 * NL)
            for l in range(NL):
                if l:
                    dve.wait_ge(s_prod, 3 * l)
                nc.vector.tensor_copy(w.ent_b_wide, w.ent_b[:, l, :].unsqueeze(2).broadcast_to([P, EW // P, P])
                                      ).then_inc(s_wide, 1)
                for c in range(KC):
                    dve.wait_ge(s_prod, 3 * l + c + 1)
                    chain(nc.vector.tensor_copy(w.ent[:, l, c, :], m.banks[:, c, 0:D]))
                    part = w.ent[:, l, c, c * P:(c + 1) * P]
                    chain(nc.vector.tensor_tensor(part, part, m.ident[:, :], ALU.add))
                dve.wait_ge(s_prod, 3 * l + 3)
                nc.vector.tensor_tensor(w.ent_bias[:, l, :], m.banks[:, 2, 0:D], row(w, f"ent_pb{l}"),
                                        ALU.add).then_inc(s_used, 1)
            dve.wait_ge(s_used, NL)

        @block.tensor
        def _(pe):
            pe.wait_ge(s_ent, 16 * 3 * NL)
            for l in range(NL):
                if l:
                    pe.wait_ge(s_used, l)
                for c in range(KC):
                    for e in range(EW // P):
                        last = nc.tensor.matmul(m.banks[:, c, 0:D], w.ent_wT[:, l, e, c * P:(c + 1) * P],
                                                w.ent_pw[:, l, e, :], start=(e == 0), stop=(e == EW // P - 1))
                    last.then_inc(s_prod, 1)
                pe.wait_ge(s_wide, l + 1)
                for e in range(EW // P):
                    last = nc.tensor.matmul(m.banks[:, 2, 0:D], w.ent_b_wide[:, e, :], w.ent_pw[:, l, e, :],
                                            start=(e == 0), stop=(e == EW // P - 1))
                last.then_inc(s_prod, 1)
    return w


STEPS = 2 * NL


class WaveSems:
    def __init__(self, sem, name):
        self.z = sem(f"{name}_z_ready")
        self.zb = sem(f"{name}_z_with_bias_ready")
        self.tanh = sem(f"{name}_tanh_ready")
        self.abs = sem(f"{name}_abs_ready")
        self.sines = sem(f"{name}_sines_ready")
        self.h = sem(f"{name}_h_ready")
        self.turned = sem(f"{name}_h_turned")
        self.hT = sem(f"{name}_h_T_ready")
        self.lin = sem(f"{name}_linear_ready")
        self.var = sem(f"{name}_variance_ready")
        self.rstd = sem(f"{name}_rstd_ready")
        self.scaled = sem(f"{name}_normed_ready")
        self.gained = sem(f"{name}_gained_ready")


class WavePlaces:
    def __init__(self, m):
        area = m.w_dn
        self.xn = flat(area, 6144, (HALF, D))
        self.hT = flat(m.work, 0, (KC, HALF * P))
        self.h = flat(area, 7168, (HALF, D))
        self.z = flat(area, 8192, (HALF, 2 * D))
        self.abs = flat(area, 10240, (HALF, D))
        self.sines = flat(area, 11264, (HALF, 2, D))
        self.p_turn = [m.banks[:, 4 + t, 0:KC * P].rearrange("p (c t) -> p c t", t=P) for t in range(HALF)]
        self.p_lin = [m.banks[:, t, 0:D] for t in range(HALF)]


def wave_tensor(nc, m, w, f, s, eng, norm, turn):
    eng.wait_ge(norm.xnT, turn + 1)
    for t in range(HALF):
        for c in range(KC):
            last = nc.tensor.matmul(m.banks[:, t, :], f.hT[:, c, t * P:(t + 1) * P], w.amp_ph[:, c, :],
                                    start=(c == 0), stop=(c == KC - 1))
        last.then_inc(s.z, 1)
    for step in range(STEPS):
        weights = (w.ent, w.wave)[step % 2][:, step // 2]
        for t in range(HALF):
            eng.wait_ge(s.h, turn * (STEPS * HALF + HALF) + (step * HALF + t + 1))
            for c in range(KC):
                last = nc.tensor.transpose(f.p_turn[t][:, c, :], f.h[:, t, c * P:(c + 1) * P],
                                           m.ident[:, :])
            last.then_inc(s.turned, 1)
        for t in range(HALF):
            eng.wait_ge(s.hT, turn * (STEPS * HALF) + (step * HALF + t + 1))
            for c in range(KC):
                last = nc.tensor.matmul(f.p_lin[t], f.hT[:, c, t * P:(t + 1) * P], weights[:, c, :],
                                        start=(c == 0), stop=(c == KC - 1))
            last.then_inc(s.lin, 1)


def wave_scalar(nc, m, w, f, s, eng, turn):
    for t in range(HALF):
        eng.wait_ge(s.zb, turn * HALF + (t + 1))
        nc.scalar.activation(f.z[:, t, :], f.z[:, t, :], ACT.Tanh).then_inc(s.tanh, 1)
    for t in range(HALF):
        eng.wait_ge(s.abs, turn * HALF + (t + 1))
        nc.scalar.activation(f.sines[:, t, 0, :], f.z[:, t, D:2 * D], ACT.Sin, scale=TURN_PI)
        nc.scalar.activation(f.sines[:, t, 1, :], f.abs[:, t, :], ACT.Sin, scale=-TURN_PI,
                             bias=w.half_pi).then_inc(s.sines, 1)
    for step in range(STEPS):
        for t in range(HALF):
            eng.wait_ge(s.turned, turn * (STEPS * HALF) + (step * HALF + t + 1))
            nc.scalar.copy(f.hT[:, :, t * P:(t + 1) * P], f.p_turn[t]).then_inc(s.hT, 1)


def wave_vector(nc, m, w, f, s, eng, chain, turn, x_tiles):
    both = w.rows[:, 0:2, :].rearrange("p a b -> p (a b)")
    for t in range(HALF):
        eng.wait_ge(s.z, turn * HALF + (t + 1))
        nc.vector.tensor_tensor(f.z[:, t, :], m.banks[:, t, :], both, ALU.add).then_inc(s.zb, 1)
    for t in range(HALF):
        eng.wait_ge(s.tanh, turn * HALF + (t + 1))
        nc.vector.scalar_tensor_tensor(out=f.abs[:, t, :], in0=f.z[:, t, D:2 * D], scalar=-1.0,
                                       in1=f.z[:, t, D:2 * D], op0=ALU.mult, op1=ALU.max).then_inc(s.abs, 1)
    for t in range(HALF):
        chain(nc.vector.tensor_scalar(f.z[:, t, 0:D], f.z[:, t, 0:D], 0.5, 0.5, ALU.mult, ALU.add))
    for t in range(HALF):
        eng.wait_ge(s.sines, turn * HALF + (t + 1))
        chain(nc.vector.tensor_tensor(f.sines[:, t, 0, :], f.sines[:, t, 0, :], f.sines[:, t, 1, :], ALU.add))
        nc.vector.tensor_tensor(f.h[:, t, :], f.sines[:, t, 0, :], f.z[:, t, 0:D], ALU.mult).then_inc(s.h, 1)
    for step in range(STEPS):
        bias = (w.ent_bias, w.wave_bias)[step % 2][:, step // 2, :]
        done = turn * (STEPS * HALF)
        for t in range(HALF):
            eng.wait_ge(s.lin, done + (step * HALF + t + 1))
            chain(nc.vector.tensor_tensor(f.xn[:, t, :], f.p_lin[t], bias, ALU.add))
            chain(nc.vector.bn_stats(m.stats[:, t, :], f.xn[:, t, :]))
            chain(nc.vector.bn_aggr(m.mv[:, t, :], m.stats[:, t, :]))
        nc.vector.tensor_scalar(m.var_eps[:, :], m.mv[:, :, 1], EPS, None, ALU.add).then_inc(s.var, 1)
        eng.wait_ge(s.rstd, turn * STEPS + (step + 1))
        gain, shift = (row(w, f"ln{3 + step % 2}_{which}{step // 2}") for which in "gb")
        for t in range(HALF):
            chain(nc.vector.tensor_scalar(f.xn[:, t, :], f.xn[:, t, :], m.mv[:, t, 0:1], m.rstd[:, t:t + 1],
                                          ALU.subtract, ALU.mult))
            chain(nc.vector.tensor_tensor(f.xn[:, t, :], f.xn[:, t, :], gain, ALU.mult))
            nc.vector.tensor_tensor(f.h[:, t, :], f.xn[:, t, :], shift, ALU.add).then_inc(s.h, 1)
    for t in range(HALF):
        eng.wait_ge(s.h, turn * (STEPS * HALF + HALF) + (STEPS * HALF + t + 1))
        chain(nc.vector.scalar_tensor_tensor(out=x_tiles[t], in0=f.h[:, t, :], scalar=0.5, in1=x_tiles[t],
                                             op0=ALU.mult, op1=ALU.add))


def wave_pool(nc, m, s, eng, turn):
    for step in range(STEPS):
        eng.wait_ge(s.var, turn * STEPS + (step + 1))
        nc.gpsimd.tensor_tensor(m.rstd[:, :], m.var_eps[:, :], m.minus_half[:, :], ALU.pow).then_inc(s.rstd, 1)


def last_phase(nc, m, w, a, sem):
    v_chain = sem("last_vector_chain")
    comb, norm = m.combine, m.norm
    norm4, wave = NormSems(sem, "norm_of_half"), WaveSems(sem, "wave")
    done = 3 * B
    sa = AttnSems(sem, "attn2")
    s_pad, s_out, s_stored = sem("padding2_cleared"), sem("out_ready"), sem("out_stored")
    f = WavePlaces(m)
    rows = flat(m.work, 0, (TB * TOPK, D))
    area = m.w_gu[:, 0:8192]
    at = AttnPlaces(m, HKV, area, m.work, w.qkv2, w.wo, w.qkv2_b, row(w, "bo"))
    p_norm = m.banks[:, 7, :].rearrange("p (a b) -> p a b", b=T)
    p_half = m.banks[:, 4:6, :]

    with nc.Block() as block:
        @block.scalar
        def _(act):
            with act.Fori(0, 2) as i:
                norm_scalar(nc, act, norm4, 2 * i, p_half, f.hT)
                wave_scalar(nc, m, w, f, wave, act, 2 * i)
                for q in range(2):
                    norm_scalar(nc, act, norm, i * 2 + (q + done), m.banks[:, 7, :], m.work[:, 0:512])
                    attn_scalar(nc, m, sa, at, act, i * 2 + q)
                norm_scalar(nc, act, norm4, 2 * i + 1, p_half, f.hT)
                wave_scalar(nc, m, w, f, wave, act, 2 * i + 1)

        @block.vector
        def _(dve):
            nc.vector.memset(at.qk, 0.0).then_inc(s_pad, 1)
            dve.wait_ge(s_pad, 1)
            with dve.Fori(0, 2) as i:
                chain = Chain(dve, v_chain)
                x_tiles = [m.x[:, i * HALF + t, :] for t in range(HALF)]
                for q in range(2):
                    combine_vector(nc, m, rows, dve, chain, comb, i * 2 + (q + B), i * 2 + q, x_tiles[q * TB:(q + 1) * TB])
                norm_vector(nc, m, dve, chain, norm4, 2 * i, x_tiles, f.xn, HALF)
                wave_vector(nc, m, w, f, wave, dve, chain, 2 * i, x_tiles)
                for q in range(2):
                    own = x_tiles[q * TB:(q + 1) * TB]
                    norm_vector(nc, m, dve, chain, norm, i * 2 + (q + done), own, m.xn)
                    attn_vector(nc, m, sa, at, dve, chain, i * 2 + q, own)
                norm_vector(nc, m, dve, chain, norm4, 2 * i + 1, x_tiles, f.xn, HALF)
                wave_vector(nc, m, w, f, wave, dve, chain, 2 * i + 1, x_tiles)
                dve.sem_inc(s_out, 1)

        @block.tensor
        def _(pe):
            with pe.Fori(0, 2) as i:
                norm_tensor(nc, m, pe, norm4, 2 * i, f.xn, p_half, HALF)
                wave_tensor(nc, m, w, f, wave, pe, norm4, 2 * i)
                for q in range(2):
                    norm_tensor(nc, m, pe, norm, i * 2 + (q + done), m.xn, p_norm)
                    attn_tensor(nc, m, sa, at, pe, (norm.xnT, i * 2 + (q + done + 1)), i * 2 + q)
                norm_tensor(nc, m, pe, norm4, 2 * i + 1, f.xn, p_half, HALF)
                wave_tensor(nc, m, w, f, wave, pe, norm4, 2 * i + 1)

        @block.gpsimd
        def _(pool):
            last_row = pool.to_reg(SLOTS + P - 1)
            with pool.Fori(0, 2) as i:
                for q in range(2):
                    combine_pool(nc, m, rows, pool, comb, i * 2 + (q + B), last_row)
                norm_pool(nc, m, pool, norm4, 2 * i, HALF)
                wave_pool(nc, m, wave, pool, 2 * i)
                for q in range(2):
                    norm_pool(nc, m, pool, norm, i * 2 + (q + done))
                norm_pool(nc, m, pool, norm4, 2 * i + 1, HALF)
                wave_pool(nc, m, wave, pool, 2 * i + 1)

        @block.sync
        def _(sp):
            out = a["out"].rearrange("(t p) c -> p t c", p=P)
            with sp.Fori(0, 2) as i:
                sp.wait_ge(s_out, i + 1)
                sp.dma_start(out[:, bass.ds(i * HALF, HALF), :], m.x[:, bass.ds(i * HALF, HALF), :]
                             ).then_inc(s_stored, 16)
            sp.wait_ge(s_stored, 32)


def build(nc, a):
    with ExitStack() as ctx:
        m = allocate(nc, ctx)

        def sem(name):
            return ctx.enter_context(nc.semaphore(name))

        m.norm, m.route, m.combine = NormSems(sem, "norm"), RouteSems(sem, "route"), CombineSems(sem, "combine")
        m.experts = ExpertSems(sem)
        first_phase(nc, m, a, sem)
        experts_phase(nc, m, a, 0)
        middle_phase(nc, m, sem)
        experts_phase(nc, m, a, 1)
        w = fold_phase(nc, m, a, sem)
        last_phase(nc, m, w, a, sem)



def shape_constants():
    i = np.arange(P)
    consts = np.concatenate([np.eye(P), i[:, None] < i[None, :], i[None, :] > i[:, None],
                             np.tile(np.arange(NE), (P, 1))], axis=1).astype(np.float32)
    inv_freq = (1.0 / np.float32(10000.0) ** (np.arange(0, DH, 2, dtype=np.float32) / np.float32(DH))).astype(np.float32)
    angle = np.arange(T, dtype=np.float32)[:, None] * inv_freq[None, :]
    cos, sin = np.cos(angle), np.sin(angle)
    tables = np.stack([np.concatenate([cos, cos], 1), np.concatenate([-sin, sin], 1)], 1)
    tables = np.stack([tables * DH ** -0.5, tables], 2)
    rope = tables.reshape(TB, P, 2, 2, DH).transpose(1, 0, 2, 3, 4).reshape(P, -1)
    return consts, rope.astype(np.float32)


def kernel(**inputs):
    import concourse.bacc as _bacc
    from concourse.bass_utils import run_bass_kernel_spmd as _run

    v = {k: np.asarray(x) for k, x in inputs.items()}
    consts, rope = shape_constants()
    ffn, at = "L1_ffn_", "L1_attn_"
    turn = np.concatenate([np.arange(0, DH, 2), np.arange(1, DH, 2)])
    heads_first = lambda x: x.reshape(*x.shape[:-1], -1, DH)[..., turn].reshape(x.shape)
    vectors = [v[ffn + "amp_b"], v[ffn + "ph_b"], *v[ffn + "ent_pb"], *v[ffn + "path_b"].reshape(NL * PW, D),
               *v[ffn + "phase"].reshape(NL * PW, D), *v[ffn + "ln3_g"], *v[ffn + "ln3_b"], *v[ffn + "ln4_g"],
               *v[ffn + "ln4_b"], v[at + "bo"], heads_first(v[at + "bq"])]
    arrays = {
        "x": v["L0_attn_x"].reshape(TOK, D),
        "consts": consts,
        "rope": rope,
        "router": v["L0_ffn_gate_w"].T,
        "shared_gate": v["L0_ffn_shared_gate_w"].T,
        "shared_up": v["L0_ffn_shared_up_w"].T,
        "shared_down": v["L0_ffn_shared_down_w"].T,
        "gate_up": v["L0_ffn_gate_up_proj"].reshape(NE, KC, P, SHID).transpose(2, 0, 1, 3).reshape(P, -1),
        "down": v["L0_ffn_down_proj"].transpose(1, 0, 2).reshape(HID, -1),
        "qkv": v["L0_attn_w_qkv"].T,
        "proj": v["L0_attn_w_proj"].T,
        "ent_wT": v[ffn + "ent_w"].transpose(0, 2, 1),
        "ent_pw": v[ffn + "ent_pw"],
        "ent_b": v[ffn + "ent_b"].reshape(NL, EW // P, P).transpose(2, 0, 1).reshape(P, -1),
        "path_w": v[ffn + "path_w"].reshape(NL * PW, D, D),
        "amp_w": v[ffn + "amp_w"],
        "ph_w": v[ffn + "ph_w"],
        "rows": np.concatenate(vectors).reshape(1, -1),
        "kv_b": np.concatenate([heads_first(v[at + "bk"]), v[at + "bv"]]).reshape(1, -1),
        "Wq": heads_first(v[at + "Wq"]),
        "Wk": heads_first(v[at + "Wk"]),
        "Wv": v[at + "Wv"],
        "Wo": v[at + "Wo"],
    }
    nc = _bacc.Bacc("TRN2", target_bir_lowering=False, num_devices=1)
    sent, a = {}, {}
    for name, x in arrays.items():
        sent[f"in_{name}"] = np.ascontiguousarray(x)
        a[name] = nc.dram_tensor(f"in_{name}", sent[f"in_{name}"].shape, mybir.dt.from_np(x.dtype),
                                 kind="ExternalInput").ap()
    a["out"] = nc.dram_tensor("out_0", (TOK, D), F32, kind="ExternalOutput").ap()
    build(nc, a)
    r = _run(nc, [sent], core_ids=[0])
    return r.results[0]["out_0"].reshape(B, T, D)
```

```python
from contextlib import ExitStack

import numpy as np
import concourse.bass as bass
from concourse import mybir

F32 = mybir.dt.float32
BF16 = mybir.dt.bfloat16
U32 = mybir.dt.uint32
ALU = mybir.AluOpType
ACT = mybir.ActivationFunctionType
AX = mybir.AxisListType

P = 128
D = 256
KC = D // P
B, T = 4, 256
TOK = B * T
TILES = TOK // P
TB = T // P
NE, TOPK, CAP, HID, SHID = 64, 6, 64, 96, 192
PAIRS = NE // 2
SLOTS = NE * CAP
H, DH = 16, 16
HKV = 4
EPS = 1e-5
NL = 2
PW = 2
EW = 4 * D
MASKED = -1.0e30
PI = float(np.pi)


def flat(buf, first, shape):
    n = int(np.prod(shape))
    v = buf[:, first:first + n]
    if len(shape) == 2:
        return v.rearrange("p (a b) -> p a b", b=shape[1])
    if len(shape) == 3:
        return v.rearrange("p (a b c) -> p a b c", b=shape[1], c=shape[2])
    if len(shape) == 4:
        return v.rearrange("p (a b c d) -> p a b c d", b=shape[1], c=shape[2], d=shape[3])
    return v


class Chain:

    def __init__(self, engine, sem):
        self.engine, self.sem, self.links = engine, sem, 0
        engine.sem_clear(sem)

    def __call__(self, instruction):
        instruction.then_inc(self.sem, 1)
        self.links += 1
        self.engine.wait_ge(self.sem, self.links)

    def count(self, instruction):
        instruction.then_inc(self.sem, 1)
        self.links += 1


class Places:
    pass


def allocate(nc, ctx):
    m = Places()

    def sb(name, shape, dt=F32):
        return ctx.enter_context(nc.sbuf_tensor(name, shape, dt))

    m.w_gu = sb("w_gu", [P, NE * KC * SHID])
    m.w_dn = sb("w_dn", [P, NE * D])
    m.x = sb("x", [P, TILES, D])
    m.ident = sb("ident", [P, P])
    m.ident_b = sb("ident_b", [P, 3 * P], BF16)
    m.before_b = sb("before_b", [P, P], BF16)
    m.ones_b = sb("ones_b", [P, P], BF16)
    m.causal_b = sb("causal_b", [P, 3 * P], BF16)
    m.expert_no = sb("expert_no", [P, NE])
    m.rope = sb("rope", [P, TB, 2, 2, DH])
    m.w_router = sb("w_router", [P, KC, NE])
    m.w_sgu = sb("w_sgu", [P, KC, 2 * SHID])
    m.w_sdn = sb("w_sdn", [HID, 2, D])
    m.w_qkv = sb("w_qkv", [P, KC, 3 * D])
    m.w_proj = sb("w_proj", [P, KC, D])
    m.slots = sb("slots", [P, TILES, TOPK], U32)
    m.weights = sb("weights", [P, TILES, TOPK])
    m.taken = sb("taken", [P, NE], BF16)
    m.scatter_slots = [sb(f"scatter_slots{u}", [P, TB * TOPK], U32) for u in range(2)]
    m.gather_slots = sb("gather_slots", [P, TB * TOPK], U32)
    m.cur_weights = sb("cur_weights", [P, TB, TOPK])
    m.stats = sb("stats", [P, TILES, 6])
    m.mv = sb("mv", [P, TILES, 2])
    m.cur_mv = sb("cur_mv", [P, TB, 2])
    m.var_eps = sb("var_eps", [P, TILES])
    m.rstd = sb("rstd", [P, TILES])
    m.minus_half = sb("minus_half", [P, TILES])
    m.eps = sb("eps", [P, TILES])
    m.xn = sb("xn", [P, TB, D])
    m.xn_sent = sb("xn_sent", [P, TB, D])
    m.work = sb("work", [P, 3840])
    m.banks = ctx.enter_context(nc.psum_tensor("banks", [P, 8, 512], F32))
    m.expert_in = nc.dram_tensor("expert_in", [SLOTS, D], F32, kind="Internal").ap()
    m.expert_out = nc.dram_tensor("expert_out", [SLOTS + P, D], F32, kind="Internal").ap()
    return m



class NormSems:
    def __init__(self, sem, name):
        self.var = sem(f"{name}_variance_ready")
        self.rstd = sem(f"{name}_rstd_ready")
        self.xn = sem(f"{name}_normed_ready")
        self.turned = sem(f"{name}_transposed")
        self.xnT = sem(f"{name}_normed_T_ready")


def norm_vector(nc, m, eng, chain, s, turn, x_tiles, xn, tiles=TB, free=None):
    for t in range(tiles):
        chain(nc.vector.bn_stats(m.stats[:, t, :], x_tiles[t]))
    for t in range(tiles):
        chain(nc.vector.bn_aggr(m.mv[:, t, :], m.stats[:, t, :]))
    nc.vector.tensor_scalar(m.var_eps[:, 0:tiles], m.mv[:, 0:tiles, 1], EPS, None, ALU.add).then_inc(s.var, 1)
    if free:
        eng.wait_ge(*free)
    eng.wait_ge(s.rstd, turn + 1)
    for t in range(tiles):
        nc.vector.tensor_scalar(xn[:, t, :], x_tiles[t], m.mv[:, t, 0:1], m.rstd[:, t:t + 1],
                                ALU.subtract, ALU.mult).then_inc(s.xn, 1)


def norm_pool(nc, m, eng, s, turn, tiles=TB):
    eng.wait_ge(s.var, turn + 1)
    nc.gpsimd.tensor_tensor(m.rstd[:, 0:tiles], m.var_eps[:, 0:tiles], m.minus_half[:, 0:tiles],
                            ALU.pow).then_inc(s.rstd, 1)


def norm_tensor(nc, m, eng, s, turn, xn, out, tiles=TB):
    for t in range(tiles):
        eng.wait_ge(s.xn, turn * tiles + (t + 1))
        for c in range(KC):
            last = nc.tensor.transpose(out[:, c, t * P:(t + 1) * P], xn[:, t, c * P:(c + 1) * P], m.ident[:, :])
    last.then_inc(s.turned, 1)


def norm_scalar(nc, eng, s, turn, src, dst):
    eng.wait_ge(s.turned, turn + 1)
    nc.scalar.copy(dst, src).then_inc(s.xnT, 1)


class RouteSems:
    def __init__(self, sem, name):
        self.logits = sem(f"{name}_logits_ready")
        self.shared_in = sem(f"{name}_shared_gate_up_ready")
        self.neg_max = sem(f"{name}_neg_max_ready")
        self.exps = sem(f"{name}_exps_ready")
        self.mask = sem(f"{name}_choice_mask_ready")
        self.rank = sem(f"{name}_rank_ready")
        self.slots = [sem(f"{name}_slots_ready{u}") for u in range(2)]
        self.scattered = sem(f"{name}_rows_scattered")
        self.tanh = sem(f"{name}_shared_tanh_ready")
        self.hidden = sem(f"{name}_shared_hidden_ready")
        self.turned = sem(f"{name}_shared_hidden_turned")
        self.hiddenT = sem(f"{name}_shared_hidden_T_ready")
        self.shared_out = sem(f"{name}_shared_out_ready")
        self.banks_read = sem(f"{name}_banks_read")


class RoutePlaces:

    def __init__(self, m):
        w = m.work
        self.xnT = flat(w, 0, (KC, T))
        self.logits = flat(w, 512, (TB, NE))
        self.top = flat(w, 640, (TB, 8))
        self.neg_max = flat(w, 656, (TB,))
        self.sum = flat(w, 658, (TB,))
        self.rsum = flat(w, 660, (TB,))
        self.top_exp = flat(w, 664, (TB, 8))
        self.index_f = flat(w, 680, (TB, 8))
        self.rank = flat(w, 696, (TB, TOPK))
        self.keep = flat(w, 708, (TB, TOPK))
        self.slot_f = flat(w, 720, (TB, TOPK))
        self.index = w[:, 732:748].bitcast(U32).rearrange("p (a b) -> p a b", b=8)
        self.exps = flat(w, 748, (TB, NE))
        self.mask = w[:, 876:940].bitcast(BF16).rearrange("p (a b) -> p a b", b=NE)
        self.onehot = flat(w, 940, (TB, TOPK, NE))
        self.product = flat(w, 1708, (TB, TOPK, NE))
        self.tanh = flat(w, 2476, (TB, SHID))
        self.hidden = flat(w, 2860, (TB, SHID))
        self.hiddenT = flat(w, 3244, (2, T))
        self.p_logits = m.banks[:, 6, 0:TB * NE].rearrange("p (a b) -> p a b", b=NE)
        self.p_rank = m.banks[:, 6, TB * NE:2 * TB * NE].rearrange("p (a b) -> p a b", b=NE)
        self.p_shared = m.banks[:, 0:TB, :]
        self.p_hiddenT = m.banks[:, 2, :].rearrange("p (a b) -> p a b", b=T)
        self.p_out = m.banks[:, 3, :].rearrange("p (a b) -> p a b", b=D)


def route_tensor(nc, m, r, eng, s, ready, turn):
    eng.wait_ge(*ready)
    for t in range(TB):
        for c in range(KC):
            last = nc.tensor.matmul(r.p_logits[:, t, :], r.xnT[:, c, t * P:(t + 1) * P], m.w_router[:, c, :],
                                    start=(c == 0), stop=(c == KC - 1))
    last.then_inc(s.logits, 1)
    for t in range(TB):
        for c in range(KC):
            last = nc.tensor.matmul(r.p_shared[:, t, 0:2 * SHID], r.xnT[:, c, t * P:(t + 1) * P],
                                    m.w_sgu[:, c, :], start=(c == 0), stop=(c == KC - 1))
        last.then_inc(s.shared_in, 1)
    eng.wait_ge(s.mask, turn + 1)
    for t in range(TB):
        nc.tensor.matmul(r.p_rank[:, t, :], m.before_b[:, :], r.mask[:, t, :], start=True, stop=False)
        last = nc.tensor.matmul(r.p_rank[:, t, :], m.ones_b[:, :], m.taken[:, :], start=False, stop=(t == 0))
        if t == 1:
            last = nc.tensor.matmul(r.p_rank[:, t, :], m.ones_b[:, :], r.mask[:, 0, :], start=False, stop=True)
    last.then_inc(s.rank, 1)
    for t in range(TB):
        eng.wait_ge(s.hidden, turn * TB + (t + 1))
        for j in range(2):
            last = nc.tensor.transpose(r.p_hiddenT[0:HID, j, t * P:(t + 1) * P],
                                       r.hidden[:, t, j * HID:(j + 1) * HID], m.ident[:, :])
    last.then_inc(s.turned, 1)
    eng.wait_ge(s.hiddenT, turn + 1)
    for t in range(TB):
        for j in range(2):
            last = nc.tensor.matmul(r.p_out[:, t, :], r.hiddenT[0:HID, j, t * P:(t + 1) * P], m.w_sdn[:, j, :],
                                    start=(j == 0), stop=(j == 1))
    last.then_inc(s.shared_out, 1)


def route_scalar(nc, r, eng, s, turn):
    eng.wait_ge(s.neg_max, turn + 1)
    for t in range(TB):
        nc.scalar.activation(r.exps[:, t, :], r.logits[:, t, :], ACT.Exp, bias=r.neg_max[:, t:t + 1],
                             accum_out=r.sum[:, t:t + 1])
        last = nc.scalar.activation(r.top_exp[:, t, :], r.top[:, t, :], ACT.Exp, bias=r.neg_max[:, t:t + 1])
    last.then_inc(s.exps, 1)
    for t in range(TB):
        eng.wait_ge(s.shared_in, turn * TB + (t + 1))
        nc.scalar.activation(r.tanh[:, t, :], r.p_shared[:, t, 0:SHID], ACT.Tanh, scale=0.5).then_inc(s.tanh, 1)
    eng.wait_ge(s.turned, turn + 1)
    nc.scalar.copy(r.hiddenT[0:HID, :, :], r.p_hiddenT[0:HID, :, :]).then_inc(s.hiddenT, 1)


def route_vector(nc, m, r, eng, chain, s, turn, sequence, x_tiles, u):
    eng.wait_ge(s.logits, turn + 1)
    chain(nc.vector.tensor_copy(r.logits[:, :, :], r.p_logits))
    for t in range(TB):
        last = nc.vector.max(r.top[:, t, :], r.logits[:, t, :])
        if t == 0:
            chain.count(last)
    chain(last)
    nc.vector.tensor_scalar(r.neg_max, r.top[:, :, 0], -1.0, None, ALU.mult).then_inc(s.neg_max, 1)
    for t in range(TB):
        chain(nc.vector.max_index(r.index[:, t, :], r.top[:, t, :], r.logits[:, t, :]))
    chain(nc.vector.tensor_copy(r.index_f, r.index))
    numbers = m.expert_no[:, :].unsqueeze(1).broadcast_to([P, TOPK, NE])
    for t in range(TB):
        chosen = r.index_f[:, t, 0:TOPK].unsqueeze(2).broadcast_to([P, TOPK, NE])
        chain(nc.vector.tensor_tensor(r.onehot[:, t], numbers, chosen, ALU.is_equal))
    for t in range(TB):
        with nc.allow_low_precision(reason="sums of zeros and a one"):
            last = nc.vector.tensor_reduce(r.mask[:, t, :], r.onehot[:, t].rearrange("p k e -> p e k"), AX.X,
                                           ALU.add)
        if t == 0:
            chain(last)
    last.then_inc(s.mask, 1)
    for t in range(TB):
        eng.wait_ge(s.tanh, turn * TB + (t + 1))
        chain(nc.vector.scalar_tensor_tensor(out=r.tanh[:, t, :], in0=r.tanh[:, t, :], scalar=1.0,
                                             in1=r.p_shared[:, t, 0:SHID], op0=ALU.add, op1=ALU.mult))
        nc.vector.tensor_tensor(r.hidden[:, t, :], r.tanh[:, t, :], r.p_shared[:, t, SHID:2 * SHID],
                                ALU.mult).then_inc(s.hidden, 1)
    eng.wait_ge(s.rank, turn + 1)
    for t in range(TB):
        ranks = r.p_rank[:, t, :].unsqueeze(1).broadcast_to([P, TOPK, NE])
        chain(nc.vector.tensor_tensor(r.product[:, t], r.onehot[:, t], ranks, ALU.mult))
    chain(nc.vector.tensor_reduce(r.rank, r.product, AX.X, ALU.add))
    chain(nc.vector.tensor_scalar(r.keep, r.rank, float(CAP), None, ALU.is_lt))
    chain(nc.vector.scalar_tensor_tensor(out=r.slot_f, in0=r.index_f[:, :, 0:TOPK], scalar=float(CAP),
                                         in1=r.rank, op0=ALU.mult, op1=ALU.add))
    chain(nc.vector.scalar_tensor_tensor(out=r.slot_f, in0=r.slot_f, scalar=-float(SLOTS), in1=r.keep,
                                         op0=ALU.add, op1=ALU.mult))
    chain(nc.vector.tensor_scalar(m.scatter_slots[u][:, :].rearrange("p (a b) -> p a b", b=TOPK), r.slot_f,
                                  float(SLOTS), None, ALU.add))
    nc.vector.tensor_copy(m.slots[:, bass.ds(sequence * TB, TB), :],
                          m.scatter_slots[u][:, :].rearrange("p (a b) -> p a b", b=TOPK)).then_inc(s.slots[u], 1)
    chain(nc.vector.tensor_tensor(m.taken[:, :], m.taken[:, :], r.mask[:, 0, :], ALU.add))
    chain(nc.vector.tensor_tensor(m.taken[:, :], m.taken[:, :], r.mask[:, 1, :], ALU.add))
    eng.wait_ge(s.exps, turn + 1)
    chain(nc.vector.reciprocal(r.rsum, r.sum))
    for t in range(TB):
        chain(nc.vector.tensor_scalar(r.top_exp[:, t, 0:TOPK], r.top_exp[:, t, 0:TOPK], r.rsum[:, t:t + 1], 0.25,
                                      ALU.mult, ALU.mult))
    chain(nc.vector.tensor_tensor(m.weights[:, bass.ds(sequence * TB, TB), :], r.top_exp[:, :, 0:TOPK], r.keep,
                                  ALU.mult))
    eng.wait_ge(s.shared_out, turn + 1)
    for t in range(TB):
        chain(nc.vector.scalar_tensor_tensor(out=x_tiles[t], in0=r.p_out[:, t, :], scalar=0.25, in1=x_tiles[t],
                                             op0=ALU.mult, op1=ALU.add))
    eng.sem_inc(s.banks_read, 1)


SCATTER = 16 * TB * TOPK


def scattered(turn):
    return turn * SCATTER + SCATTER


def route_pool(nc, m, eng, s, xn, u, last_slot):
    eng.wait_ge(s.slots[u], 1)
    eng.sem_clear(s.slots[u])
    for t in range(TB):
        for k in range(TOPK):
            at = t * TOPK + k
            nc.gpsimd.indirect_dma_start(
                out=m.expert_in, out_offset=bass.IndirectOffsetOnAxis(m.scatter_slots[u][:, at:at + 1], 0),
                in_=xn[:, t, :], in_offset=None, bounds_check=last_slot, oob_is_err=False
            ).then_inc(s.scattered, 16)



GROUP = 8
GROUPS = NE // GROUP
EARLY_GROUPS = 3


def load_expert_group(m, a, eng, g):
    if not isinstance(g, int) or g > 0:
        eng.wait_ge(m.s_expert_weights, g * 32)
    n, k = GROUP * KC * SHID, GROUP * D
    for own, source, width in ((m.w_gu, a["gate_up"], n), (m.w_dn[0:HID], a["down"], k)):
        eng.dma_start(own[:, bass.ds(g * width, width)], source[:, bass.ds(g * width, width)]
                      ).then_inc(m.s_expert_weights, 16)


def first_phase(nc, m, a, sem):
    s_const = sem("constants_loaded")
    s_x = sem("x_loaded")
    s_w = sem("small_weights_loaded")
    s_exp = sem("expert_weights_loaded")
    s_made = m.made = sem("constants_made")
    s_zero = sem("zeros_made")
    s_zeroed = sem("scratch_zeroed")
    v_chain = sem("first_vector_chain")
    norm, s = m.norm, m.route
    r = RoutePlaces(m)
    consts = m.w_dn[:, 0:512]
    zeros = m.w_dn[:, 1024:3072]
    xn = [m.xn, m.xn_sent]
    m.s_expert_weights, m.s_attn_weights = s_exp, sem("attention_weights_loaded")
    x_in = a["x"].rearrange("(t p) c -> p t c", p=P)
    s_free = sem("places_to_scatter_from_free")
    s_stats = sem("all_means_and_deviations_ready")

    with nc.Block() as block:
        @block.sync
        def _(sp):
            for h in range(2):
                tiles = slice(h * TILES // 2, (h + 1) * TILES // 2)
                sp.dma_start(m.x[:, tiles, :], x_in[:, tiles, :]).then_inc(s_x, 16)
            sp.dma_start(m.w_router[:, :, :], a["router"].rearrange("(c p) n -> p c n", p=P)).then_inc(s_w, 16)
            sp.dma_start(m.w_sgu[:, :, 0:SHID], a["shared_gate"].rearrange("(c p) n -> p c n", p=P)).then_inc(s_w, 16)
            sp.dma_start(m.w_sgu[:, :, SHID:2 * SHID],
                         a["shared_up"].rearrange("(c p) n -> p c n", p=P)).then_inc(s_w, 16)
            sp.dma_start(m.w_sdn[:, :, :], a["shared_down"].rearrange("(j p) n -> p j n", p=HID)).then_inc(s_w, 16)
            sp.wait_ge(s_zero, 1)
            sp.wait_ge(s_x, 32)
            for g in range(4):
                sp.dma_start(m.expert_in[g * 1024:(g + 1) * 1024, :].rearrange("(p n) d -> p (n d)", p=P),
                             zeros).then_inc(s_zeroed, 16)
            sp.dma_start(m.expert_out[SLOTS:SLOTS + P, :], zeros[:, 0:D]).then_inc(s_zeroed, 16)
            sp.wait_ge(s_zeroed, 80)
            sp.wait_ge(s_made, 9)
            for g in range(EARLY_GROUPS):
                if g:
                    sp.wait_ge(s.scattered, scattered(g - 1))
                load_expert_group(m, a, sp, g)

        @block.scalar
        def _(act):
            act.dma_start(consts[:, 0:448], a["consts"][:, 0:448]).then_inc(s_const, 16)
            act.dma_start(m.rope[:, :, :, :, :], a["rope"].rearrange("p (a b c d) -> p a b c d", b=2, c=2, d=DH)
                          ).then_inc(s_const, 16)
            with act.Fori(0, B) as i:
                norm_scalar(nc, act, norm, i, m.banks[:, 7, :], m.work[:, 0:512])
                route_scalar(nc, r, act, s, i)

        @block.vector
        def _(dve):
            nc.vector.memset(zeros, 0.0).then_inc(s_zero, 1)
            nc.vector.memset(m.minus_half[:, :], -0.5)
            nc.vector.memset(m.eps[:, :], EPS)
            nc.vector.memset(m.taken[:, :], 0.0)
            nc.vector.memset(m.ones_b[:, :], 1.0)
            dve.wait_ge(s_const, 32)
            nc.vector.tensor_copy(m.ident[:, :], consts[:, 0:P]).then_inc(s_made, 1)
            for wide in (m.ident_b, m.causal_b):
                nc.vector.memset(wide[:, P:2 * P], 0.0).then_inc(s_made, 1)
            for first in (0, 2 * P):
                nc.vector.tensor_copy(m.ident_b[:, first:first + P], consts[:, 0:P]).then_inc(s_made, 1)
                nc.vector.tensor_scalar(m.causal_b[:, first:first + P], consts[:, 2 * P:3 * P], MASKED, None, ALU.mult
                                        ).then_inc(s_made, 1)
            nc.vector.tensor_copy(m.before_b[:, :], consts[:, P:2 * P]).then_inc(s_made, 1)
            nc.vector.tensor_copy(m.expert_no[:, :], consts[:, 3 * P:3 * P + NE]).then_inc(s_made, 1)
            dve.wait_ge(s_made, 9)
            dve.wait_ge(s_x, 32)
            stats_chain = Chain(dve, v_chain)
            for t in range(TILES):
                last = nc.vector.bn_stats(m.stats[:, t, :], m.x[:, t, :])
                stats_chain.count(last)
            dve.wait_ge(v_chain, stats_chain.links)
            for t in range(TILES):
                stats_chain.count(nc.vector.bn_aggr(m.mv[:, t, :], m.stats[:, t, :]))
            dve.wait_ge(v_chain, stats_chain.links)
            nc.vector.tensor_scalar(m.var_eps[:, :], m.mv[:, :, 1], EPS, None, ALU.add).then_inc(s_stats, 1)
            dve.sem_inc(s_free, 2)
            dve.sem_inc(norm.var, B)
            dve.sem_inc(norm.rstd, B)
            dve.wait_ge(s_stats, 2)
            with dve.Fori(0, B // 2) as i:
                for u in range(2):
                    turn = i * 2 + u
                    chain = Chain(dve, v_chain)
                    x_tiles = [m.x[:, i * (2 * TB) + (u * TB + t), :] for t in range(TB)]
                    chain(nc.vector.tensor_copy(m.cur_mv[:, :, :], m.mv[:, bass.ds(i * (2 * TB) + u * TB, TB), :]))
                    dve.wait_ge(s_free, turn + 1)
                    for t in range(TB):
                        nc.vector.tensor_scalar(xn[u][:, t, :], x_tiles[t], m.cur_mv[:, t, 0:1], m.cur_mv[:, t, 1:2],
                                                ALU.subtract, ALU.mult).then_inc(norm.xn, 1)
                    route_vector(nc, m, r, dve, chain, s, turn, turn, x_tiles, u)

        @block.tensor
        def _(pe):
            pe.wait_ge(s_made, 9)
            pe.wait_ge(s_w, 64)
            with pe.Fori(0, B // 2) as i:
                for u in range(2):
                    turn = i * 2 + u
                    norm_tensor(nc, m, pe, norm, turn, xn[u], m.banks[:, 7, :].rearrange("p (a b) -> p a b", b=T))
                    route_tensor(nc, m, r, pe, s, (norm.xnT, turn + 1), turn)

        @block.gpsimd
        def _(pool):
            last_slot = pool.to_reg(SLOTS - 1)
            pool.wait_ge(s_stats, 1)
            nc.gpsimd.tensor_tensor(m.mv[:, :, 1], m.var_eps[:, :], m.minus_half[:, :], ALU.pow).then_inc(s_stats, 1)
            pool.wait_ge(s_zeroed, 80)
            with pool.Fori(0, B // 2) as i:
                for u in range(2):
                    route_pool(nc, m, pool, s, xn[u], u, last_slot)
                    pool.wait_ge(s.scattered, scattered(i * 2 + u))
                    pool.sem_inc(s_free, 1)



RING = 4


class ExpertSems:
    def __init__(self, sem):
        self.rows = [sem(f"expert_rows_loaded{b}") for b in range(RING)]
        self.rows_turned = sem("expert_rows_turned")
        self.rowsT = sem("expert_rows_T_ready")
        self.gate_up = sem("expert_gate_up_ready")
        self.tanh = sem("expert_tanh_ready")
        self.gated = sem("expert_gated_ready")
        self.hidden = sem("expert_hidden_ready")
        self.hidden_turned = sem("expert_hidden_turned")
        self.hiddenT = sem("expert_hidden_T_ready")
        self.out = sem("expert_out_ready")
        self.copied = sem("expert_out_copied")
        self.stored = [sem(f"expert_out_stored{b}") for b in range(RING)]


class with_turn:

    def __init__(self, stage):
        self.stage = stage


def in_steps(engine, stages, items=PAIRS, ring=RING):
    longest = max(lag for lag, _ in stages)
    turns = (items - longest) // ring

    def run(stage, item, place, turn):
        if isinstance(stage, with_turn):
            stage.stage(item, place, turn)
        else:
            stage(item, place)

    def peeled(p):
        for lag, stage in stages:
            if 0 <= p - lag < items:
                run(stage, p - lag, (p - lag) % ring, (p - lag) // ring)

    for p in range(longest):
        peeled(p)
    with engine.Fori(0, turns) as i:
        for u in range(ring):
            for lag, stage in stages:
                at = longest + u - lag
                run(stage, i * ring + at, at % ring, i + at // ring)
    for p in range(longest + turns * ring, items + longest):
        peeled(p)


def experts_phase(nc, m, a, call):
    x, w = m.experts, m.work
    rows = [flat(w, 256 * b, (D,)) for b in range(RING)]
    rowsT = [flat(w, 1024 + 256 * b, (KC, P)) for b in range(2)]
    tanh = [flat(w, 1536 + 192 * b, (2, HID)) for b in range(2)]
    hidden = [flat(w, 1920 + 192 * b, (2, HID)) for b in range(2)]
    hiddenT = [flat(w, 2304 + 128 * b, (2, CAP)) for b in range(2)]
    out = [flat(w, 2560 + 512 * b, (2, D)) for b in range(2)]
    p_rowsT = [m.banks[:, b, 0:D].rearrange("p (c t) -> p c t", t=P) for b in range(2)]
    p_gu = [m.banks[0:CAP, 2 + b, 0:2 * SHID].rearrange("p (e n) -> p e n", n=SHID) for b in range(2)]
    p_hiddenT = [m.banks[0:HID, 4 + b, 0:2 * CAP].rearrange("p (e n) -> p e n", n=CAP) for b in range(2)]
    p_out = [m.banks[0:CAP, 6 + b, :].rearrange("p (e n) -> p e n", n=D) for b in range(2)]
    w_gu = m.w_gu[:, :].rearrange("p (e c n) -> p e c n", c=KC, n=SHID)
    w_dn = m.w_dn[0:HID, :].rearrange("p (e n) -> p e n", n=D)
    before = call * PAIRS

    def rows_loaded(pair, b):
        return pair * (16 // RING) + (16 + (before - b) * 16 // RING)

    def out_stored(pair, b):
        return pair * (32 // RING) + (64 + (before - b) * 32 // RING)

    with nc.Block() as block:
        @block.sync
        def _(sp):
            if call == 0:
                sp.sem_inc(x.rows_turned, RING)

            def load(pair, b):
                sp.wait_ge(x.rows_turned, pair + (before + 1))
                sp.dma_start(rows[b], m.expert_in[bass.ds(pair * P, P), :]).then_inc(x.rows[b], 16)

            fetching = GROUPS - EARLY_GROUPS if call == 0 else 0
            if fetching:
                with sp.Fori(0, fetching) as i:
                    for b in range(RING):
                        load(i * RING + b, b)
                    load_expert_group(m, a, sp, i + EARLY_GROUPS)
                sp.dma_start(m.w_qkv[:, :, :], a["qkv"].rearrange("(c p) n -> p c n", p=P)
                             ).then_inc(m.s_attn_weights, 16)
                sp.dma_start(m.w_proj[:, :, :], a["proj"].rearrange("(c p) n -> p c n", p=P)
                             ).then_inc(m.s_attn_weights, 16)
            starts = [fetching, GROUPS] if call == 0 else [0, 4, 5, 7, GROUPS]
            for part, (first, end) in enumerate(zip(starts, starts[1:])):
                if part:
                    groups_used = first - 1
                    sp.wait_ge(x.gate_up, before + groups_used * RING)
                    load_last_weights(m, a, sp, part, groups_used)
                with sp.Fori(first, end) as i:
                    for b in range(RING):
                        load(i * RING + b, b)

        @block.scalar
        def _(act):
            if call == 0:
                act.sem_inc(x.copied, 2)
                for b in range(RING):
                    act.sem_inc(x.stored[b], 32)

            def copy_rows(pair, b):
                act.wait_ge(x.rows_turned, pair + (before + RING + 1))
                nc.scalar.copy(rowsT[b % 2], p_rowsT[b % 2]).then_inc(x.rowsT, 1)

            def gate(pair, b):
                act.wait_ge(x.gate_up, pair + (before + 1))
                nc.scalar.activation(tanh[b % 2][0:CAP], p_gu[b % 2][:, :, 0:HID], ACT.Tanh,
                                     scale=0.5).then_inc(x.tanh, 1)

            def store(pair, b):
                act.wait_ge(x.out, pair + (before + 1))
                act.wait_ge(x.stored[(b + 2) % RING], out_stored(pair - 2, (b + 2) % RING))
                nc.scalar.copy(out[b % 2][0:CAP], p_out[b % 2]).then_inc(x.copied, 1)
                act.wait_ge(x.copied, pair + (before + 3))
                for e in range(2):
                    act.dma_start(m.expert_out[bass.ds(pair * P + e * CAP, CAP), :],
                                  out[b % 2][0:CAP, e, :]).then_inc(x.stored[b], 16)

            in_steps(act, [(0, copy_rows), (1, gate), (3, store)])
            for b in range(RING):
                act.wait_ge(x.stored[b], out_stored(PAIRS - RING + b, b))

        @block.vector
        def _(dve):
            def gated(pair, b):
                dve.wait_ge(x.tanh, pair + (before + 1))
                nc.vector.scalar_tensor_tensor(out=tanh[b % 2][0:CAP], in0=tanh[b % 2][0:CAP], scalar=1.0,
                                               in1=p_gu[b % 2][:, :, 0:HID], op0=ALU.add,
                                               op1=ALU.mult).then_inc(x.gated, 1)
                dve.wait_ge(x.gated, pair + (before + 1))
                nc.vector.tensor_tensor(hidden[b % 2][0:CAP], tanh[b % 2][0:CAP], p_gu[b % 2][:, :, HID:2 * HID],
                                        ALU.mult).then_inc(x.hidden, 1)

            def copy_hidden(pair, b):
                dve.wait_ge(x.hidden_turned, pair + (before + 1))
                nc.vector.tensor_copy(hiddenT[b % 2][0:HID], p_hiddenT[b % 2]).then_inc(x.hiddenT, 1)

            in_steps(dve, [(1, gated), (2, copy_hidden)])

        @block.tensor
        def _(pe):
            if call == 1:
                pe.wait_ge(m.s_refetched, 48)

            def turn_rows(pair, b):
                pe.wait_ge(x.rows[b], rows_loaded(pair, b))
                for c in range(KC):
                    last = nc.tensor.transpose(p_rowsT[b % 2][:, c, :], rows[b][:, c * P:(c + 1) * P], m.ident[:, :])
                last.then_inc(x.rows_turned, 1)

            def gate_up(pair, b, turn):
                pe.wait_ge(m.s_expert_weights, (turn + 1) * 32)
                pe.wait_ge(x.rowsT, pair + (before + 1))
                for e in range(2):
                    for c in range(KC):
                        last = nc.tensor.matmul(p_gu[b % 2][:, e, :], rowsT[b % 2][:, c, e * CAP:(e + 1) * CAP],
                                                w_gu[:, pair * 2 + e, c, :], start=(c == 0), stop=(c == KC - 1))
                last.then_inc(x.gate_up, 1)

            def turn_hidden(pair, b):
                pe.wait_ge(x.hidden, pair + (before + 1))
                for e in range(2):
                    last = nc.tensor.matmul(p_hiddenT[b % 2][:, e, :], hidden[b % 2][0:CAP, e, :],
                                            m.ident[0:CAP, 0:CAP], start=True, stop=True)
                last.then_inc(x.hidden_turned, 1)

            def down(pair, b):
                pe.wait_ge(x.hiddenT, pair + (before + 1))
                pe.wait_ge(x.copied, pair + (before + 1))
                for e in range(2):
                    last = nc.tensor.matmul(p_out[b % 2][:, e, :], hiddenT[b % 2][0:HID, e, :],
                                            w_dn[:, pair * 2 + e, :], start=True, stop=True)
                last.then_inc(x.out, 1)

            in_steps(pe, [(0, turn_rows), (1, with_turn(gate_up)), (2, turn_hidden), (3, down)])



UNITS = 16
GROUPS4 = UNITS // 4
UPAIRS = UNITS // 2
COPIES = 5
SLOTS3 = 3


class AttnSems:
    def __init__(self, sem, name):
        self.qkv = sem(f"{name}_qkv_ready")
        self.biased = sem(f"{name}_qkv_biased")
        self.v = sem(f"{name}_v_ready")
        self.rope = sem(f"{name}_rope_ready")
        self.turned = sem(f"{name}_qk_turned")
        self.qkT = sem(f"{name}_qk_T_ready")
        self.scores = sem(f"{name}_scores_ready")
        self.neg_max = sem(f"{name}_neg_max_ready")
        self.q_turned = sem(f"{name}_q_with_max_turned")
        self.qmT = sem(f"{name}_q_with_max_T_ready")
        self.scoresT = sem(f"{name}_scores_T_ready")
        self.probs = sem(f"{name}_probs_T_ready")
        self.pv = sem(f"{name}_pv_ready")
        self.pv_copied = sem(f"{name}_pv_copied")
        self.back = sem(f"{name}_pv_turned_back")
        self.y = sem(f"{name}_y_ready")
        self.y_turned = sem(f"{name}_y_turned")
        self.yT = sem(f"{name}_y_T_ready")
        self.proj = sem(f"{name}_proj_ready")


class AttnPlaces:

    def __init__(self, m, heads, area, work, xnT, kT, w_qkv, w_proj, bias=None):
        self.heads, self.sequences = heads, UNITS // heads
        self.tiles, self.width = TB * self.sequences, heads * DH
        self.w_qkv, self.w_proj, self.bias, self.xnT = w_qkv, w_proj, bias, xnT
        self.qk = flat(area, 0, (self.tiles, 2 * heads, 32))
        self.qT = flat(area, 2048, (GROUPS4, T))
        self.kT = kT.rearrange("p (g j t) -> p g j t", j=4, t=T)
        self.v = flat(area, 4096, (self.tiles, heads, 32))
        self.pT = [flat(area, 5120 + 768 * b, (2, 3 * P)) for b in range(SLOTS3)]
        self.rsum = flat(area, 7424, (2, UNITS))
        self.y = flat(work, 0, (2, UNITS * DH))
        self.tmp = flat(work, 512, (self.tiles, 2 * self.width))
        self.pv = flat(work, 1536, (GROUPS4, T))
        self.yT = flat(work, 2560, (1024,))
        self.qkv_sb = flat(work, 3584, (self.tiles, 3 * self.width)) if bias is not None else None
        self.p_pairs = [m.banks[:, 2 * b:2 * b + 2, 0:3 * P] for b in range(SLOTS3)]
        self.one_sequence = self.sequences == 1

    def group(self, g, t):
        return (t, 4 * g) if self.one_sequence else (TB * g + t, 0)

    def back(self, m, g, t):
        bank, col = (2 + t, g) if self.one_sequence else (2 + g // 2, g % 2 * TB + t)
        return m.banks[:, bank, col * P:(col + 1) * P]


def attn_tensor(nc, m, s, a, eng, ready, turn):
    n = a.width
    for t in range(a.tiles):
        eng.wait_ge(*ready(t))
        if a.one_sequence:
            parts = [(2 * t, 0, 0, 2 * n), (2 * t + 1, 0, 2 * n, 3 * n)]
        else:
            parts = [(t // 2, t % 2 * 3 * n, 0, 3 * n)]
        for bank, at, first, end in parts:
            for c in range(KC):
                last = nc.tensor.matmul(m.banks[:, bank, at:at + end - first], a.xnT[:, c, t * P:(t + 1) * P],
                                        a.w_qkv[:, c, first:end], start=(c == 0), stop=(c == KC - 1))
        last.then_inc(s.qkv, 1)
    for t in range(a.tiles):
        eng.wait_ge(s.rope, turn * a.tiles + (t + 1))
        groups = range(GROUPS4) if a.one_sequence else [t // TB]
        for g in groups:
            for k in range(2):
                place, first = GROUPS4 * k + g, (4 * g if a.one_sequence else 0) + k * a.heads
                last = nc.tensor.transpose(
                    m.banks[:, 4 + place // 2, place % 2 * T + t % TB * P:place % 2 * T + (t % TB + 1) * P],
                    a.qk[:, t, first:first + 4, :].rearrange("p h d -> p (h d)"), m.ident[:, :])
    last.then_inc(s.turned, 1)
    eng.wait_ge(s.qkT, turn * COPIES + COPIES)

    def scores(p):
        if p >= SLOTS3:
            eng.wait_ge(s.neg_max, turn * UPAIRS + (p - SLOTS3 + 1))
        outs = [m.banks[:, 2 * (p % SLOTS3) + j, 0:3 * P] for j in range(2)]
        for out in outs:
            nc.tensor.matmul(out, m.ident_b[:, 0:P], m.causal_b[:, :], start=True, stop=False)
        for j, out in enumerate(outs):
            u = 2 * p + j
            q, k = a.qT[:, u // 4, :], a.kT[:, u // 4, u % 4, :]
            nc.tensor.matmul(out[:, 0:P], q[:, 0:P], k[:, 0:P], start=False, stop=False)
            last = nc.tensor.matmul(out[:, P:3 * P], q[:, P:T], k[:, 0:T], start=False, stop=True)
        last.then_inc(s.scores, 1)

    def turn_q(g):
        eng.wait_ge(s.neg_max, turn * UPAIRS + (2 * g + 2))
        if g >= 2:
            eng.wait_ge(s.qmT, turn * GROUPS4 + (g - 1))
        for t in range(TB):
            tile, head = a.group(g, t)
            last = nc.tensor.transpose(m.banks[:, 6 + g % 2, t * P:(t + 1) * P],
                                       a.qk[:, tile, head:head + 4, :].rearrange("p h d -> p (h d)"), m.ident[:, :])
        last.then_inc(s.q_turned, 1)

    def scores_T(p):
        if p < SLOTS3:
            eng.wait_ge(s.neg_max, turn * UPAIRS + (UPAIRS - SLOTS3 + p + 1))
        else:
            eng.wait_ge(s.probs, turn * UPAIRS + (p - SLOTS3 + 1))
        eng.wait_ge(s.qmT, turn * GROUPS4 + (p // 2 + 1))
        outs = [m.banks[:, 2 * ((p + UPAIRS) % SLOTS3) + j, 0:3 * P] for j in range(2)]
        for out in outs:
            nc.tensor.matmul(out, m.causal_b[:, 0:P], m.ident_b[:, :], start=True, stop=False)
        for j, out in enumerate(outs):
            u = 2 * p + j
            q, k = a.qT[:, u // 4, :], a.kT[:, u // 4, u % 4, :]
            nc.tensor.matmul(out[:, 0:T], k[:, 0:P], q[:, 0:T], start=False, stop=False)
            last = nc.tensor.matmul(out[:, T:3 * P], k[:, P:T], q[:, P:T], start=False, stop=True)
        last.then_inc(s.scoresT, 1)

    def values(p):
        eng.wait_ge(s.probs, turn * UPAIRS + (p + 1))
        for j in range(2):
            u = 2 * p + j
            g, rows = u // 4, slice(32 * (u % 4), 32 * (u % 4) + 32)
            out, probs = m.banks[rows, 6 + g // 2, g % 2 * T:(g % 2 + 1) * T], a.pT[p % SLOTS3][:, j, :]
            (first, head), (second, _) = a.group(g, 0), a.group(g, 1)
            nc.tensor.matmul(out, a.v[:, first, head + u % 4, :], probs[:, 0:T], start=True, stop=False)
            last = nc.tensor.matmul(out[:, P:T], a.v[:, second, head + u % 4, :], probs[:, T:3 * P],
                                    start=False, stop=True)
        last.then_inc(s.pv, 1)

    def turn_back(half):
        eng.wait_ge(s.pv_copied, turn * 2 + (half + 1))
        for g in (2 * half, 2 * half + 1):
            for t in range(TB):
                last = nc.tensor.transpose(a.back(m, g, t), a.pv[:, g, t * P:(t + 1) * P], m.ident[:, :])
        last.then_inc(s.back, 1)

    for p in range(UPAIRS):
        scores(p)
        if p >= 3 and p % 2 == 1:
            turn_q((p - 3) // 2)
    eng.wait_ge(s.v, turn * a.tiles + a.tiles)
    scores_T(0)
    scores_T(1)
    turn_q(GROUPS4 - 1)
    scores_T(2)
    for p in range(UPAIRS):
        values(p)
        if p + SLOTS3 < UPAIRS:
            scores_T(p + SLOTS3)
        if p == UPAIRS - 2:
            turn_back(0)
    turn_back(1)
    eng.wait_ge(s.y, turn * 2 + 2)
    if a.one_sequence:
        for t in range(TB):
            for c in range(KC):
                last = nc.tensor.matmul(m.banks[:, 4, c * T + t * P:c * T + (t + 1) * P],
                                        a.y[:, t, c * P:(c + 1) * P], m.ident[:, :], start=True, stop=True)
        last.then_inc(s.y_turned, 1)
        eng.wait_ge(s.yT, turn + 1)
        for t in range(TB):
            for c in range(KC):
                last = nc.tensor.matmul(m.banks[:, 6, t * D:(t + 1) * D], a.yT[:, c * T + t * P:c * T + (t + 1) * P],
                                        a.w_proj[:, c, :], start=(c == 0), stop=(c == KC - 1))
        last.then_inc(s.proj, 1)
    else:
        for t in range(a.tiles):
            last = nc.tensor.matmul(m.banks[0:n, 4 + t // 4, t % 4 * P:(t % 4 + 1) * P],
                                    a.y[:, t // 4, t % 4 * n:(t % 4 + 1) * n], m.ident[:, :], start=True, stop=True)
            if t % 4 == 3:
                last.then_inc(s.y_turned, 1)
        for t in range(a.tiles):
            eng.wait_ge(s.yT, t // 4 + 1)
            last = nc.tensor.matmul(m.banks[:, (6 + t // 2) % 8, t % 2 * D:(t % 2 + 1) * D],
                                    a.yT[0:n, t * P:(t + 1) * P], a.w_proj[0:n, 0, :], start=True, stop=True)
            if t % 2:
                last.then_inc(s.proj, 1)


def copy_k(m, copy, s, a, j):
    rows = slice(32 * j, 32 * (j + 1))
    copy(a.kT[rows, :, j, :], m.banks[rows, 6:8, :].rearrange("p b (g t) -> p (b g) t", t=T)).then_inc(s.qkT, 1)


def attn_scalar(nc, m, s, a, eng, turn):
    n = a.width
    for t in range(a.tiles):
        if a.one_sequence:
            eng.wait_ge(s.qkv, turn * a.tiles + (t + 1))
            v = m.banks[:, 2 * t + 1, 0:n]
        else:
            eng.wait_ge(s.biased, t + 1)
            v = a.qkv_sb[:, t, 2 * n:3 * n]
        nc.scalar.copy(a.v[:, t, :, 0:DH], v.rearrange("p (h d) -> p h d", d=DH)).then_inc(s.v, 1)
    eng.wait_ge(s.turned, turn + 1)
    nc.scalar.copy(a.qT[:, :, :], m.banks[:, 4:6, :].rearrange("p b (g t) -> p (b g) t", t=T)
                   ).then_inc(s.qkT, 1)
    copy_k(m, nc.scalar.copy, s, a, 3)

    def copy_q(g):
        eng.wait_ge(s.q_turned, turn * GROUPS4 + (g + 1))
        nc.scalar.copy(a.qT[:, g, :], m.banks[:, 6 + g % 2, 0:T]).then_inc(s.qmT, 1)

    for g in range(GROUPS4 - 1):
        copy_q(g)
    for p in range(UPAIRS):
        eng.wait_ge(s.scoresT, turn * UPAIRS + (p + 1))
        if p >= SLOTS3:
            eng.wait_ge(s.pv, turn * UPAIRS + (p - SLOTS3 + 1))
        nc.scalar.activation(a.pT[p % SLOTS3], a.p_pairs[(p + UPAIRS) % SLOTS3], ACT.Exp).then_inc(s.probs, 1)
        if p == 0:
            copy_q(GROUPS4 - 1)
    if a.one_sequence:
        eng.wait_ge(s.y_turned, turn + 1)
        nc.scalar.copy(a.yT[:, 0:512], m.banks[:, 4, :]).then_inc(s.yT, 1)
    else:
        for h in range(2):
            eng.wait_ge(s.y_turned, h + 1)
            nc.scalar.copy(a.yT[0:n, 512 * h:512 * (h + 1)], m.banks[0:n, 4 + h, :]).then_inc(s.yT, 1)


def attn_vector(nc, m, s, a, eng, chain, turn, x_tiles, meanwhile=None):
    n, heads, half = a.width, a.heads, DH // 2
    chain(nc.vector.memset(a.qk[:, :, 0:heads, DH:DH + 1], 0.0))
    for t in range(a.tiles):
        eng.wait_ge(s.qkv, turn * a.tiles + (t + 1 if a.one_sequence else t // 2 * 2 + 2))
        if a.one_sequence:
            qk = m.banks[:, 2 * t, 0:2 * n]
        else:
            if t % 2 == 0:
                both = slice(t, t + 2)
                nc.vector.tensor_tensor(a.qkv_sb[:, both, :], m.banks[:, t // 2, 0:6 * n].rearrange("p (t n) -> p t n", t=2),
                                        a.bias.unsqueeze(1).broadcast_to([P, 2, 3 * n]), ALU.add).then_inc(s.biased, 2)
            eng.wait_ge(s.biased, t + 1)
            qk = a.qkv_sb[:, t, 0:2 * n]
        z = qk.rearrange("p (s h d) -> p s h d", s=2, d=DH)
        out = a.qk[:, t, :, :].rearrange("p (s h) d -> p s h d", s=2)
        tmp = a.tmp[:, t, :].rearrange("p (s h d) -> p s h d", s=2, d=DH)

        def table(which, first, end):
            v = m.rope[:, t % TB, which, :, first:end]
            return v.unsqueeze(2).broadcast_to([P, 2, heads, end - first])

        chain.count(nc.vector.tensor_tensor(tmp, z, table(0, 0, DH), ALU.mult))
        chain.count(nc.vector.tensor_tensor(out[:, :, :, 0:half], z[:, :, :, half:DH], table(1, 0, half), ALU.mult))
        chain(nc.vector.tensor_tensor(out[:, :, :, half:DH], z[:, :, :, 0:half], table(1, half, DH), ALU.mult))
        nc.vector.tensor_tensor(out[:, :, :, 0:DH], out[:, :, :, 0:DH], tmp, ALU.add).then_inc(s.rope, 1)
    eng.wait_ge(s.turned, turn + 1)
    for j in range(3):
        copy_k(m, nc.vector.tensor_copy, s, a, j)
    for p in range(UPAIRS):
        eng.wait_ge(s.scores, turn * UPAIRS + (p + 1))
        g, at = p // 2, p % 2 * 2
        for t, cols in enumerate((slice(0, P), slice(P, 3 * P))):
            tile, head = a.group(g, t)
            last = nc.vector.tensor_reduce(a.qk[:, tile, head + at:head + at + 2, DH], a.p_pairs[p % SLOTS3][:, :, cols],
                                           AX.X, ALU.max, negate=True)
            if t == 0:
                chain.count(last)
        eng.wait_ge(chain.sem, chain.links)
        last.then_inc(s.neg_max, 1)
    if meanwhile:
        meanwhile()
    for h in range(2):
        eng.wait_ge(s.pv, turn * UPAIRS + (h + 1) * (UPAIRS // 2))
        nc.vector.tensor_copy(a.pv[:, 2 * h:2 * h + 2, :], m.banks[:, 6 + h, :].rearrange("p (g t) -> p g t", t=T)
                              ).then_inc(s.pv_copied, 1)
    eng.wait_ge(s.back, turn * 2 + 2)
    for b in range(2):
        back = m.banks[:, 2 + b, :].rearrange("p (u d) -> p u d", d=32)
        chain(nc.vector.reciprocal(a.rsum[:, b, :], back[:, :, DH]))
        nc.vector.tensor_tensor(a.y[:, b, :].rearrange("p (u d) -> p u d", d=DH), back[:, :, 0:DH],
                                a.rsum[:, b, :].unsqueeze(2).broadcast_to([P, UNITS, DH]), ALU.mult).then_inc(s.y, 1)
    if a.one_sequence:
        eng.wait_ge(s.proj, turn + 1)
        for t in range(TB):
            chain(nc.vector.tensor_tensor(x_tiles[t], x_tiles[t], m.banks[:, 6, t * D:(t + 1) * D], ALU.add))
    else:
        for t in range(0, a.tiles, 2):
            eng.wait_ge(s.proj, t // 2 + 1)
            own = m.x[:, t:t + 2, :]
            chain.count(nc.vector.tensor_tensor(own, own, m.banks[:, (6 + t // 2) % 8, :].rearrange("p (t d) -> p t d", d=D),
                                                ALU.add))
        eng.wait_ge(chain.sem, chain.links)


def attn_padding(engine, a, sem, eng):
    engine.memset(a.qk, 0.0).then_inc(sem, 1)
    engine.memset(a.v[:, :, :, DH:], 1.0).then_inc(sem, 1)
    engine.memset(a.kT, 0.0).then_inc(sem, 1)
    eng.wait_ge(sem, 3)
    engine.memset(a.qk[:, :, a.heads:, DH:DH + 1], 1.0).then_inc(sem, 1)
    eng.wait_ge(sem, 4)



class CombineSems:
    def __init__(self, sem, name):
        self.slots = sem(f"{name}_slots_ready")
        self.gathered = [sem(f"{name}_rows_gathered{t}") for t in range(TB)]


def combine_pool(nc, m, rows, eng, s, last_row):
    eng.wait_ge(s.slots, 1)
    eng.sem_clear(s.slots)
    for t in range(TB):
        for k in range(TOPK):
            at = t * TOPK + k
            nc.gpsimd.indirect_dma_start(
                out=rows[:, at, :], out_offset=None, in_=m.expert_out,
                in_offset=bass.IndirectOffsetOnAxis(m.gather_slots[:, at:at + 1], 0),
                bounds_check=last_row, oob_is_err=False).then_inc(s.gathered[t], 16)


def gather_vector(nc, m, eng, s, sequence):
    nc.vector.tensor_copy(m.gather_slots[:, :].rearrange("p (a b) -> p a b", b=TOPK),
                          m.slots[:, bass.ds(sequence * TB, TB), :]).then_inc(s.slots, 1)


def combine_vector(nc, m, rows, eng, chain, s, turn, sequence, x_tiles):
    chain(nc.vector.tensor_copy(m.cur_weights[:, :, :], m.weights[:, bass.ds(sequence * TB, TB), :]))
    for t in range(TB):
        eng.wait_ge(s.gathered[t], turn * (16 * TOPK) + 16 * TOPK)
    for k in range(TOPK):
        for t in range(TB):
            chain.count(nc.vector.scalar_tensor_tensor(out=x_tiles[t], in0=rows[:, t * TOPK + k, :],
                                                       scalar=m.cur_weights[:, t, k:k + 1], in1=x_tiles[t],
                                                       op0=ALU.mult, op1=ALU.add))
        eng.wait_ge(chain.sem, chain.links)



def middle_phase(nc, m, arrays, sem):
    v_chain = sem("middle_vector_chain")
    comb, norm, sr = m.combine, m.norm, m.route
    norm1 = NormSems(sem, "attention_norm")
    sa = AttnSems(sem, "attn1")
    s_pad = sem("padding_cleared")
    half = NE // 2 * D
    area = m.w_dn[:, half:]
    over = NE * KC * SHID - TB * TOPK * D
    keys = over - 512 - UNITS * T
    rows = flat(m.w_gu, over, (TB * TOPK, D))
    a = AttnPlaces(m, H, area, m.work[:, 256:], flat(m.w_gu, over - 512, (KC, T)), m.w_gu[:, keys:over - 512], m.w_qkv, m.w_proj)
    r = RoutePlaces(m)
    p_norm = m.banks[:, 7, :].rearrange("p (a b) -> p a b", b=T)
    m.s_refetched = sem("covered_weights_refetched")

    with nc.Block() as block:
        @block.sync
        def _(sp):
            sp.wait_ge(sa.qkv, TB * B)
            sp.dma_start(m.w_gu[:, over - 512:], arrays["gate_up"][:, over - 512:]).then_inc(m.s_refetched, 16)
            sp.wait_ge(sa.proj, B)
            sp.dma_start(m.w_gu[:, keys:over - 512], arrays["gate_up"][:, keys:over - 512]).then_inc(m.s_refetched, 16)
            sp.dma_start(m.w_dn[0:HID, half:], arrays["down"][:, half:]).then_inc(m.s_refetched, 16)

        @block.scalar
        def _(act):
            with act.Fori(0, B) as i:
                norm_scalar(nc, act, norm1, i, p_norm, a.xnT)
                attn_scalar(nc, m, sa, a, act, i)
                norm_scalar(nc, act, norm, i + B, m.banks[:, 7, :], m.work[:, 0:512])
                route_scalar(nc, r, act, sr, i + B)

        @block.vector
        def _(dve):
            gather_vector(nc, m, dve, comb, 0)
            attn_padding(nc.vector, a, s_pad, dve)
            nc.vector.memset(m.taken[:, :], 0.0).then_inc(s_pad, 1)
            dve.wait_ge(s_pad, 5)

            def combine_and_norm(chain, i):
                x_tiles = [m.x[:, i * TB + t, :] for t in range(TB)]
                combine_vector(nc, m, rows, dve, chain, comb, i, i, x_tiles)
                if not isinstance(i, int) or i + 1 < B:
                    gather_vector(nc, m, dve, comb, i + 1)
                norm_vector(nc, m, dve, chain, norm1, i, x_tiles, m.xn)

            def turn(i):
                chain = Chain(dve, v_chain)
                x_tiles = [m.x[:, i * TB + t, :] for t in range(TB)]
                last = isinstance(i, int) and i == B - 1
                attn_vector(nc, m, sa, a, dve, chain, i, x_tiles,
                            None if last else lambda: combine_and_norm(chain, i + 1))
                norm_vector(nc, m, dve, chain, norm, i + B, x_tiles, m.xn_sent,
                            free=(sr.scattered, scattered(i + (B - 1))))
                route_vector(nc, m, r, dve, chain, sr, i + B, i, x_tiles, 1)

            combine_and_norm(Chain(dve, v_chain), 0)
            with dve.Fori(0, B - 2) as i:
                turn(i)
            turn(B - 2)
            turn(B - 1)

        @block.tensor
        def _(pe):
            pe.wait_ge(m.s_attn_weights, 32)
            with pe.Fori(0, B) as i:
                norm_tensor(nc, m, pe, norm1, i, m.xn, p_norm)
                pe.wait_ge(sr.banks_read, i + B)
                attn_tensor(nc, m, sa, a, pe, lambda t: (norm1.xnT, i + 1), i)
                norm_tensor(nc, m, pe, norm, i + B, m.xn_sent, p_norm)
                route_tensor(nc, m, r, pe, sr, (norm.xnT, i + (B + 1)), i + B)

        @block.gpsimd
        def _(pool):
            last_slot, last_row = pool.to_reg(SLOTS - 1), pool.to_reg(SLOTS + P - 1)

            def turn(i, gather, norm_next):
                if norm_next:
                    norm_pool(nc, m, pool, norm1, i + 1)
                norm_pool(nc, m, pool, norm, i + B)
                if gather:
                    combine_pool(nc, m, rows, pool, comb, last_row)
                route_pool(nc, m, pool, sr, m.xn_sent, 1, last_slot)

            combine_pool(nc, m, rows, pool, comb, last_row)
            norm_pool(nc, m, pool, norm1, 0)
            combine_pool(nc, m, rows, pool, comb, last_row)
            with pool.Fori(0, B - 2) as i:
                turn(i, True, True)
            turn(B - 2, False, True)
            turn(B - 1, False, False)
            pool.wait_ge(sr.scattered, scattered(2 * B - 1))



ROW_NAMES = ["amp_b", "ph_b", "ent_pb0", "ent_pb1", "path_b00", "path_b01", "path_b10", "path_b11",
             "phase00", "phase01", "phase10", "phase11", "bo", "bq", "ln4_g1", "ln4_b1"]
STEPS = 2 * NL
TURN_PI = float(np.nextafter(np.float32(np.pi), np.float32(0)))


def last_weights(m):
    w, g = Places(), m.w_gu
    w.ent_wT = flat(g, 0, (NL, EW // P, D))
    w.ent_pw = flat(g, 4096, (NL, EW // P, D))
    w.path = flat(g, 8192, (NL * PW, KC, D))
    w.amp_ph = flat(g, 10240, (KC, 2 * D))
    w.rows = flat(g, 11264, (len(ROW_NAMES), D))
    w.kv_b = flat(g, 15360, (2 * HKV * DH,))
    w.ent_b = flat(g, 15488, (NL, EW // P))
    w.gain_cols = flat(g, 15504, (STEPS, KC))
    w.shift_cols = flat(g, 15512, (STEPS, KC))
    w.lin = flat(g, 15520, (STEPS, KC, D))
    w.bias = flat(g, 17568, (2 + STEPS, D))
    w.qkv2_b = flat(g, 19104, (3 * HKV * DH,))
    w.scaled = flat(g, 19296, (KC, D))
    w.half_pi = flat(g, 19808, (1,))
    w.minus_quarter = flat(g, 19809, (1,))
    w.means = flat(g, 19812, (STEPS * KC,))
    w.bias_means = flat(g, 19820, (STEPS,))
    w.wq = flat(g, 20624, (KC, D))
    w.qkv2 = flat(g, 21136, (KC, 3 * HKV * DH))
    w.wo = flat(g, 21520, (1, D))
    w.bias_b = g[:, 21776:22544].bitcast(BF16).rearrange("p (a b) -> p a b", b=D)
    d = m.w_dn
    w.ent_b_wide = flat(d, 0, (NL, EW // P, P))
    w.phase_turns = flat(d, 5376, (NL * PW, D))
    w.phase_sin = flat(d, 2048, (NL * PW, D))
    w.phase_cos = flat(d, 3072, (NL * PW, D))
    w.mod = flat(d, 4096, (NL * PW, D))
    w.shift_wide = flat(d, 5120, (KC, P))
    w.rest = flat(g, 22544, (2 + STEPS, D))
    w.parts = [g[:, first:first + 768].bitcast(BF16).rearrange("p (a b) -> p a b", b=D)
               for first in (8192, 8960, 3072)]
    w.combined = [flat(d, 10240 + 3072 * b, (TB * TOPK, D)) for b in range(2)]
    return w


def row(w, name):
    return w.rows[:, ROW_NAMES.index(name), :]


def load_last_weights(m, a, eng, part, groups_used):
    w = last_weights(m)
    free = groups_used * GROUP * KC * SHID
    if part == 1:
        assert free >= 8192
        for l in range(NL):
            eng.dma_start(w.ent_wT[:, l], a["ent_wT"][l].rearrange("(c p) d -> p c d", p=P)).then_inc(m.s_ent, 16)
            eng.dma_start(w.ent_pw[:, l], a["ent_pw"][l].rearrange("(c p) d -> p c d", p=P)).then_inc(m.s_ent, 16)
    elif part == 2:
        assert free >= 11264
        for q in range(NL * PW):
            eng.dma_start(w.path[:, q], a["path_w"][q].rearrange("(c p) d -> p c d", p=P)).then_inc(m.s_path, 16)
        eng.dma_start(w.amp_ph[:, :, 0:D], a["amp_w"].rearrange("(c p) n -> p c n", p=P)).then_inc(m.s_path, 16)
        eng.dma_start(w.amp_ph[:, :, D:2 * D], a["ph_w"].rearrange("(c p) n -> p c n", p=P)).then_inc(m.s_path, 16)
    else:
        assert free >= 15520
        n = len(ROW_NAMES) * D
        eng.dma_start(w.rows.rearrange("p a b -> p (a b)"), a["rows"].broadcast_to([P, n])).then_inc(m.s_rows, 16)
        eng.dma_start(w.kv_b, a["kv_b"].broadcast_to([P, 2 * HKV * DH])).then_inc(m.s_rows, 16)
        for own, name in ((w.ent_b, "ent_b"), (w.gain_cols, "gain_cols"), (w.shift_cols, "shift_cols")):
            eng.dma_start(own.rearrange("p a b -> p (a b)"), a[name]).then_inc(m.s_rows, 16)


def split_bias(nc, m, w, chain, rows):
    bias, rest, (one, two, three) = w.bias[:, rows], w.rest[:, rows], [part[:, rows] for part in w.parts]
    chain(nc.vector.tensor_copy(one, bias))
    chain(nc.vector.tensor_tensor(rest, bias, one, ALU.subtract))
    chain(nc.vector.tensor_copy(two, rest))
    chain(nc.vector.tensor_tensor(three, rest, two, ALU.subtract))
    chain(nc.vector.tensor_scalar(w.bias_b[:, rows], one, m.ident[:, 0:1], None, ALU.mult))
    for place, part in ((1, two), (2, three)):
        chain(nc.vector.scalar_tensor_tensor(out=w.bias_b[:, rows], in0=part, scalar=m.ident[:, place:place + 1],
                                             in1=w.bias_b[:, rows], op0=ALU.mult, op1=ALU.add))


def finish_maps(nc, m, w, eng, chain, s_ready):
    maps = w.lin.rearrange("p s c d -> p (s c) d")
    chain.count(nc.vector.tensor_reduce(w.bias_means, w.bias[:, 2:, :], AX.X, ALU.add))
    chain(nc.vector.tensor_reduce(w.means, maps, AX.X, ALU.add))
    chain.count(nc.vector.tensor_scalar(w.bias_means, w.bias_means, 1.0 / D, None, ALU.mult))
    chain(nc.vector.tensor_scalar(w.means, w.means, 1.0 / D, None, ALU.mult))
    for k in range(STEPS):
        for c in range(KC):
            gain = w.gain_cols[:, k - 1, c:c + 1] if k else float(np.sqrt(0.5))
            chain.count(nc.vector.tensor_scalar(w.lin[:, k, c, :], w.lin[:, k, c, :],
                                                w.means[:, k * KC + c:k * KC + c + 1], gain,
                                                ALU.subtract, ALU.mult))
        chain.count(nc.vector.tensor_scalar(w.bias[:, 2 + k, :], w.bias[:, 2 + k, :], w.bias_means[:, k:k + 1],
                                            None, ALU.subtract))
    eng.wait_ge(chain.sem, chain.links)
    split_bias(nc, m, w, chain, slice(2, 2 + STEPS))
    eng.sem_inc(s_ready, 1)
    for c in range(KC):
        chain.count(nc.vector.tensor_reduce(w.qkv2[:, c, 0:64].rearrange("p (h d) -> p h d", d=DH),
                                            w.wq[:, c, :].rearrange("p (h g d) -> p h d g", g=4, d=DH),
                                            AX.X, ALU.add))
    chain.count(nc.vector.tensor_reduce(w.qkv2_b[:, 0:64].rearrange("p (h d) -> p h d", d=DH),
                                        row(w, "bq").rearrange("p (h g d) -> p h d g", g=4, d=DH), AX.X, ALU.add))
    chain(nc.vector.tensor_copy(w.qkv2_b[:, 64:192], w.kv_b))


def fold_phase(nc, m, a, sem):
    w = last_weights(m)
    w.s_small = s_small = sem("small_last_weights_loaded")
    s_wide, s_prod = sem("bias_columns_spread"), sem("fold_product_ready")
    s_sin, s_half = sem("phase_sines_ready"), sem("phase_reduced")
    s_combined = sem("sequence_combined")
    v_chain = sem("fold_vector_chain")
    s_gathered = [sem(f"last_rows_gathered{b}") for b in range(2)]

    with nc.Block() as block:
        @block.sync
        def _(sp):
            sp.dma_start(w.wq, a["Wq"].rearrange("(c p) n -> p c n", p=P)).then_inc(s_small, 16)
            sp.dma_start(w.qkv2[:, :, 64:128], a["Wk"].rearrange("(c p) n -> p c n", p=P)).then_inc(s_small, 16)
            sp.dma_start(w.qkv2[:, :, 128:192], a["Wv"].rearrange("(c p) n -> p c n", p=P)).then_inc(s_small, 16)
            sp.dma_start(w.wo[0:64, 0, :], a["Wo"]).then_inc(s_small, 16)

        @block.gpsimd
        def _(pool):
            last_row = pool.to_reg(SLOTS + P - 1)
            for q in range(B):
                if q >= 2:
                    pool.wait_ge(s_combined, q - 1)
                for t in range(TB):
                    for k in range(TOPK):
                        nc.gpsimd.indirect_dma_start(
                            out=w.combined[q % 2][:, t * TOPK + k, :], out_offset=None, in_=m.expert_out,
                            in_offset=bass.IndirectOffsetOnAxis(m.slots[:, q * TB + t, k:k + 1], 0),
                            bounds_check=last_row, oob_is_err=False).then_inc(s_gathered[q % 2], 16)

        @block.scalar
        def _(act):
            act.wait_ge(s_half, 1)
            nc.scalar.activation(w.phase_sin, w.phase_turns, ACT.Sin).then_inc(s_sin, 1)
            act.wait_ge(s_half, 2)
            nc.scalar.activation(w.phase_cos, w.phase_cos, ACT.Sin, scale=-1.0, bias=w.half_pi).then_inc(s_sin, 1)

        @block.vector
        def _(dve):
            chain = Chain(dve, v_chain)

            def combine(q):
                x_tiles = [m.x[:, q * TB + t, :] for t in range(TB)]
                dve.wait_ge(s_gathered[q % 2], (q // 2 + 1) * 16 * TB * TOPK)
                for k in range(TOPK):
                    for t in range(TB):
                        chain.count(nc.vector.scalar_tensor_tensor(
                            out=x_tiles[t], in0=w.combined[q % 2][:, t * TOPK + k, :],
                            scalar=m.weights[:, q * TB + t, k:k + 1], in1=x_tiles[t], op0=ALU.mult, op1=ALU.add))
                    dve.wait_ge(v_chain, chain.links)
                dve.sem_inc(s_combined, 1)

            nc.vector.memset(w.minus_quarter, -0.25)
            chain(nc.vector.memset(w.half_pi, PI / 2))
            dve.wait_ge(m.s_rows, 5 * 16)
            for l in range(NL):
                nc.vector.tensor_copy(w.ent_b_wide[:, l], w.ent_b[:, l, :].unsqueeze(2).broadcast_to([P, EW // P, P])
                                      ).then_inc(s_wide, 1)
            phase = w.rows[:, ROW_NAMES.index("phase00"):ROW_NAMES.index("phase00") + NL * PW, :]
            big = 12582912.0
            chain(nc.vector.tensor_scalar(w.phase_turns, phase, 0.5 / PI, big, ALU.mult, ALU.add))
            chain(nc.vector.tensor_scalar(w.phase_sin, w.phase_turns, -big, None, ALU.add))
            c1 = 6.28125
            c2 = float(np.float32(2 * np.pi - c1))
            chain(nc.vector.scalar_tensor_tensor(out=w.phase_turns, in0=w.phase_sin, scalar=-c1, in1=phase,
                                                 op0=ALU.mult, op1=ALU.add))
            chain(nc.vector.scalar_tensor_tensor(out=w.phase_turns, in0=w.phase_sin, scalar=-c2, in1=w.phase_turns,
                                                 op0=ALU.mult, op1=ALU.add))
            nc.vector.tensor_scalar(w.phase_turns, w.phase_turns, TURN_PI, -TURN_PI, ALU.min, ALU.max).then_inc(s_half, 1)
            dve.wait_ge(s_half, 1)
            nc.vector.scalar_tensor_tensor(out=w.phase_cos, in0=w.phase_turns, scalar=-1.0, in1=w.phase_turns,
                                           op0=ALU.mult, op1=ALU.max).then_inc(s_half, 1)
            combine(0)
            dve.wait_ge(s_sin, 2)
            chain(nc.vector.tensor_tensor(w.mod, w.phase_sin, w.phase_cos, ALU.add))
            dve.wait_ge(m.s_path, 16 * (NL * PW + 2))
            for l in range(NL):
                step = 2 * l + 1
                for q in range(PW):
                    mod = w.mod[:, l * PW + q, :].unsqueeze(1).broadcast_to([P, KC, D])
                    target = w.lin[:, step] if q == 0 else w.scaled
                    chain(nc.vector.tensor_tensor(target, w.path[:, l * PW + q], mod, ALU.mult))
                chain(nc.vector.tensor_tensor(w.lin[:, step], w.lin[:, step], w.scaled, ALU.add))
                for c in range(KC):
                    part = w.lin[:, step, c, c * P:(c + 1) * P]
                    chain(nc.vector.tensor_tensor(part, part, m.ident[:, :], ALU.add))
                own = w.bias[:, 2 + step, :]
                chain(nc.vector.tensor_tensor(own, row(w, f"path_b{l}0"), w.mod[:, l * PW, :], ALU.mult))
                chain(nc.vector.tensor_tensor(w.scaled[:, 0, :], row(w, f"path_b{l}1"), w.mod[:, l * PW + 1, :],
                                              ALU.mult))
                chain(nc.vector.tensor_tensor(own, own, w.scaled[:, 0, :], ALU.add))
                step = 2 * l
                for c in range(KC):
                    dve.wait_ge(s_prod, 3 * l + c + 1)
                    chain(nc.vector.tensor_copy(w.lin[:, step, c, :], m.banks[:, 3 * l + c, 0:D]))
                    part = w.lin[:, step, c, c * P:(c + 1) * P]
                    chain(nc.vector.tensor_tensor(part, part, m.ident[:, :], ALU.add))
                dve.wait_ge(s_prod, 3 * l + 3)
                chain(nc.vector.tensor_tensor(w.bias[:, 2 + step, :], m.banks[:, 3 * l + 2, 0:D], row(w, f"ent_pb{l}"),
                                              ALU.add))
                if l == 0:
                    combine(1)
            chain(nc.vector.tensor_scalar(w.amp_ph[:, :, 0:D], w.amp_ph[:, :, 0:D], 0.5, None, ALU.mult))
            chain(nc.vector.tensor_scalar(w.bias[:, 0, :], row(w, "amp_b"), 0.5, None, ALU.mult))
            chain(nc.vector.tensor_copy(w.bias[:, 1, :], row(w, "ph_b")))
            for k in range(1, STEPS):
                nc.vector.tensor_copy(w.shift_wide, w.shift_cols[:, k - 1, :].unsqueeze(2).broadcast_to([P, KC, P])
                                      ).then_inc(s_wide, 1)
                dve.wait_ge(s_prod, 3 * NL + k)
                chain(nc.vector.tensor_tensor(w.bias[:, 2 + k, :], w.bias[:, 2 + k, :], m.banks[:, 6, 0:D], ALU.add))
            split_bias(nc, m, w, chain, slice(0, 2))
            chain(nc.vector.tensor_scalar(w.rows[:, -2:, :], w.rows[:, -2:, :], 0.5, None, ALU.mult))
            combine(2)
            combine(3)

        @block.tensor
        def _(pe):
            pe.wait_ge(m.s_ent, 16 * 2 * NL)
            for l in range(NL):
                for c in range(KC):
                    for e in range(EW // P):
                        last = nc.tensor.matmul(m.banks[:, 3 * l + c, 0:D], w.ent_wT[:, l, e, c * P:(c + 1) * P],
                                                w.ent_pw[:, l, e, :], start=(e == 0), stop=(e == EW // P - 1))
                    last.then_inc(s_prod, 1)
                pe.wait_ge(s_wide, l + 1)
                for e in range(EW // P):
                    last = nc.tensor.matmul(m.banks[:, 3 * l + 2, 0:D], w.ent_b_wide[:, l, e, :], w.ent_pw[:, l, e, :],
                                            start=(e == 0), stop=(e == EW // P - 1))
                last.then_inc(s_prod, 1)
            for k in range(1, STEPS):
                pe.wait_ge(s_wide, NL + k)
                for c in range(KC):
                    last = nc.tensor.matmul(m.banks[:, 6, 0:D], w.shift_wide[:, c, :], w.lin[:, k, c, :],
                                            start=(c == 0), stop=(c == KC - 1))
                last.then_inc(s_prod, 1)
    return w


ITEMS = STEPS * TILES
DEEP = 4
LAG = 2


class WaveSems:

    def __init__(self, sem, name):
        self.stats = sem(f"{name}_x_variance_ready")
        self.x_rstd = sem(f"{name}_x_rstd_ready")
        self.xn = sem(f"{name}_x_normed")
        self.x_turned = sem(f"{name}_x_turned")
        self.xT = sem(f"{name}_x_T_ready")
        self.z = sem(f"{name}_z_ready")
        self.tanh = sem(f"{name}_tanh_ready")
        self.abs = sem(f"{name}_sine_argument_ready")
        self.sines = sem(f"{name}_sines_ready")
        self.u = sem(f"{name}_input_or_normed_ready")
        self.turned = sem(f"{name}_turned")
        self.uT = sem(f"{name}_turned_copied")
        self.lin = sem(f"{name}_linear_ready")
        self.square = sem(f"{name}_mean_square_ready")
        self.eps = sem(f"{name}_eps_added")
        self.rstd = sem(f"{name}_rstd_ready")
        self.shifted = sem(f"{name}_shift_added_to_x")


class WavePlaces:
    def __init__(self, m):
        area = m.w_dn
        self.u = flat(area, 0, (TILES, D))
        self.z = flat(area, 2048, (TILES, 2 * D))
        self.squares = [flat(area, 6144 + 256 * b, (D,)) for b in range(DEEP)]
        self.uT = [flat(area, 7168 + 256 * b, (KC, P)) for b in range(DEEP)]
        self.xn = flat(area, 8192, (TILES, D))
        self.p_turn = [m.banks[:, b, 0:KC * P].rearrange("p (c t) -> p c t", t=P) for b in range(DEEP)]
        self.p_lin = [m.banks[:, 4 + b, 0:D] for b in range(DEEP)]
        self.p_z = [m.banks[:, 4 + b, :] for b in range(DEEP)]


def turn_x(nc, m, f, s, eng, norms, t, banks):
    eng.wait_ge(s.xn, norms * TILES + (t + 1))
    for c in range(KC):
        last = nc.tensor.transpose(banks[t % DEEP][:, c, :], f.xn[:, t, c * P:(c + 1) * P], m.ident[:, :])
    last.then_inc(s.x_turned, 1)


def wave_tensor(nc, m, w, f, s, eng, ffn, s_maps):
    first_u = ffn * (TILES + ITEMS)
    norms = 2 * ffn

    def product_x(t):
        eng.wait_ge(s.xT, norms * TILES + (t + 1))
        if t >= DEEP:
            eng.wait_ge(s.tanh, ffn * TILES + (t - DEEP + 1))
        nc.tensor.matmul(f.p_z[t % DEEP], m.ones_b[:, :], w.bias_b[:, 0:2, :].rearrange("p a b -> p (a b)"),
                         start=True, stop=False)
        for c in range(KC):
            last = nc.tensor.matmul(f.p_z[t % DEEP], f.uT[t % DEEP][:, c, :], w.amp_ph[:, c, :],
                                    start=False, stop=(c == KC - 1))
        last.then_inc(s.z, 1)

    for p in range(TILES + LAG):
        if p < TILES:
            turn_x(nc, m, f, s, eng, norms, p, f.p_turn)
        if p >= LAG:
            product_x(p - LAG)

    def turn_u(n, t):
        eng.wait_ge(s.u, n + (first_u + 1))
        for c in range(KC):
            last = nc.tensor.transpose(f.p_turn[t % DEEP][:, c, :], f.u[:, t, c * P:(c + 1) * P], m.ident[:, :])
        last.then_inc(s.turned, 1)

    def product_u(n, t, step):
        eng.wait_ge(s.uT, n + (ffn * ITEMS + 1))
        eng.wait_ge(s.u, n + (first_u + TILES - DEEP + 1))
        nc.tensor.matmul(f.p_lin[t % DEEP], m.ones_b[:, :], w.bias_b[:, step + 2, :], start=True, stop=False)
        for c in range(KC):
            last = nc.tensor.matmul(f.p_lin[t % DEEP], f.uT[t % DEEP][:, c, :], w.lin[:, step, c, :],
                                    start=False, stop=(c == KC - 1))
        last.then_inc(s.lin, 1)

    eng.wait_ge(s_maps, 1)
    in_steps(eng, [(0, turn_u), (LAG, with_turn(product_u))], ITEMS, TILES)


def wave_scalar(nc, m, w, f, s, eng, ffn):
    def copy_x(t):
        eng.wait_ge(s.x_turned, 2 * ffn * TILES + (t + 1))
        nc.scalar.copy(f.uT[t % DEEP], f.p_turn[t % DEEP]).then_inc(s.xT, 1)

    def tanh(t):
        eng.wait_ge(s.z, ffn * TILES + (t + 1))
        nc.scalar.activation(f.z[:, t, :], f.p_z[t % DEEP], ACT.Tanh).then_inc(s.tanh, 1)

    def argument(t):
        eng.wait_ge(s.tanh, ffn * TILES + (t + 1))
        nc.scalar.activation(f.z[:, t, D:2 * D], f.z[:, t, D:2 * D], ACT.Abs, bias=w.minus_quarter).then_inc(s.abs, 1)

    for p in range(TILES + LAG + 1):
        if p < TILES:
            copy_x(p)
        if LAG <= p < TILES + LAG:
            tanh(p - LAG)
        if p > LAG:
            argument(p - LAG - 1)
    for t in range(TILES):
        eng.wait_ge(s.abs, ffn * TILES + (t + 1))
        nc.scalar.activation(f.z[:, t, D:2 * D], f.z[:, t, D:2 * D], ACT.Sin, scale=-PI, bias=w.half_pi
                             ).then_inc(s.sines, 1)

    def copy_u(n, t):
        eng.wait_ge(s.turned, n + (ffn * ITEMS + 1))
        nc.scalar.copy(f.uT[t % DEEP], f.p_turn[t % DEEP]).then_inc(s.uT, 1)

    def square(n, t):
        eng.wait_ge(s.lin, n + (ffn * ITEMS + 1))
        nc.scalar.activation(f.squares[t % DEEP], f.p_lin[t % DEEP], ACT.Square, scale=D ** -0.5,
                             accum_out=m.mv[:, t, 1:2]).then_inc(s.square, 1)

    in_steps(eng, [(0, copy_u), (LAG, square)], ITEMS, TILES)


def norm_all_vector(nc, m, f, s, eng, chain, norms):
    for first in range(0, TILES, 4):
        group = range(first, first + 4)
        for t in group:
            chain.count(nc.vector.bn_stats(m.stats[:, t, :], m.x[:, t, :]))
        eng.wait_ge(chain.sem, chain.links)
        for t in group:
            nc.vector.bn_aggr(m.mv[:, t, :], m.stats[:, t, :]).then_inc(s.stats, 1)
    for t in range(TILES):
        eng.wait_ge(s.stats, norms * TILES + TILES)
        eng.wait_ge(s.x_rstd, norms * 2 + t // 4 + 1)
        nc.vector.tensor_scalar(f.xn[:, t, :], m.x[:, t, :], m.mv[:, t, 0:1], m.rstd[:, t:t + 1],
                                ALU.subtract, ALU.mult).then_inc(s.xn, 1)


def wave_vector(nc, m, w, f, s, eng, v_chain, ffn, s_out=None, meanwhile=None):
    chain = Chain(eng, v_chain)
    norm_all_vector(nc, m, f, s, eng, chain, 2 * ffn)
    if meanwhile:
        meanwhile(chain)
    for t in range(TILES):
        eng.wait_ge(s.sines, ffn * TILES + (t + 1))
        nc.vector.scalar_tensor_tensor(out=f.u[:, t, :], in0=f.z[:, t, 0:D], scalar=1.0, in1=f.z[:, t, D:2 * D],
                                       op0=ALU.add, op1=ALU.mult).then_inc(s.u, 1)

    def normalise(n, t):
        eng.wait_ge(s.rstd, n + (ffn * ITEMS + 1))
        nc.vector.tensor_scalar(f.u[:, t, :], f.p_lin[t % DEEP], m.rstd[:, t:t + 1], None, ALU.mult).then_inc(s.u, 1)

    in_steps(eng, [(0, normalise)], ITEMS, TILES)
    eng.wait_ge(s.shifted, 2 * ffn + 1)
    for h in range(2):
        group = slice(4 * h, 4 * h + 4)
        eng.wait_ge(s.u, (ffn + 1) * (TILES + ITEMS) - 4 * (1 - h))
        gain = row(w, "ln4_g1").unsqueeze(1).broadcast_to([P, 4, D])
        chain(nc.vector.tensor_tensor(f.u[:, group, :], f.u[:, group, :], gain, ALU.mult))
        chain(nc.vector.tensor_tensor(m.x[:, group, :], m.x[:, group, :], f.u[:, group, :], ALU.add))
        if s_out is not None:
            eng.sem_inc(s_out, 1)


def root(nc, m, s, eng, eps_done, src, group, ready, done):
    eng.wait_ge(*ready)
    nc.gpsimd.tensor_tensor(m.var_eps[:, group], src, m.eps[:, group], ALU.add).then_inc(s.eps, 1)
    eng.wait_ge(s.eps, eps_done)
    nc.gpsimd.tensor_tensor(m.rstd[:, group], m.var_eps[:, group], m.minus_half[:, group], ALU.pow).then_inc(done, 1)


def norm_all_pool(nc, m, s, eng, norms, vector):
    before = 2 * norms + (norms > 0) * ITEMS
    for h in range(2):
        group = slice(4 * h, 4 * h + 4)
        root(nc, m, s, eng, before + h + 1, m.mv[:, group, 1], group, (s.stats, norms * TILES + 4 * h + 4), s.x_rstd)
    eng.wait_ge(s.xn, (norms + 1) * TILES)
    nc.gpsimd.tensor_tensor(m.x[:, :, :], m.x[:, :, :], vector.unsqueeze(1).broadcast_to([P, TILES, D]), ALU.add
                            ).then_inc(s.shifted, 1)


def wave_pool(nc, m, w, s, eng, ffn, meanwhile=None):
    norm_all_pool(nc, m, s, eng, 2 * ffn, row(w, "ln4_b1"))
    if meanwhile:
        meanwhile()
    before = 2 * (2 * ffn + 1) + ffn * ITEMS

    def rstd(n, t):
        root(nc, m, s, eng, n + (before + 1), m.mv[:, t, 1:2], slice(t, t + 1),
             (s.square, n + (ffn * ITEMS + 1)), s.rstd)

    in_steps(eng, [(0, rstd)], ITEMS, TILES)


def last_phase(nc, m, w, a, sem):
    v_chain = sem("last_vector_chain")
    wave, sa = WaveSems(sem, "wave"), AttnSems(sem, "attn2")
    s_maps = sem("step_maps_ready")
    s_pad, s_out, s_stored = sem("padding2_cleared"), sem("out_ready"), sem("out_stored")
    f = WavePlaces(m)
    area = m.w_gu[:, 0:8192]
    at = AttnPlaces(m, HKV, area, m.w_dn[:, 0:6144], flat(m.w_dn, 10240, (KC, TILES * P)), m.w_dn[:, 12288:16384],
                    w.qkv2, w.wo, w.qkv2_b)
    p_turn = [m.banks[:, 4 + b, 0:KC * P].rearrange("p (c t) -> p c t", t=P) for b in range(DEEP)]

    with nc.Block() as block:
        @block.scalar
        def _(act):
            wave_scalar(nc, m, w, f, wave, act, 0)
            for t in range(TILES):
                act.wait_ge(wave.x_turned, TILES + t + 1)
                nc.scalar.copy(at.xnT[:, :, t * P:(t + 1) * P], p_turn[t % DEEP]).then_inc(wave.xT, 1)
            attn_scalar(nc, m, sa, at, act, 0)
            wave_scalar(nc, m, w, f, wave, act, 1)

        @block.vector
        def _(dve):
            dve.wait_ge(w.s_small, 4 * 16)
            wave_vector(nc, m, w, f, wave, dve, v_chain, 0,
                        meanwhile=lambda chain: finish_maps(nc, m, w, dve, chain, s_maps))
            dve.wait_ge(s_pad, 4)
            chain = Chain(dve, v_chain)
            norm_all_vector(nc, m, f, wave, dve, chain, 1)
            dve.wait_ge(wave.shifted, 2)
            attn_vector(nc, m, sa, at, dve, chain, 0, None)
            wave_vector(nc, m, w, f, wave, dve, v_chain, 1, s_out)

        @block.tensor
        def _(pe):
            wave_tensor(nc, m, w, f, wave, pe, 0, s_maps)
            for t in range(TILES):
                if t >= DEEP:
                    pe.wait_ge(wave.xT, TILES + t - DEEP + 1)
                turn_x(nc, m, f, wave, pe, 1, t, p_turn)
            attn_tensor(nc, m, sa, at, pe, lambda t: (wave.xT, TILES + t + 1), 0)
            wave_tensor(nc, m, w, f, wave, pe, 1, s_maps)

        @block.gpsimd
        def _(pool):
            wave_pool(nc, m, w, wave, pool, 0, meanwhile=lambda: attn_padding(nc.gpsimd, at, s_pad, pool))
            norm_all_pool(nc, m, wave, pool, 1, row(w, "bo"))
            wave_pool(nc, m, w, wave, pool, 1)

        @block.sync
        def _(sp):
            out = a["out"].rearrange("(t p) c -> p t c", p=P)
            for h in range(2):
                sp.wait_ge(s_out, h + 1)
                sp.dma_start(out[:, 4 * h:4 * h + 4, :], m.x[:, 4 * h:4 * h + 4, :]).then_inc(s_stored, 16)
            sp.wait_ge(s_stored, 32)


def build(nc, a):
    with ExitStack() as ctx:
        m = allocate(nc, ctx)

        def sem(name):
            return ctx.enter_context(nc.semaphore(name))

        m.norm, m.route, m.combine = NormSems(sem, "norm"), RouteSems(sem, "route"), CombineSems(sem, "combine")
        m.experts = ExpertSems(sem)
        m.s_ent, m.s_path, m.s_rows = (sem(f"{name}_weights_loaded") for name in ("entangling", "path", "vector"))
        first_phase(nc, m, a, sem)
        experts_phase(nc, m, a, 0)
        middle_phase(nc, m, a, sem)
        experts_phase(nc, m, a, 1)
        w = fold_phase(nc, m, a, sem)
        last_phase(nc, m, w, a, sem)



def shape_constants():
    i = np.arange(P)
    consts = np.concatenate([np.eye(P), i[:, None] < i[None, :], i[None, :] > i[:, None],
                             np.tile(np.arange(NE), (P, 1))], axis=1).astype(np.float32)
    inv_freq = (1.0 / np.float32(10000.0) ** (np.arange(0, DH, 2, dtype=np.float32) / np.float32(DH))).astype(np.float32)
    angle = np.arange(T, dtype=np.float32)[:, None] * inv_freq[None, :]
    cos, sin = np.cos(angle), np.sin(angle)
    tables = np.stack([np.concatenate([cos, cos], 1), np.concatenate([-sin, sin], 1)], 1)
    tables = np.stack([tables * DH ** -0.5, tables], 2)
    rope = tables.reshape(TB, P, 2, 2, DH).transpose(1, 0, 2, 3, 4).reshape(P, -1)
    return consts, rope.astype(np.float32)


def kernel(**inputs):
    import concourse.bacc as _bacc
    from concourse.bass_utils import run_bass_kernel_spmd as _run

    v = {k: np.asarray(x) for k, x in inputs.items()}
    consts, rope = shape_constants()
    ffn, at = "L1_ffn_", "L1_attn_"
    turn = np.concatenate([np.arange(0, DH, 2), np.arange(1, DH, 2)])
    heads_first = lambda x: x.reshape(*x.shape[:-1], -1, DH)[..., turn].reshape(x.shape)
    vectors = [v[ffn + "amp_b"], v[ffn + "ph_b"], *v[ffn + "ent_pb"], *v[ffn + "path_b"].reshape(NL * PW, D),
               *v[ffn + "phase"].reshape(NL * PW, D), v[at + "bo"], heads_first(v[at + "bq"]),
               v[ffn + "ln4_g"][-1], v[ffn + "ln4_b"][-1]]

    def columns(*names):
        return np.stack([v[ffn + n] for n in names], 1).reshape(NL, 2, KC, P).transpose(3, 0, 1, 2).reshape(P, -1)

    arrays = {
        "x": v["L0_attn_x"].reshape(TOK, D),
        "consts": consts,
        "rope": rope,
        "router": v["L0_ffn_gate_w"].T,
        "shared_gate": v["L0_ffn_shared_gate_w"].T,
        "shared_up": v["L0_ffn_shared_up_w"].T,
        "shared_down": v["L0_ffn_shared_down_w"].T,
        "gate_up": v["L0_ffn_gate_up_proj"].reshape(NE, KC, P, SHID).transpose(2, 0, 1, 3).reshape(P, -1),
        "down": v["L0_ffn_down_proj"].transpose(1, 0, 2).reshape(HID, -1),
        "qkv": v["L0_attn_w_qkv"].T,
        "proj": v["L0_attn_w_proj"].T,
        "ent_wT": v[ffn + "ent_w"].transpose(0, 2, 1),
        "ent_pw": v[ffn + "ent_pw"],
        "ent_b": v[ffn + "ent_b"].reshape(NL, EW // P, P).transpose(2, 0, 1).reshape(P, -1),
        "path_w": v[ffn + "path_w"].reshape(NL * PW, D, D),
        "amp_w": v[ffn + "amp_w"],
        "ph_w": v[ffn + "ph_w"],
        "rows": np.concatenate(vectors).reshape(1, -1),
        "gain_cols": columns("ln3_g", "ln4_g"),
        "shift_cols": columns("ln3_b", "ln4_b"),
        "kv_b": np.concatenate([heads_first(v[at + "bk"]), v[at + "bv"]]).reshape(1, -1),
        "Wq": heads_first(v[at + "Wq"]),
        "Wk": heads_first(v[at + "Wk"]),
        "Wv": v[at + "Wv"],
        "Wo": v[at + "Wo"],
    }
    nc = _bacc.Bacc("TRN2", target_bir_lowering=False, num_devices=1)
    sent, a = {}, {}
    for name, x in arrays.items():
        sent[f"in_{name}"] = np.ascontiguousarray(x)
        a[name] = nc.dram_tensor(f"in_{name}", sent[f"in_{name}"].shape, mybir.dt.from_np(x.dtype),
                                 kind="ExternalInput").ap()
    a["out"] = nc.dram_tensor("out_0", (TOK, D), F32, kind="ExternalOutput").ap()
    build(nc, a)
    r = _run(nc, [sent], core_ids=[0])
    return r.results[0]["out_0"].reshape(B, T, D)
```

```python
from contextlib import ExitStack

import numpy as np
import concourse.bass as bass
from concourse import mybir

F32 = mybir.dt.float32
BF16 = mybir.dt.bfloat16
U32 = mybir.dt.uint32
ALU = mybir.AluOpType
ACT = mybir.ActivationFunctionType
AX = mybir.AxisListType

P = 128
D = 256
KC = D // P
B, T = 4, 256
TOK = B * T
TILES = TOK // P
TB = T // P
NE, TOPK, CAP, HID, SHID = 64, 6, 64, 96, 192
PAIRS = NE // 2
SLOTS = NE * CAP
H, DH = 16, 16
HKV = 4
EPS = 1e-5
NL = 2
PW = 2
EW = 4 * D
MASKED = -1.0e30
PI = float(np.pi)


def flat(buf, first, shape):
    n = int(np.prod(shape))
    v = buf[:, first:first + n]
    if len(shape) == 2:
        return v.rearrange("p (a b) -> p a b", b=shape[1])
    if len(shape) == 3:
        return v.rearrange("p (a b c) -> p a b c", b=shape[1], c=shape[2])
    if len(shape) == 4:
        return v.rearrange("p (a b c d) -> p a b c d", b=shape[1], c=shape[2], d=shape[3])
    return v


class Chain:

    def __init__(self, engine, sem):
        self.engine, self.sem, self.links = engine, sem, 0
        engine.sem_clear(sem)

    def __call__(self, instruction):
        instruction.then_inc(self.sem, 1)
        self.links += 1
        self.engine.wait_ge(self.sem, self.links)

    def count(self, instruction):
        instruction.then_inc(self.sem, 1)
        self.links += 1


class Places:
    pass


def allocate(nc, ctx):
    m = Places()

    def sb(name, shape, dt=F32):
        return ctx.enter_context(nc.sbuf_tensor(name, shape, dt))

    m.w_gu = sb("w_gu", [P, NE * KC * SHID])
    m.w_dn = sb("w_dn", [P, NE * D])
    m.x = sb("x", [P, TILES, D])
    m.ident = sb("ident", [P, P])
    m.ident_b = sb("ident_b", [P, 3 * P], BF16)
    m.before_b = sb("before_b", [P, P], BF16)
    m.ones_b = sb("ones_b", [P, P], BF16)
    m.causal_b = sb("causal_b", [P, 3 * P], BF16)
    m.expert_no = sb("expert_no", [P, NE])
    m.rope = sb("rope", [P, TB, 2, 2, DH])
    m.w_router = sb("w_router", [P, KC, NE])
    m.w_sgu = sb("w_sgu", [P, KC, 2 * SHID])
    m.w_sdn = sb("w_sdn", [HID, 2, D])
    m.w_qkv = sb("w_qkv", [P, KC, 3 * D])
    m.w_proj = sb("w_proj", [P, KC, D])
    m.slots = sb("slots", [P, TILES, TOPK], U32)
    m.weights = sb("weights", [P, TILES, TOPK])
    m.taken = sb("taken", [P, NE], BF16)
    m.scatter_slots = [sb(f"scatter_slots{u}", [P, TB * TOPK], U32) for u in range(2)]
    m.gather_slots = sb("gather_slots", [P, TB * TOPK], U32)
    m.cur_weights = sb("cur_weights", [P, TB, TOPK])
    m.stats = sb("stats", [P, TILES, 6])
    m.mv = sb("mv", [P, TILES, 2])
    m.cur_mv = sb("cur_mv", [P, TB, 2])
    m.var_eps = sb("var_eps", [P, TILES])
    m.rstd = sb("rstd", [P, TILES])
    m.minus_half = sb("minus_half", [P, TILES])
    m.eps = sb("eps", [P, TILES])
    m.xn = sb("xn", [P, TB, D])
    m.xn_sent = sb("xn_sent", [P, TB, D])
    m.work = sb("work", [P, 3840])
    m.banks = ctx.enter_context(nc.psum_tensor("banks", [P, 8, 512], F32))
    m.expert_in = nc.dram_tensor("expert_in", [SLOTS, D], F32, kind="Internal").ap()
    m.expert_out = nc.dram_tensor("expert_out", [SLOTS + P, D], F32, kind="Internal").ap()
    return m



class NormSems:
    def __init__(self, sem, name):
        self.var = sem(f"{name}_variance_ready")
        self.rstd = sem(f"{name}_rstd_ready")
        self.xn = sem(f"{name}_normed_ready")
        self.turned = sem(f"{name}_transposed")
        self.xnT = sem(f"{name}_normed_T_ready")


def norm_stats_vector(nc, m, chain, s, x_tiles, tiles=TB):
    for t in range(tiles):
        chain.count(nc.vector.bn_stats(m.stats[:, t, :], x_tiles[t]))
    chain.engine.wait_ge(chain.sem, chain.links)
    for t in range(tiles):
        chain.count(nc.vector.bn_aggr(m.mv[:, t, :], m.stats[:, t, :]))
    chain.engine.wait_ge(chain.sem, chain.links)
    nc.vector.tensor_scalar(m.var_eps[:, 0:tiles], m.mv[:, 0:tiles, 1], EPS, None, ALU.add).then_inc(s.var, 1)


def norm_apply_vector(nc, m, eng, s, turn, x_tiles, xn, tiles=TB, free=None):
    if free:
        eng.wait_ge(*free)
    eng.wait_ge(s.rstd, turn + 1)
    for t in range(tiles):
        nc.vector.tensor_scalar(xn[:, t, :], x_tiles[t], m.mv[:, t, 0:1], m.rstd[:, t:t + 1],
                                ALU.subtract, ALU.mult).then_inc(s.xn, 1)


def norm_vector(nc, m, eng, chain, s, turn, x_tiles, xn, tiles=TB, free=None):
    norm_stats_vector(nc, m, chain, s, x_tiles, tiles)
    norm_apply_vector(nc, m, eng, s, turn, x_tiles, xn, tiles, free)


def norm_pool(nc, m, eng, s, turn, tiles=TB):
    eng.wait_ge(s.var, turn + 1)
    nc.gpsimd.tensor_tensor(m.rstd[:, 0:tiles], m.var_eps[:, 0:tiles], m.minus_half[:, 0:tiles],
                            ALU.pow).then_inc(s.rstd, 1)


def norm_tensor(nc, m, eng, s, turn, xn, out, tiles=TB):
    for t in range(tiles):
        eng.wait_ge(s.xn, turn * tiles + (t + 1))
        for c in range(KC):
            last = nc.tensor.transpose(out[:, c, t * P:(t + 1) * P], xn[:, t, c * P:(c + 1) * P], m.ident[:, :])
    last.then_inc(s.turned, 1)


def norm_scalar(nc, eng, s, turn, src, dst):
    eng.wait_ge(s.turned, turn + 1)
    nc.scalar.copy(dst, src).then_inc(s.xnT, 1)


class RouteSems:
    def __init__(self, sem, name):
        self.logits = sem(f"{name}_logits_ready")
        self.shared_in = sem(f"{name}_shared_gate_up_ready")
        self.neg_max = sem(f"{name}_neg_max_ready")
        self.exps = sem(f"{name}_exps_ready")
        self.mask = sem(f"{name}_choice_mask_ready")
        self.rank = sem(f"{name}_rank_ready")
        self.slots = [sem(f"{name}_slots_ready{u}") for u in range(2)]
        self.scattered = sem(f"{name}_rows_scattered")
        self.tanh = sem(f"{name}_shared_tanh_ready")
        self.hidden = sem(f"{name}_shared_hidden_ready")
        self.turned = sem(f"{name}_shared_hidden_turned")
        self.hiddenT = sem(f"{name}_shared_hidden_T_ready")
        self.shared_out = sem(f"{name}_shared_out_ready")
        self.out_read = sem(f"{name}_shared_out_read")
        self.rank_read = sem(f"{name}_rank_read")


class RoutePlaces:

    def __init__(self, m, beside=False):
        w = m.work
        self.xnT = flat(w, 0, (KC, T))
        self.logits = flat(w, 512, (TB, NE))
        self.top = flat(w, 640, (TB, 8))
        self.neg_max = flat(w, 656, (TB,))
        self.sum = flat(w, 658, (TB,))
        self.rsum = flat(w, 660, (TB,))
        self.top_exp = flat(w, 664, (TB, 8))
        self.index_f = flat(w, 680, (TB, 8))
        self.rank = flat(w, 696, (TB, TOPK))
        self.keep = flat(w, 708, (TB, TOPK))
        self.slot_f = flat(w, 720, (TB, TOPK))
        self.index = w[:, 732:748].bitcast(U32).rearrange("p (a b) -> p a b", b=8)
        self.exps = flat(w, 748, (TB, NE))
        self.mask = w[:, 876:940].bitcast(BF16).rearrange("p (a b) -> p a b", b=NE)
        self.onehot = flat(w, 940, (TB, TOPK, NE))
        self.product = flat(w, 1708, (TB, TOPK, NE))
        self.tanh = flat(w, 2476, (TB, SHID))
        self.hidden = flat(w, 2860, (TB, SHID))
        self.hiddenT = flat(w, 3244, (2, T))
        logits, rank, shared, hidden, out = (3, 7, (0, 1), 7, 7) if beside else (6, 4, (0, 1), 2, 3)
        self.p_logits = m.banks[:, logits, 0:TB * NE].rearrange("p (a b) -> p a b", b=NE)
        self.p_rank = m.banks[:, rank, 0:TB * NE].rearrange("p (a b) -> p a b", b=NE)
        self.p_shared = [m.banks[:, bank, :] for bank in shared]
        self.p_hiddenT = m.banks[:, hidden, :].rearrange("p (a b) -> p a b", b=T)
        self.p_out = m.banks[:, out, :].rearrange("p (a b) -> p a b", b=D)


def route_tensor_front(nc, m, r, eng, s, ready):
    eng.wait_ge(*ready)
    for t in range(TB):
        for c in range(KC):
            last = nc.tensor.matmul(r.p_logits[:, t, :], r.xnT[:, c, t * P:(t + 1) * P], m.w_router[:, c, :],
                                    start=(c == 0), stop=(c == KC - 1))
    last.then_inc(s.logits, 1)
    for t in range(TB):
        for c in range(KC):
            last = nc.tensor.matmul(r.p_shared[t][:, 0:2 * SHID], r.xnT[:, c, t * P:(t + 1) * P],
                                    m.w_sgu[:, c, :], start=(c == 0), stop=(c == KC - 1))
        last.then_inc(s.shared_in, 1)


def route_tensor_rank(nc, m, r, eng, s, turn):
    eng.wait_ge(s.mask, turn + 1)
    for t in range(TB):
        nc.tensor.matmul(r.p_rank[:, t, :], m.before_b[:, :], r.mask[:, t, :], start=True, stop=False)
        last = nc.tensor.matmul(r.p_rank[:, t, :], m.ones_b[:, :], m.taken[:, :], start=False, stop=(t == 0))
        if t == 1:
            last = nc.tensor.matmul(r.p_rank[:, t, :], m.ones_b[:, :], r.mask[:, 0, :], start=False, stop=True)
    last.then_inc(s.rank, 1)


def route_tensor_hidden(nc, m, r, eng, s, turn):
    for t in range(TB):
        eng.wait_ge(s.hidden, turn * TB + (t + 1))
        for j in range(2):
            last = nc.tensor.transpose(r.p_hiddenT[0:HID, j, t * P:(t + 1) * P],
                                       r.hidden[:, t, j * HID:(j + 1) * HID], m.ident[:, :])
    last.then_inc(s.turned, 1)


def route_tensor_out(nc, m, r, eng, s, turn):
    eng.wait_ge(s.hiddenT, turn + 1)
    for t in range(TB):
        for j in range(2):
            last = nc.tensor.matmul(r.p_out[:, t, :], r.hiddenT[0:HID, j, t * P:(t + 1) * P], m.w_sdn[:, j, :],
                                    start=(j == 0), stop=(j == 1))
    last.then_inc(s.shared_out, 1)


def route_tensor(nc, m, r, eng, s, ready, turn):
    route_tensor_front(nc, m, r, eng, s, ready)
    route_tensor_rank(nc, m, r, eng, s, turn)
    route_tensor_hidden(nc, m, r, eng, s, turn)
    route_tensor_out(nc, m, r, eng, s, turn)


def route_scalar_exps(nc, r, eng, s, turn):
    eng.wait_ge(s.neg_max, turn + 1)
    for t in range(TB):
        nc.scalar.activation(r.exps[:, t, :], r.logits[:, t, :], ACT.Exp, bias=r.neg_max[:, t:t + 1],
                             accum_out=r.sum[:, t:t + 1])
        last = nc.scalar.activation(r.top_exp[:, t, :], r.top[:, t, :], ACT.Exp, bias=r.neg_max[:, t:t + 1])
    last.then_inc(s.exps, 1)


def route_scalar_tanh(nc, r, eng, s, turn):
    for t in range(TB):
        eng.wait_ge(s.shared_in, turn * TB + (t + 1))
        nc.scalar.activation(r.tanh[:, t, :], r.p_shared[t][:, 0:SHID], ACT.Tanh, scale=0.5).then_inc(s.tanh, 1)


def route_scalar_hidden(nc, r, eng, s, turn):
    eng.wait_ge(s.turned, turn + 1)
    nc.scalar.copy(r.hiddenT[0:HID, :, :], r.p_hiddenT[0:HID, :, :]).then_inc(s.hiddenT, 1)


def route_scalar(nc, r, eng, s, turn):
    route_scalar_exps(nc, r, eng, s, turn)
    route_scalar_tanh(nc, r, eng, s, turn)
    route_scalar_hidden(nc, r, eng, s, turn)


def route_vector_top(nc, m, r, eng, chain, s, turn):
    eng.wait_ge(s.logits, turn + 1)
    chain(nc.vector.tensor_copy(r.logits[:, :, :], r.p_logits))
    for t in range(TB):
        last = nc.vector.max(r.top[:, t, :], r.logits[:, t, :])
        if t == 0:
            chain.count(last)
    chain(last)
    nc.vector.tensor_scalar(r.neg_max, r.top[:, :, 0], -1.0, None, ALU.mult).then_inc(s.neg_max, 1)


def route_vector_mask(nc, m, r, eng, chain, s, turn):
    for t in range(TB):
        chain.count(nc.vector.max_index(r.index[:, t, :], r.top[:, t, :], r.logits[:, t, :]))
    eng.wait_ge(chain.sem, chain.links)
    chain(nc.vector.tensor_copy(r.index_f, r.index))
    numbers = m.expert_no[:, :].unsqueeze(1).broadcast_to([P, TOPK, NE])
    for t in range(TB):
        chosen = r.index_f[:, t, 0:TOPK].unsqueeze(2).broadcast_to([P, TOPK, NE])
        chain.count(nc.vector.tensor_tensor(r.onehot[:, t], numbers, chosen, ALU.is_equal))
    eng.wait_ge(chain.sem, chain.links)
    for t in range(TB):
        with nc.allow_low_precision(reason="sums of zeros and a one"):
            last = nc.vector.tensor_reduce(r.mask[:, t, :], r.onehot[:, t].rearrange("p k e -> p e k"), AX.X,
                                           ALU.add)
        if t == 0:
            chain.count(last)
    last.then_inc(s.mask, 1)


def route_vector_hidden(nc, r, eng, chain, s, turn):
    for t in range(TB):
        eng.wait_ge(s.tanh, turn * TB + (t + 1))
        chain(nc.vector.scalar_tensor_tensor(out=r.tanh[:, t, :], in0=r.tanh[:, t, :], scalar=1.0,
                                             in1=r.p_shared[t][:, 0:SHID], op0=ALU.add, op1=ALU.mult))
        nc.vector.tensor_tensor(r.hidden[:, t, :], r.tanh[:, t, :], r.p_shared[t][:, SHID:2 * SHID],
                                ALU.mult).then_inc(s.hidden, 1)


def route_vector_slots(nc, m, r, eng, chain, s, turn, sequence, u):
    eng.wait_ge(s.rank, turn + 1)
    for t in range(TB):
        ranks = r.p_rank[:, t, :].unsqueeze(1).broadcast_to([P, TOPK, NE])
        chain.count(nc.vector.tensor_tensor(r.product[:, t], r.onehot[:, t], ranks, ALU.mult))
    eng.wait_ge(chain.sem, chain.links)
    eng.sem_inc(s.rank_read, 1)
    chain(nc.vector.tensor_reduce(r.rank, r.product, AX.X, ALU.add))
    chain.count(nc.vector.tensor_scalar(r.keep, r.rank, float(CAP), None, ALU.is_lt))
    chain(nc.vector.scalar_tensor_tensor(out=r.slot_f, in0=r.index_f[:, :, 0:TOPK], scalar=float(CAP),
                                         in1=r.rank, op0=ALU.mult, op1=ALU.add))
    chain(nc.vector.scalar_tensor_tensor(out=r.slot_f, in0=r.slot_f, scalar=-float(SLOTS), in1=r.keep,
                                         op0=ALU.add, op1=ALU.mult))
    chain(nc.vector.tensor_scalar(m.scatter_slots[u][:, :].rearrange("p (a b) -> p a b", b=TOPK), r.slot_f,
                                  float(SLOTS), None, ALU.add))
    nc.vector.tensor_copy(m.slots[:, bass.ds(sequence * TB, TB), :],
                          m.scatter_slots[u][:, :].rearrange("p (a b) -> p a b", b=TOPK)).then_inc(s.slots[u], 1)
    chain(nc.vector.tensor_tensor(m.taken[:, :], m.taken[:, :], r.mask[:, 0, :], ALU.add))
    chain(nc.vector.tensor_tensor(m.taken[:, :], m.taken[:, :], r.mask[:, 1, :], ALU.add))
    eng.wait_ge(s.exps, turn + 1)
    chain(nc.vector.reciprocal(r.rsum, r.sum))
    for t in range(TB):
        chain.count(nc.vector.tensor_scalar(r.top_exp[:, t, 0:TOPK], r.top_exp[:, t, 0:TOPK], r.rsum[:, t:t + 1], 0.25,
                                            ALU.mult, ALU.mult))
    eng.wait_ge(chain.sem, chain.links)
    chain(nc.vector.tensor_tensor(m.weights[:, bass.ds(sequence * TB, TB), :], r.top_exp[:, :, 0:TOPK], r.keep,
                                  ALU.mult))


def route_vector_out(nc, r, eng, chain, s, turn, x_tiles):
    eng.wait_ge(s.shared_out, turn + 1)
    for t in range(TB):
        chain.count(nc.vector.scalar_tensor_tensor(out=x_tiles[t], in0=r.p_out[:, t, :], scalar=0.25, in1=x_tiles[t],
                                                   op0=ALU.mult, op1=ALU.add))
    eng.wait_ge(chain.sem, chain.links)
    eng.sem_inc(s.out_read, 1)


def route_vector(nc, m, r, eng, chain, s, turn, sequence, x_tiles, u, slots_first=False):
    route_vector_top(nc, m, r, eng, chain, s, turn)
    route_vector_mask(nc, m, r, eng, chain, s, turn)
    if slots_first:
        route_vector_slots(nc, m, r, eng, chain, s, turn, sequence, u)
    route_vector_hidden(nc, r, eng, chain, s, turn)
    if not slots_first:
        route_vector_slots(nc, m, r, eng, chain, s, turn, sequence, u)
    route_vector_out(nc, r, eng, chain, s, turn, x_tiles)


SCATTER = 16 * TB * TOPK


def scattered(turn):
    return turn * SCATTER + SCATTER


def route_pool(nc, m, eng, s, xn, u, last_slot):
    eng.wait_ge(s.slots[u], 1)
    eng.sem_clear(s.slots[u])
    for t in range(TB):
        for k in range(TOPK):
            at = t * TOPK + k
            nc.gpsimd.indirect_dma_start(
                out=m.expert_in, out_offset=bass.IndirectOffsetOnAxis(m.scatter_slots[u][:, at:at + 1], 0),
                in_=xn[:, t, :], in_offset=None, bounds_check=last_slot, oob_is_err=False
            ).then_inc(s.scattered, 16)



GROUP = 8
GROUPS = NE // GROUP
EARLY_GROUPS = 5


def load_expert_group(m, a, eng, g):
    if not isinstance(g, int) or g > 0:
        eng.wait_ge(m.s_expert_weights, g * 32)
    n, k = GROUP * KC * SHID, GROUP * D
    for own, source, width in ((m.w_gu, a["gate_up"], n), (m.w_dn[0:HID], a["down"], k)):
        eng.dma_start(own[:, bass.ds(g * width, width)], source[:, bass.ds(g * width, width)]
                      ).then_inc(m.s_expert_weights, 16)


def first_phase(nc, m, a, sem):
    s_const = sem("constants_loaded")
    s_x = sem("x_loaded")
    s_w = sem("small_weights_loaded")
    s_exp = sem("expert_weights_loaded")
    s_made = m.made = sem("constants_made")
    s_zero = sem("zeros_made")
    s_zeroed = sem("scratch_zeroed")
    v_chain = sem("first_vector_chain")
    norm, s = m.norm, m.route
    r = RoutePlaces(m)
    consts = m.w_dn[:, 0:512]
    zeros = m.w_dn[:, 1024:3072]
    xn = [m.xn, m.xn_sent]
    m.s_expert_weights, m.s_attn_weights = s_exp, sem("attention_weights_loaded")
    x_in = a["x"].rearrange("(t p) c -> p t c", p=P)
    s_free = sem("places_to_scatter_from_free")
    s_stats = sem("all_means_and_deviations_ready")

    with nc.Block() as block:
        @block.sync
        def _(sp):
            for h in range(2):
                tiles = slice(h * TILES // 2, (h + 1) * TILES // 2)
                sp.dma_start(m.x[:, tiles, :], x_in[:, tiles, :]).then_inc(s_x, 16)
            sp.dma_start(m.w_router[:, :, :], a["router"].rearrange("(c p) n -> p c n", p=P)).then_inc(s_w, 16)
            sp.dma_start(m.w_sgu[:, :, 0:SHID], a["shared_gate"].rearrange("(c p) n -> p c n", p=P)).then_inc(s_w, 16)
            sp.dma_start(m.w_sgu[:, :, SHID:2 * SHID],
                         a["shared_up"].rearrange("(c p) n -> p c n", p=P)).then_inc(s_w, 16)
            sp.dma_start(m.w_sdn[:, :, :], a["shared_down"].rearrange("(j p) n -> p j n", p=HID)).then_inc(s_w, 16)
            sp.wait_ge(s_zero, 1)
            sp.wait_ge(s_x, 32)
            for g in range(4):
                sp.dma_start(m.expert_in[g * 1024:(g + 1) * 1024, :].rearrange("(p n) d -> p (n d)", p=P),
                             zeros).then_inc(s_zeroed, 16)
            sp.dma_start(m.expert_out[SLOTS:SLOTS + P, :], zeros[:, 0:D]).then_inc(s_zeroed, 16)
            sp.wait_ge(s_zeroed, 80)
            sp.wait_ge(s_made, 9)
            for g in range(EARLY_GROUPS):
                if g >= 3:
                    sp.wait_ge(s.scattered, scattered(g - 3))
                load_expert_group(m, a, sp, g)

        @block.scalar
        def _(act):
            act.dma_start(consts[:, 0:448], a["consts"][:, 0:448]).then_inc(s_const, 16)
            act.dma_start(m.rope[:, :, :, :, :], a["rope"].rearrange("p (a b c d) -> p a b c d", b=2, c=2, d=DH)
                          ).then_inc(s_const, 16)
            with act.Fori(0, B) as i:
                norm_scalar(nc, act, norm, i, m.banks[:, 7, :], m.work[:, 0:512])
                route_scalar(nc, r, act, s, i)

        @block.vector
        def _(dve):
            nc.vector.memset(zeros, 0.0).then_inc(s_zero, 1)
            nc.vector.memset(m.minus_half[:, :], -0.5)
            nc.vector.memset(m.eps[:, :], EPS)
            nc.vector.memset(m.taken[:, :], 0.0)
            nc.vector.memset(m.ones_b[:, :], 1.0)
            dve.wait_ge(s_const, 32)
            nc.vector.tensor_copy(m.ident[:, :], consts[:, 0:P]).then_inc(s_made, 1)
            for wide in (m.ident_b, m.causal_b):
                nc.vector.memset(wide[:, P:2 * P], 0.0).then_inc(s_made, 1)
            for first in (0, 2 * P):
                nc.vector.tensor_copy(m.ident_b[:, first:first + P], consts[:, 0:P]).then_inc(s_made, 1)
                nc.vector.tensor_scalar(m.causal_b[:, first:first + P], consts[:, 2 * P:3 * P], MASKED, None, ALU.mult
                                        ).then_inc(s_made, 1)
            nc.vector.tensor_copy(m.before_b[:, :], consts[:, P:2 * P]).then_inc(s_made, 1)
            nc.vector.tensor_copy(m.expert_no[:, :], consts[:, 3 * P:3 * P + NE]).then_inc(s_made, 1)
            dve.wait_ge(s_made, 9)
            dve.wait_ge(s_x, 32)
            stats_chain = Chain(dve, v_chain)
            for t in range(TILES):
                last = nc.vector.bn_stats(m.stats[:, t, :], m.x[:, t, :])
                stats_chain.count(last)
            dve.wait_ge(v_chain, stats_chain.links)
            for t in range(TILES):
                stats_chain.count(nc.vector.bn_aggr(m.mv[:, t, :], m.stats[:, t, :]))
            dve.wait_ge(v_chain, stats_chain.links)
            nc.vector.tensor_scalar(m.var_eps[:, :], m.mv[:, :, 1], EPS, None, ALU.add).then_inc(s_stats, 1)
            dve.sem_inc(s_free, 2)
            dve.sem_inc(norm.var, B)
            dve.sem_inc(norm.rstd, B)
            dve.wait_ge(s_stats, 2)
            with dve.Fori(0, B // 2) as i:
                for u in range(2):
                    turn = i * 2 + u
                    chain = Chain(dve, v_chain)
                    x_tiles = [m.x[:, i * (2 * TB) + (u * TB + t), :] for t in range(TB)]
                    chain(nc.vector.tensor_copy(m.cur_mv[:, :, :], m.mv[:, bass.ds(i * (2 * TB) + u * TB, TB), :]))
                    dve.wait_ge(s_free, turn + 1)
                    for t in range(TB):
                        nc.vector.tensor_scalar(xn[u][:, t, :], x_tiles[t], m.cur_mv[:, t, 0:1], m.cur_mv[:, t, 1:2],
                                                ALU.subtract, ALU.mult).then_inc(norm.xn, 1)
                    route_vector(nc, m, r, dve, chain, s, turn, turn, x_tiles, u)

        @block.tensor
        def _(pe):
            pe.wait_ge(s_made, 9)
            pe.wait_ge(s_w, 64)
            with pe.Fori(0, B // 2) as i:
                for u in range(2):
                    turn = i * 2 + u
                    norm_tensor(nc, m, pe, norm, turn, xn[u], m.banks[:, 7, :].rearrange("p (a b) -> p a b", b=T))
                    route_tensor(nc, m, r, pe, s, (norm.xnT, turn + 1), turn)

        @block.gpsimd
        def _(pool):
            last_slot = pool.to_reg(SLOTS - 1)
            pool.wait_ge(s_stats, 1)
            nc.gpsimd.tensor_tensor(m.mv[:, :, 1], m.var_eps[:, :], m.minus_half[:, :], ALU.pow).then_inc(s_stats, 1)
            pool.wait_ge(s_zeroed, 80)
            with pool.Fori(0, B // 2) as i:
                for u in range(2):
                    route_pool(nc, m, pool, s, xn[u], u, last_slot)
                    pool.wait_ge(s.scattered, scattered(i * 2 + u))
                    pool.sem_inc(s_free, 1)



RING = 4


class ExpertSems:
    def __init__(self, sem):
        self.rows = [sem(f"expert_rows_loaded{b}") for b in range(RING)]
        self.rows_turned = sem("expert_rows_turned")
        self.rowsT = sem("expert_rows_T_ready")
        self.gate_up = sem("expert_gate_up_ready")
        self.tanh = sem("expert_tanh_ready")
        self.gated = sem("expert_gated_ready")
        self.hidden = sem("expert_hidden_ready")
        self.hidden_turned = sem("expert_hidden_turned")
        self.hiddenT = sem("expert_hidden_T_ready")
        self.out = sem("expert_out_ready")
        self.copied = sem("expert_out_copied")
        self.stored = [sem(f"expert_out_stored{b}") for b in range(RING)]


class with_turn:

    def __init__(self, stage):
        self.stage = stage


def in_steps(engine, stages, items=PAIRS, ring=RING):
    longest = max(lag for lag, _ in stages)
    turns = (items - longest) // ring

    def run(stage, item, place, turn):
        if isinstance(stage, with_turn):
            stage.stage(item, place, turn)
        else:
            stage(item, place)

    def peeled(p):
        for lag, stage in stages:
            if 0 <= p - lag < items:
                run(stage, p - lag, (p - lag) % ring, (p - lag) // ring)

    for p in range(longest):
        peeled(p)
    with engine.Fori(0, turns) as i:
        for u in range(ring):
            for lag, stage in stages:
                at = longest + u - lag
                run(stage, i * ring + at, at % ring, i + at // ring)
    for p in range(longest + turns * ring, items + longest):
        peeled(p)


def experts_phase(nc, m, a, call):
    x, w = m.experts, m.work
    rows = [flat(w, 256 * b, (D,)) for b in range(RING)]
    rowsT = [flat(w, 1024 + 256 * b, (KC, P)) for b in range(2)]
    tanh = [flat(w, 1536 + 192 * b, (2, HID)) for b in range(2)]
    hidden = [flat(w, 1920 + 192 * b, (2, HID)) for b in range(2)]
    hiddenT = [flat(w, 2304 + 128 * b, (2, CAP)) for b in range(2)]
    out = [flat(w, 2560 + 512 * b, (2, D)) for b in range(2)]
    p_rowsT = [m.banks[:, b, 0:D].rearrange("p (c t) -> p c t", t=P) for b in range(2)]
    p_gu = [m.banks[0:CAP, 2 + b, 0:2 * SHID].rearrange("p (e n) -> p e n", n=SHID) for b in range(2)]
    p_hiddenT = [m.banks[0:HID, 4 + b, 0:2 * CAP].rearrange("p (e n) -> p e n", n=CAP) for b in range(2)]
    p_out = [m.banks[0:CAP, 6 + b, :].rearrange("p (e n) -> p e n", n=D) for b in range(2)]
    w_gu = m.w_gu[:, :].rearrange("p (e c n) -> p e c n", c=KC, n=SHID)
    w_dn = m.w_dn[0:HID, :].rearrange("p (e n) -> p e n", n=D)
    before = call * PAIRS

    def rows_loaded(pair, b):
        return pair * (16 // RING) + (16 + (before - b) * 16 // RING)

    def out_stored(pair, b):
        return pair * (32 // RING) + (64 + (before - b) * 32 // RING)

    with nc.Block() as block:
        @block.sync
        def _(sp):
            if call == 0:
                sp.sem_inc(x.rows_turned, RING)

            def load(pair, b):
                sp.wait_ge(x.rows_turned, pair + (before + 1))
                sp.dma_start(rows[b], m.expert_in[bass.ds(pair * P, P), :]).then_inc(x.rows[b], 16)

            fetching = GROUPS - EARLY_GROUPS if call == 0 else 0
            if fetching:
                with sp.Fori(0, fetching) as i:
                    for b in range(RING):
                        load(i * RING + b, b)
                    load_expert_group(m, a, sp, i + EARLY_GROUPS)
                sp.dma_start(m.w_qkv[:, :, :], a["qkv"].rearrange("(c p) n -> p c n", p=P)
                             ).then_inc(m.s_attn_weights, 16)
                sp.dma_start(m.w_proj[:, :, :], a["proj"].rearrange("(c p) n -> p c n", p=P)
                             ).then_inc(m.s_attn_weights, 16)
            with sp.Fori(fetching, GROUPS) as i:
                for b in range(RING):
                    load(i * RING + b, b)

        if call == 1:
            @block.gpsimd
            def _(pool):
                for part, groups_used in enumerate((2, 3, 4, 6), 1):
                    pool.wait_ge(x.gate_up, before + groups_used * RING)
                    load_last_weights(m, a, pool, part, groups_used)

        @block.scalar
        def _(act):
            if call == 0:
                act.sem_inc(x.copied, 2)
                for b in range(RING):
                    act.sem_inc(x.stored[b], 32)

            def copy_rows(pair, b):
                act.wait_ge(x.rows_turned, pair + (before + RING + 1))
                nc.scalar.copy(rowsT[b % 2], p_rowsT[b % 2]).then_inc(x.rowsT, 1)

            def gate(pair, b):
                act.wait_ge(x.gate_up, pair + (before + 1))
                nc.scalar.activation(tanh[b % 2][0:CAP], p_gu[b % 2][:, :, 0:HID], ACT.Tanh,
                                     scale=0.5).then_inc(x.tanh, 1)

            def store(pair, b):
                act.wait_ge(x.out, pair + (before + 1))
                act.wait_ge(x.stored[(b + 2) % RING], out_stored(pair - 2, (b + 2) % RING))
                nc.scalar.copy(out[b % 2][0:CAP], p_out[b % 2]).then_inc(x.copied, 1)
                act.wait_ge(x.copied, pair + (before + 3))
                for e in range(2):
                    act.dma_start(m.expert_out[bass.ds(pair * P + e * CAP, CAP), :],
                                  out[b % 2][0:CAP, e, :]).then_inc(x.stored[b], 16)

            in_steps(act, [(0, copy_rows), (1, gate), (3, store)])
            for b in range(RING):
                act.wait_ge(x.stored[b], out_stored(PAIRS - RING + b, b))

        @block.vector
        def _(dve):
            def gated(pair, b):
                dve.wait_ge(x.tanh, pair + (before + 1))
                nc.vector.scalar_tensor_tensor(out=tanh[b % 2][0:CAP], in0=tanh[b % 2][0:CAP], scalar=1.0,
                                               in1=p_gu[b % 2][:, :, 0:HID], op0=ALU.add,
                                               op1=ALU.mult).then_inc(x.gated, 1)
                dve.wait_ge(x.gated, pair + (before + 1))
                nc.vector.tensor_tensor(hidden[b % 2][0:CAP], tanh[b % 2][0:CAP], p_gu[b % 2][:, :, HID:2 * HID],
                                        ALU.mult).then_inc(x.hidden, 1)

            def copy_hidden(pair, b):
                dve.wait_ge(x.hidden_turned, pair + (before + 1))
                nc.vector.tensor_copy(hiddenT[b % 2][0:HID], p_hiddenT[b % 2]).then_inc(x.hiddenT, 1)

            in_steps(dve, [(1, gated), (2, copy_hidden)])

        @block.tensor
        def _(pe):
            if call == 1:
                pe.wait_ge(m.s_refetched, 48)

            def turn_rows(pair, b):
                pe.wait_ge(x.rows[b], rows_loaded(pair, b))
                for c in range(KC):
                    last = nc.tensor.transpose(p_rowsT[b % 2][:, c, :], rows[b][:, c * P:(c + 1) * P], m.ident[:, :])
                last.then_inc(x.rows_turned, 1)

            def gate_up(pair, b, turn):
                pe.wait_ge(m.s_expert_weights, (turn + 1) * 32)
                pe.wait_ge(x.rowsT, pair + (before + 1))
                for e in range(2):
                    for c in range(KC):
                        last = nc.tensor.matmul(p_gu[b % 2][:, e, :], rowsT[b % 2][:, c, e * CAP:(e + 1) * CAP],
                                                w_gu[:, pair * 2 + e, c, :], start=(c == 0), stop=(c == KC - 1))
                last.then_inc(x.gate_up, 1)

            def turn_hidden(pair, b):
                pe.wait_ge(x.hidden, pair + (before + 1))
                for e in range(2):
                    last = nc.tensor.matmul(p_hiddenT[b % 2][:, e, :], hidden[b % 2][0:CAP, e, :],
                                            m.ident[0:CAP, 0:CAP], start=True, stop=True)
                last.then_inc(x.hidden_turned, 1)

            def down(pair, b):
                pe.wait_ge(x.hiddenT, pair + (before + 1))
                pe.wait_ge(x.copied, pair + (before + 1))
                for e in range(2):
                    last = nc.tensor.matmul(p_out[b % 2][:, e, :], hiddenT[b % 2][0:HID, e, :],
                                            w_dn[:, pair * 2 + e, :], start=True, stop=True)
                last.then_inc(x.out, 1)

            in_steps(pe, [(0, turn_rows), (1, with_turn(gate_up)), (2, turn_hidden), (3, down)])



UNITS = 16
GROUPS4 = UNITS // 4
UPAIRS = UNITS // 2
COPIES = 5
SLOTS3 = 3


class AttnSems:
    def __init__(self, sem, name):
        self.qkv = sem(f"{name}_qkv_ready")
        self.biased = sem(f"{name}_qkv_biased")
        self.v = sem(f"{name}_v_ready")
        self.rope = sem(f"{name}_rope_ready")
        self.turned = sem(f"{name}_qk_turned")
        self.qkT = sem(f"{name}_qk_T_ready")
        self.scores = sem(f"{name}_scores_ready")
        self.neg_max = sem(f"{name}_neg_max_ready")
        self.q_turned = sem(f"{name}_q_with_max_turned")
        self.qmT = sem(f"{name}_q_with_max_T_ready")
        self.scoresT = sem(f"{name}_scores_T_ready")
        self.probs = sem(f"{name}_probs_T_ready")
        self.pv = sem(f"{name}_pv_ready")
        self.pv_copied = sem(f"{name}_pv_copied")
        self.back = sem(f"{name}_pv_turned_back")
        self.y = sem(f"{name}_y_ready")
        self.y_turned = sem(f"{name}_y_turned")
        self.yT = sem(f"{name}_y_T_ready")
        self.proj = sem(f"{name}_proj_ready")


class AttnPlaces:

    def __init__(self, m, heads, area, work, xnT, kT, w_qkv, w_proj, bias=None):
        self.heads, self.sequences = heads, UNITS // heads
        self.tiles, self.width = TB * self.sequences, heads * DH
        self.w_qkv, self.w_proj, self.bias, self.xnT = w_qkv, w_proj, bias, xnT
        self.qk = flat(area, 0, (self.tiles, 2 * heads, 32))
        self.qT = flat(area, 2048, (GROUPS4, T))
        self.kT = kT.rearrange("p (g j t) -> p g j t", j=4, t=T)
        self.v = flat(area, 4096, (self.tiles, heads, 32))
        self.pT = [flat(area, 5120 + 768 * b, (2, 3 * P)) for b in range(SLOTS3)]
        self.rsum = flat(area, 7424, (2, UNITS))
        self.y = flat(work, 0, (2, UNITS * DH))
        self.tmp = flat(work, 512, (self.tiles, 2 * self.width))
        self.pv = flat(work, 1536, (GROUPS4, T))
        self.yT = flat(work, 2560, (1024,))
        self.qkv_sb = flat(work, 3584, (self.tiles, 3 * self.width)) if bias is not None else None
        self.p_pairs = [m.banks[:, 2 * b:2 * b + 2, 0:3 * P] for b in range(SLOTS3)]
        self.one_sequence = self.sequences == 1

    def qkv_places(self, t):
        n = self.width
        if self.one_sequence:
            qk, v = ((0, 1), (7, 6))[t]
            return [(qk, 0, 0, 2 * n), (v, 0, 2 * n, 3 * n)]
        return [(t // 2, t % 2 * 3 * n, 0, 3 * n)]

    def group(self, g, t):
        return (t, 4 * g) if self.one_sequence else (TB * g + t, 0)

    def back(self, m, g, t):
        bank, col = (4 + t, g) if self.one_sequence else (4 + g // 2, g % 2 * TB + t)
        return m.banks[:, bank, col * P:(col + 1) * P]


class Beside:

    def __init__(self, m, r, s, norm, turn, sequence=None, x_tiles=None):
        self.r, self.s, self.norm, self.turn = r, s, norm, turn
        self.sequence, self.x_tiles = sequence, x_tiles
        self.p_norm = m.banks[:, 2, :].rearrange("p (a b) -> p a b", b=T)


def attn_tensor_qkv(nc, m, s, a, eng, ready, t):
    n = a.width
    eng.wait_ge(*ready)
    for bank, at, first, end in a.qkv_places(t):
        for c in range(KC):
            last = nc.tensor.matmul(m.banks[:, bank, at:at + end - first], a.xnT[:, c, t * P:(t + 1) * P],
                                    a.w_qkv[:, c, first:end], start=(c == 0), stop=(c == KC - 1))
    last.then_inc(s.qkv, 1)


def attn_tensor(nc, m, s, a, eng, turn, beside=None, ahead=None):
    n = a.width
    eng.wait_ge(s.v, turn * a.tiles + a.tiles)
    order = [(t, k) for k in range(2) for t in range(TB)] if a.one_sequence else \
            [(t, k) for t in range(a.tiles) for k in range(2)]
    for t, k in order:
        eng.wait_ge(s.rope, turn * a.tiles + (t + 1))
        for g in range(GROUPS4) if a.one_sequence else [t // TB]:
            place, first = GROUPS4 * k + g, (4 * g if a.one_sequence else 0) + k * a.heads
            last = nc.tensor.transpose(
                m.banks[:, 4 + place // 2, place % 2 * T + t % TB * P:place % 2 * T + (t % TB + 1) * P],
                a.qk[:, t, first:first + 4, :].rearrange("p h d -> p (h d)"), m.ident[:, :])
    last.then_inc(s.turned, 1)
    if beside:
        norm_tensor(nc, m, eng, beside.norm, beside.turn, m.xn_sent, beside.p_norm)
        route_tensor_front(nc, m, beside.r, eng, beside.s, (beside.norm.xnT, beside.turn + 1))
        eng.wait_ge(beside.s.neg_max, beside.turn + 1)
    eng.wait_ge(s.qkT, turn * COPIES + COPIES)

    def scores(p):
        if p >= SLOTS3:
            eng.wait_ge(s.neg_max, turn * UPAIRS + (p - SLOTS3 + 1))
        if beside and p == 2:
            eng.wait_ge(beside.s.hidden, (beside.turn + 1) * TB)
        outs = [m.banks[:, 2 * ((p + 1) % SLOTS3) + j, 0:3 * P] for j in range(2)]
        for out in outs:
            nc.tensor.matmul(out, m.ident_b[:, 0:P], m.causal_b[:, :], start=True, stop=False)
        for j, out in enumerate(outs):
            u = 2 * p + j
            q, k = a.qT[:, u // 4, :], a.kT[:, u // 4, u % 4, :]
            nc.tensor.matmul(out[:, 0:P], q[:, 0:P], k[:, 0:P], start=False, stop=False)
            last = nc.tensor.matmul(out[:, P:3 * P], q[:, P:T], k[:, 0:T], start=False, stop=True)
        last.then_inc(s.scores, 1)

    def turn_q(g):
        eng.wait_ge(s.neg_max, turn * UPAIRS + (2 * g + 2))
        if g >= 1:
            eng.wait_ge(s.qmT, turn * GROUPS4 + g)
        for t in range(TB):
            tile, head = a.group(g, t)
            last = nc.tensor.transpose(m.banks[:, 6, t * P:(t + 1) * P],
                                       a.qk[:, tile, head:head + 4, :].rearrange("p h d -> p (h d)"), m.ident[:, :])
        last.then_inc(s.q_turned, 1)

    def scores_T(p):
        if p < SLOTS3:
            eng.wait_ge(s.neg_max, turn * UPAIRS + (UPAIRS - SLOTS3 + p + 1))
        else:
            eng.wait_ge(s.probs, turn * UPAIRS + (p - SLOTS3 + 1))
        eng.wait_ge(s.qmT, turn * GROUPS4 + (p // 2 + 1))
        outs = [m.banks[:, 2 * (p % SLOTS3) + j, 0:3 * P] for j in range(2)]
        for out in outs:
            nc.tensor.matmul(out, m.causal_b[:, 0:P], m.ident_b[:, :], start=True, stop=False)
        for j, out in enumerate(outs):
            u = 2 * p + j
            q, k = a.qT[:, u // 4, :], a.kT[:, u // 4, u % 4, :]
            nc.tensor.matmul(out[:, 0:T], k[:, 0:P], q[:, 0:T], start=False, stop=False)
            last = nc.tensor.matmul(out[:, T:3 * P], k[:, P:T], q[:, P:T], start=False, stop=True)
        last.then_inc(s.scoresT, 1)

    def values(p):
        eng.wait_ge(s.probs, turn * UPAIRS + (p + 1))
        for j in range(2):
            u = 2 * p + j
            g, rows = u // 4, slice(32 * (u % 4), 32 * (u % 4) + 32)
            out, probs = m.banks[rows, 6 + g // 2, g % 2 * T:(g % 2 + 1) * T], a.pT[p % SLOTS3][:, j, :]
            (first, head), (second, _) = a.group(g, 0), a.group(g, 1)
            nc.tensor.matmul(out, a.v[:, first, head + u % 4, :], probs[:, 0:T], start=True, stop=False)
            last = nc.tensor.matmul(out[:, P:T], a.v[:, second, head + u % 4, :], probs[:, T:3 * P],
                                    start=False, stop=True)
        last.then_inc(s.pv, 1)

    def turn_back(half):
        eng.wait_ge(s.pv_copied, turn * 2 + (half + 1))
        for g in (2 * half, 2 * half + 1):
            for t in range(TB):
                last = nc.tensor.transpose(a.back(m, g, t), a.pv[:, g, t * P:(t + 1) * P], m.ident[:, :])
        last.then_inc(s.back, 1)

    for p in range(UPAIRS):
        scores(p)
        if p >= 3 and p % 2 == 1:
            turn_q((p - 3) // 2)
        if beside and p == 1:
            route_tensor_hidden(nc, m, beside.r, eng, beside.s, beside.turn)
        if beside and p == 3:
            route_tensor_out(nc, m, beside.r, eng, beside.s, beside.turn)
    if beside:
        eng.wait_ge(beside.s.out_read, beside.turn + 1)
        route_tensor_rank(nc, m, beside.r, eng, beside.s, beside.turn)
    scores_T(0)
    scores_T(1)
    turn_q(GROUPS4 - 1)
    scores_T(2)
    eng.wait_ge(s.qmT, turn * GROUPS4 + GROUPS4)
    for p in range(UPAIRS):
        if beside and p == UPAIRS // 2:
            eng.wait_ge(beside.s.rank_read, beside.turn + 1)
        values(p)
        if p + SLOTS3 < UPAIRS:
            scores_T(p + SLOTS3)
        if p == UPAIRS - 2:
            turn_back(0)
    if ahead:
        ahead(0)
    turn_back(1)
    if ahead:
        ahead(1)
    eng.wait_ge(s.y, turn * 2 + 2)
    if a.one_sequence:
        for t in range(TB):
            for c in range(KC):
                last = nc.tensor.matmul(m.banks[:, 2, c * T + t * P:c * T + (t + 1) * P],
                                        a.y[:, t, c * P:(c + 1) * P], m.ident[:, :], start=True, stop=True)
        last.then_inc(s.y_turned, 1)
        if ahead:
            ahead(2)
        eng.wait_ge(s.yT, turn + 1)
        for t in range(TB):
            for c in range(KC):
                last = nc.tensor.matmul(m.banks[:, 3, t * D:(t + 1) * D], a.yT[:, c * T + t * P:c * T + (t + 1) * P],
                                        a.w_proj[:, c, :], start=(c == 0), stop=(c == KC - 1))
        last.then_inc(s.proj, 1)
    else:
        for t in range(a.tiles):
            last = nc.tensor.matmul(m.banks[0:n, 2 + t // 4, t % 4 * P:(t % 4 + 1) * P],
                                    a.y[:, t // 4, t % 4 * n:(t % 4 + 1) * n], m.ident[:, :], start=True, stop=True)
            if t % 4 == 3:
                last.then_inc(s.y_turned, 1)
        for t in range(a.tiles):
            eng.wait_ge(s.yT, t // 4 + 1)
            last = nc.tensor.matmul(m.banks[:, (6 + t // 2) % 8, t % 2 * D:(t % 2 + 1) * D],
                                    a.yT[0:n, t * P:(t + 1) * P], a.w_proj[0:n, 0, :], start=True, stop=True)
            if t % 2:
                last.then_inc(s.proj, 1)


def copy_k(m, copy, s, a, j):
    rows = slice(32 * j, 32 * (j + 1))
    copy(a.kT[rows, :, j, :], m.banks[rows, 6:8, :].rearrange("p b (g t) -> p (b g) t", t=T)).then_inc(s.qkT, 1)


def attn_scalar_v(nc, m, s, a, eng, turn, t):
    n = a.width
    if a.one_sequence:
        eng.wait_ge(s.qkv, turn * a.tiles + (t + 1))
        v = m.banks[:, a.qkv_places(t)[1][0], 0:n]
    else:
        eng.wait_ge(s.biased, t + 1)
        v = a.qkv_sb[:, t, 2 * n:3 * n]
    nc.scalar.copy(a.v[:, t, :, 0:DH], v.rearrange("p (h d) -> p h d", d=DH)).then_inc(s.v, 1)


def attn_scalar(nc, m, s, a, eng, turn, beside=None, ahead=None):
    n = a.width
    eng.wait_ge(s.turned, turn + 1)
    nc.scalar.copy(a.qT[:, :, :], m.banks[:, 4:6, :].rearrange("p b (g t) -> p (b g) t", t=T)
                   ).then_inc(s.qkT, 1)
    if beside:
        norm_scalar(nc, eng, beside.norm, beside.turn, beside.p_norm, beside.r.xnT)
    copy_k(m, nc.scalar.copy, s, a, 3)
    if beside:
        route_scalar_tanh(nc, beside.r, eng, beside.s, beside.turn)
        route_scalar_exps(nc, beside.r, eng, beside.s, beside.turn)
        route_scalar_hidden(nc, beside.r, eng, beside.s, beside.turn)

    def copy_q(g):
        eng.wait_ge(s.q_turned, turn * GROUPS4 + (g + 1))
        nc.scalar.copy(a.qT[:, g, :], m.banks[:, 6, 0:T]).then_inc(s.qmT, 1)

    for g in range(GROUPS4 - 1):
        copy_q(g)
    for p in range(UPAIRS):
        eng.wait_ge(s.scoresT, turn * UPAIRS + (p + 1))
        if p >= SLOTS3:
            eng.wait_ge(s.pv, turn * UPAIRS + (p - SLOTS3 + 1))
        nc.scalar.activation(a.pT[p % SLOTS3], a.p_pairs[p % SLOTS3], ACT.Exp).then_inc(s.probs, 1)
        if p == 0:
            copy_q(GROUPS4 - 1)
    if ahead:
        ahead(0)
    if a.one_sequence:
        eng.wait_ge(s.y_turned, turn + 1)
        nc.scalar.copy(a.yT[:, 0:512], m.banks[:, 2, :]).then_inc(s.yT, 1)
        if ahead:
            ahead(1)
    else:
        for h in range(2):
            eng.wait_ge(s.y_turned, h + 1)
            nc.scalar.copy(a.yT[0:n, 512 * h:512 * (h + 1)], m.banks[0:n, 2 + h, :]).then_inc(s.yT, 1)


def attn_vector_rope(nc, m, s, a, eng, chain, turn, t):
    n, heads, half = a.width, a.heads, DH // 2
    if t == 0:
        chain(nc.vector.memset(a.qk[:, :, 0:heads, DH:DH + 1], 0.0))
    if a.one_sequence:
        tiles, shape = 1, "p (s h d) -> p s h d"
        eng.wait_ge(s.qkv, turn * a.tiles + (t + 1))
        z = m.banks[:, a.qkv_places(t)[0][0], 0:2 * n].rearrange(shape, s=2, d=DH)
        out = a.qk[:, t, :, :].rearrange("p (s h) d -> p s h d", s=2)
        tmp = a.tmp[:, t, :].rearrange(shape, s=2, d=DH)
        rope = m.rope[:, t % TB]
    else:
        tiles, shape = 2, "p t (h d) -> p t h d"
        both = slice(t, t + 2)
        eng.wait_ge(s.qkv, t + 2)
        nc.vector.tensor_tensor(a.qkv_sb[:, both, :], m.banks[:, t // 2, 0:6 * n].rearrange("p (t n) -> p t n", t=2),
                                a.bias.unsqueeze(1).broadcast_to([P, 2, 3 * n]), ALU.add).then_inc(s.biased, 2)
        eng.wait_ge(s.biased, t + 2)
        z = a.qkv_sb[:, both, 0:2 * n].rearrange(shape, d=DH)
        out = a.qk[:, both, :, :]
        tmp = a.tmp[:, both, :].rearrange(shape, d=DH)
        rope = m.rope[:, :, :, 1, :].rearrange("p t w d -> p w t d")

    def table(which, first, end):
        v = rope[:, which, :, first:end]
        return v.unsqueeze(2).broadcast_to([P, 2, z.shape[2], end - first])

    chain.count(nc.vector.tensor_tensor(tmp, z, table(0, 0, DH), ALU.mult))
    chain.count(nc.vector.tensor_tensor(out[:, :, :, 0:half], z[:, :, :, half:DH], table(1, 0, half), ALU.mult))
    chain(nc.vector.tensor_tensor(out[:, :, :, half:DH], z[:, :, :, 0:half], table(1, half, DH), ALU.mult))
    nc.vector.tensor_tensor(out[:, :, :, 0:DH], out[:, :, :, 0:DH], tmp, ALU.add).then_inc(s.rope, tiles)


def attn_vector(nc, m, s, a, eng, chain, turn, x_tiles, meanwhile=None, beside=None, ahead=None, after=None):
    eng.wait_ge(s.turned, turn + 1)
    for j in range(3):
        copy_k(m, nc.vector.tensor_copy, s, a, j)
    if beside:
        route_vector_top(nc, m, beside.r, eng, chain, beside.s, beside.turn)
        route_vector_hidden(nc, beside.r, eng, chain, beside.s, beside.turn)
        route_vector_mask(nc, m, beside.r, eng, chain, beside.s, beside.turn)
    for p in range(UPAIRS):
        eng.wait_ge(s.scores, turn * UPAIRS + (p + 1))
        g, at = p // 2, p % 2 * 2
        for t, cols in enumerate((slice(0, P), slice(P, 3 * P))):
            tile, head = a.group(g, t)
            last = nc.vector.tensor_reduce(a.qk[:, tile, head + at:head + at + 2, DH], a.p_pairs[(p + 1) % SLOTS3][:, :, cols],
                                           AX.X, ALU.max, negate=True)
            if t == 0:
                chain.count(last)
        eng.wait_ge(chain.sem, chain.links)
        last.then_inc(s.neg_max, 1)
        if beside and p == 5:
            route_vector_out(nc, beside.r, eng, chain, beside.s, beside.turn, beside.x_tiles)
    if meanwhile:
        meanwhile()
    for h in range(2):
        eng.wait_ge(s.pv, turn * UPAIRS + (h + 1) * (UPAIRS // 2))
        nc.vector.tensor_copy(a.pv[:, 2 * h:2 * h + 2, :], m.banks[:, 6 + h, :].rearrange("p (g t) -> p g t", t=T)
                              ).then_inc(s.pv_copied, 1)
    eng.wait_ge(s.back, turn * 2 + 2)
    for b in range(2):
        back = m.banks[:, 4 + b, :].rearrange("p (u d) -> p u d", d=32)
        chain(nc.vector.reciprocal(a.rsum[:, b, :], back[:, :, DH]))
        nc.vector.tensor_tensor(a.y[:, b, :].rearrange("p (u d) -> p u d", d=DH), back[:, :, 0:DH],
                                a.rsum[:, b, :].unsqueeze(2).broadcast_to([P, UNITS, DH]), ALU.mult).then_inc(s.y, 1)
    if ahead:
        ahead()
    if a.one_sequence:
        eng.wait_ge(s.proj, turn + 1)
        for t in range(TB):
            chain(nc.vector.tensor_tensor(x_tiles[t], x_tiles[t], m.banks[:, 3, t * D:(t + 1) * D], ALU.add))
    else:
        for t in range(0, a.tiles, 2):
            eng.wait_ge(s.proj, t // 2 + 1)
            own = m.x[:, t:t + 2, :]
            chain(nc.vector.tensor_tensor(own, own, m.banks[:, (6 + t // 2) % 8, :].rearrange("p (t d) -> p t d", d=D),
                                          ALU.add))
            after(t)


def attn_padding(engine, a, sem, eng):
    engine.memset(a.qk, 0.0).then_inc(sem, 1)
    engine.memset(a.v[:, :, :, DH:], 1.0).then_inc(sem, 1)
    engine.memset(a.kT, 0.0).then_inc(sem, 1)
    eng.wait_ge(sem, 3)
    engine.memset(a.qk[:, :, a.heads:, DH:DH + 1], 1.0).then_inc(sem, 1)
    eng.wait_ge(sem, 4)



class CombineSems:
    def __init__(self, sem, name):
        self.slots = sem(f"{name}_slots_ready")
        self.gathered = [sem(f"{name}_rows_gathered{t}") for t in range(TB)]


def combine_pool(nc, m, rows, eng, s, last_row):
    eng.wait_ge(s.slots, 1)
    eng.sem_clear(s.slots)
    for t in range(TB):
        for k in range(TOPK):
            at = t * TOPK + k
            nc.gpsimd.indirect_dma_start(
                out=rows[:, at, :], out_offset=None, in_=m.expert_out,
                in_offset=bass.IndirectOffsetOnAxis(m.gather_slots[:, at:at + 1], 0),
                bounds_check=last_row, oob_is_err=False).then_inc(s.gathered[t], 16)


def gather_vector(nc, m, eng, s, sequence):
    nc.vector.tensor_copy(m.gather_slots[:, :].rearrange("p (a b) -> p a b", b=TOPK),
                          m.slots[:, bass.ds(sequence * TB, TB), :]).then_inc(s.slots, 1)


def combine_vector(nc, m, rows, eng, chain, s, turn, sequence, x_tiles):
    chain(nc.vector.tensor_copy(m.cur_weights[:, :, :], m.weights[:, bass.ds(sequence * TB, TB), :]))
    for t in range(TB):
        eng.wait_ge(s.gathered[t], turn * (16 * TOPK) + 16 * TOPK)
    for k in range(TOPK):
        for t in range(TB):
            chain.count(nc.vector.scalar_tensor_tensor(out=x_tiles[t], in0=rows[:, t * TOPK + k, :],
                                                       scalar=m.cur_weights[:, t, k:k + 1], in1=x_tiles[t],
                                                       op0=ALU.mult, op1=ALU.add))
        eng.wait_ge(chain.sem, chain.links)



def middle_phase(nc, m, arrays, sem):
    v_chain = sem("middle_vector_chain")
    comb, norm, sr = m.combine, m.norm, m.route
    norm1 = NormSems(sem, "attention_norm")
    sa = AttnSems(sem, "attn1")
    s_pad = sem("padding_cleared")
    half = NE // 2 * D
    area = m.w_dn[:, half:]
    over = NE * KC * SHID - TB * TOPK * D
    keys = over - 512 - UNITS * T
    own = keys - 3584
    rows = flat(m.w_gu, over, (TB * TOPK, D))
    a = AttnPlaces(m, H, area, m.w_gu[:, own:keys], flat(m.w_gu, over - 512, (KC, T)), m.w_gu[:, keys:over - 512], m.w_qkv, m.w_proj)
    r, r_beside = RoutePlaces(m), RoutePlaces(m, beside=True)
    p_norm = m.banks[:, 7, :].rearrange("p (a b) -> p a b", b=T)
    p_norm1 = m.banks[:, 3, :].rearrange("p (a b) -> p a b", b=T)
    m.s_refetched = sem("covered_weights_refetched")

    with nc.Block() as block:
        @block.sync
        def _(sp):
            sp.wait_ge(sa.qkv, TB * B)
            sp.dma_start(m.w_gu[:, over - 512:], arrays["gate_up"][:, over - 512:]).then_inc(m.s_refetched, 16)
            sp.wait_ge(sa.proj, B)
            sp.dma_start(m.w_gu[:, own:over - 512], arrays["gate_up"][:, own:over - 512]).then_inc(m.s_refetched, 16)
            sp.dma_start(m.w_dn[0:HID, half:], arrays["down"][:, half:]).then_inc(m.s_refetched, 16)

        @block.scalar
        def _(act):
            def ahead(i, step):
                if step == 0:
                    norm_scalar(nc, act, norm1, i, p_norm1, a.xnT)
                attn_scalar_v(nc, m, sa, a, act, i, step)

            def turn(i, first=False, is_last=False):
                beside = None if first else Beside(m, r_beside, sr, norm, i + (B - 1))
                attn_scalar(nc, m, sa, a, act, i, beside, None if is_last else lambda step: ahead(i + 1, step))

            ahead(0, 0)
            ahead(0, 1)
            turn(0, first=True)
            with act.Fori(1, B - 1) as i:
                turn(i)
            turn(B - 1, is_last=True)
            norm_scalar(nc, act, norm, 2 * B - 1, p_norm, r.xnT)
            route_scalar(nc, r, act, sr, 2 * B - 1)

        @block.vector
        def _(dve):
            gather_vector(nc, m, dve, comb, 0)
            attn_padding(nc.vector, a, s_pad, dve)
            nc.vector.memset(m.taken[:, :], 0.0).then_inc(s_pad, 1)
            dve.wait_ge(s_pad, 5)

            def combine_and_norm(chain, i):
                x_tiles = [m.x[:, i * TB + t, :] for t in range(TB)]
                combine_vector(nc, m, rows, dve, chain, comb, i, i, x_tiles)
                if not isinstance(i, int) or i + 1 < B:
                    gather_vector(nc, m, dve, comb, i + 1)
                norm_stats_vector(nc, m, chain, norm1, x_tiles)

            def turn(i, first=False, is_last=False):
                chain = Chain(dve, v_chain)
                x_tiles = [m.x[:, i * TB + t, :] for t in range(TB)]
                beside = None if first else Beside(m, r_beside, sr, norm, i + (B - 1), i - 1,
                                                   [m.x[:, (i - 1) * TB + t, :] for t in range(TB)])

                def meanwhile():
                    if not is_last:
                        combine_and_norm(chain, i + 1)
                    if beside:
                        route_vector_slots(nc, m, r_beside, dve, chain, sr, beside.turn, beside.sequence, 1)
                    if not is_last:
                        norm_apply_vector(nc, m, dve, norm1, i + 1, [m.x[:, (i + 1) * TB + t, :] for t in range(TB)],
                                          m.xn)

                def ahead():
                    for t in range(TB):
                        attn_vector_rope(nc, m, sa, a, dve, chain, i + 1, t)

                attn_vector(nc, m, sa, a, dve, chain, i, x_tiles, meanwhile, beside, None if is_last else ahead)
                norm_stats_vector(nc, m, chain, norm, x_tiles)
                norm_apply_vector(nc, m, dve, norm, i + B, x_tiles, m.xn_sent,
                                  free=None if first else (sr.scattered, scattered(i + (B - 1))))

            chain = Chain(dve, v_chain)
            combine_and_norm(chain, 0)
            norm_apply_vector(nc, m, dve, norm1, 0, [m.x[:, t, :] for t in range(TB)], m.xn)
            for t in range(TB):
                attn_vector_rope(nc, m, sa, a, dve, chain, 0, t)
            turn(0, first=True)
            with dve.Fori(1, B - 2) as i:
                turn(i)
            turn(B - 2)
            turn(B - 1, is_last=True)
            chain = Chain(dve, v_chain)
            route_vector(nc, m, r, dve, chain, sr, 2 * B - 1, B - 1, [m.x[:, (B - 1) * TB + t, :] for t in range(TB)], 1,
                         slots_first=True)

        @block.tensor
        def _(pe):
            pe.wait_ge(m.s_attn_weights, 32)
            def ahead(i, step):
                if step == 0:
                    norm_tensor(nc, m, pe, norm1, i, m.xn, p_norm1)
                else:
                    attn_tensor_qkv(nc, m, sa, a, pe, (norm1.xnT, i + 1), step - 1)

            def turn(i, first=False, is_last=False):
                beside = None if first else Beside(m, r_beside, sr, norm, i + (B - 1))
                attn_tensor(nc, m, sa, a, pe, i, beside, None if is_last else lambda step: ahead(i + 1, step))

            for step in range(3):
                ahead(0, step)
            turn(0, first=True)
            with pe.Fori(1, B - 1) as i:
                turn(i)
            turn(B - 1, is_last=True)
            norm_tensor(nc, m, pe, norm, 2 * B - 1, m.xn_sent, p_norm)
            route_tensor(nc, m, r, pe, sr, (norm.xnT, 2 * B), 2 * B - 1)

        @block.gpsimd
        def _(pool):
            last_slot, last_row = pool.to_reg(SLOTS - 1), pool.to_reg(SLOTS + P - 1)

            def turn(i, gather=True, norm_next=True, scatter=True):
                if norm_next:
                    norm_pool(nc, m, pool, norm1, i + 1)
                if scatter:
                    route_pool(nc, m, pool, sr, m.xn_sent, 1, last_slot)
                norm_pool(nc, m, pool, norm, i + B)
                if gather:
                    combine_pool(nc, m, rows, pool, comb, last_row)

            combine_pool(nc, m, rows, pool, comb, last_row)
            norm_pool(nc, m, pool, norm1, 0)
            combine_pool(nc, m, rows, pool, comb, last_row)
            turn(0, scatter=False)
            with pool.Fori(1, B - 2) as i:
                turn(i)
            turn(B - 2, gather=False)
            turn(B - 1, gather=False, norm_next=False)
            route_pool(nc, m, pool, sr, m.xn_sent, 1, last_slot)
            pool.wait_ge(sr.scattered, scattered(2 * B - 1))



ROW_NAMES = ["amp_b", "ph_b", "ent_pb0", "ent_pb1", "path_b00", "path_b01", "path_b10", "path_b11",
             "phase00", "phase01", "phase10", "phase11", "bo", "bq", "ln4_g1", "ln4_b1"]
STEPS = 2 * NL
TURN_PI = float(np.nextafter(np.float32(np.pi), np.float32(0)))


def last_weights(m):
    w, g = Places(), m.w_gu
    w.ent_wT = flat(g, 0, (NL, EW // P, D))
    w.ent_pw = flat(g, 4096, (NL, EW // P, D))
    w.path = flat(g, 8192, (NL * PW, KC, D))
    w.amp_ph = flat(g, 10240, (KC, 2 * D))
    w.rows = flat(g, 11264, (len(ROW_NAMES), D))
    w.kv_b = flat(g, 15360, (2 * HKV * DH,))
    w.ent_b = flat(g, 15488, (NL, EW // P))
    w.gain_cols = flat(g, 15504, (STEPS, KC))
    w.shift_cols = flat(g, 15512, (STEPS, KC))
    w.lin = flat(g, 15520, (STEPS, KC, D))
    w.bias = flat(g, 17568, (2 + STEPS, D))
    w.qkv2_b = flat(g, 19104, (3 * HKV * DH,))
    w.scaled = flat(g, 19296, (KC, D))
    w.half_pi = flat(g, 19808, (1,))
    w.minus_quarter = flat(g, 19809, (1,))
    w.means = flat(g, 19812, (STEPS * KC,))
    w.bias_means = flat(g, 19820, (STEPS,))
    w.wq = flat(g, 20624, (KC, D))
    w.qkv2 = flat(g, 21136, (KC, 3 * HKV * DH))
    w.wo = flat(g, 21520, (1, D))
    w.bias_b = g[:, 21776:22544].bitcast(BF16).rearrange("p (a b) -> p a b", b=D)
    d = m.w_dn
    w.ent_b_wide = flat(d, 0, (NL, EW // P, P))
    w.phase_turns = flat(d, 6144, (NL * PW, D))
    w.phase_sin = flat(d, 2048, (NL * PW, D))
    w.phase_cos = flat(d, 3072, (NL * PW, D))
    w.mod = flat(d, 4096, (NL * PW, D))
    w.shift_wide = flat(d, 5120, (STEPS - 1, KC, P))
    w.rest = flat(g, 22544, (2 + STEPS, D))
    w.parts = [g[:, first:first + 768].bitcast(BF16).rearrange("p (a b) -> p a b", b=D)
               for first in (8192, 8960, 3072)]
    w.combined = [flat(d, 10240 + 3072 * b, (TB * TOPK, D)) for b in range(2)]
    return w


def row(w, name):
    return w.rows[:, ROW_NAMES.index(name), :]


def load_last_weights(m, a, eng, part, groups_used):
    w = last_weights(m)
    free = groups_used * GROUP * KC * SHID
    if part <= NL:
        l = part - 1
        assert free >= 6144 + 2048 * l
        eng.dma_start(w.ent_wT[:, l], a["ent_wT"][l].rearrange("(c p) d -> p c d", p=P)).then_inc(m.s_ent, 16)
        eng.dma_start(w.ent_pw[:, l], a["ent_pw"][l].rearrange("(c p) d -> p c d", p=P)).then_inc(m.s_ent, 16)
    elif part == 3:
        assert free >= 11264
        for q in range(NL * PW):
            eng.dma_start(w.path[:, q], a["path_w"][q].rearrange("(c p) d -> p c d", p=P)).then_inc(m.s_path, 16)
        eng.dma_start(w.amp_ph[:, :, 0:D], a["amp_w"].rearrange("(c p) n -> p c n", p=P)).then_inc(m.s_path, 16)
        eng.dma_start(w.amp_ph[:, :, D:2 * D], a["ph_w"].rearrange("(c p) n -> p c n", p=P)).then_inc(m.s_path, 16)
    else:
        assert free >= 15520
        n = len(ROW_NAMES) * D
        eng.dma_start(w.rows.rearrange("p a b -> p (a b)"), a["rows"].broadcast_to([P, n])).then_inc(m.s_rows, 16)
        eng.dma_start(w.kv_b, a["kv_b"].broadcast_to([P, 2 * HKV * DH])).then_inc(m.s_rows, 16)
        for own, name in ((w.ent_b, "ent_b"), (w.gain_cols, "gain_cols"), (w.shift_cols, "shift_cols")):
            eng.dma_start(own.rearrange("p a b -> p (a b)"), a[name]).then_inc(m.s_rows, 16)


def split_bias(nc, m, w, chain, rows):
    bias, rest, (one, two, three) = w.bias[:, rows], w.rest[:, rows], [part[:, rows] for part in w.parts]
    chain(nc.vector.tensor_copy(one, bias))
    chain(nc.vector.tensor_tensor(rest, bias, one, ALU.subtract))
    chain(nc.vector.tensor_copy(two, rest))
    chain(nc.vector.tensor_tensor(three, rest, two, ALU.subtract))
    chain(nc.vector.tensor_scalar(w.bias_b[:, rows], one, m.ident[:, 0:1], None, ALU.mult))
    for place, part in ((1, two), (2, three)):
        chain(nc.vector.scalar_tensor_tensor(out=w.bias_b[:, rows], in0=part, scalar=m.ident[:, place:place + 1],
                                             in1=w.bias_b[:, rows], op0=ALU.mult, op1=ALU.add))


def finish_maps(nc, m, w, eng, chain, s_ready):
    maps = w.lin.rearrange("p s c d -> p (s c) d")
    chain.count(nc.vector.tensor_reduce(w.bias_means, w.bias[:, 2:, :], AX.X, ALU.add))
    chain(nc.vector.tensor_reduce(w.means, maps, AX.X, ALU.add))
    chain.count(nc.vector.tensor_scalar(w.bias_means, w.bias_means, 1.0 / D, None, ALU.mult))
    chain(nc.vector.tensor_scalar(w.means, w.means, 1.0 / D, None, ALU.mult))
    for k in range(STEPS):
        for c in range(KC):
            gain = w.gain_cols[:, k - 1, c:c + 1] if k else float(np.sqrt(0.5))
            chain.count(nc.vector.tensor_scalar(w.lin[:, k, c, :], w.lin[:, k, c, :],
                                                w.means[:, k * KC + c:k * KC + c + 1], gain,
                                                ALU.subtract, ALU.mult))
        chain.count(nc.vector.tensor_scalar(w.bias[:, 2 + k, :], w.bias[:, 2 + k, :], w.bias_means[:, k:k + 1],
                                            None, ALU.subtract))
    eng.wait_ge(chain.sem, chain.links)
    split_bias(nc, m, w, chain, slice(2, 2 + STEPS))
    eng.sem_inc(s_ready, 1)
    for c in range(KC):
        chain.count(nc.vector.tensor_reduce(w.qkv2[:, c, 0:64].rearrange("p (h d) -> p h d", d=DH),
                                            w.wq[:, c, :].rearrange("p (h g d) -> p h d g", g=4, d=DH),
                                            AX.X, ALU.add))
    chain.count(nc.vector.tensor_reduce(w.qkv2_b[:, 0:64].rearrange("p (h d) -> p h d", d=DH),
                                        row(w, "bq").rearrange("p (h g d) -> p h d g", g=4, d=DH), AX.X, ALU.add))
    chain(nc.vector.tensor_copy(w.qkv2_b[:, 64:192], w.kv_b))
    for q in (w.qkv2[:, :, 0:64], w.qkv2_b[:, 0:64]):
        chain(nc.vector.tensor_scalar(q, q, DH ** -0.5, None, ALU.mult))


def fold_phase(nc, m, a, wave, sem):
    w, f = last_weights(m), WavePlaces(m)
    w.s_small = s_small = sem("small_last_weights_loaded")
    s_wide, s_prod = sem("bias_columns_spread"), sem("fold_product_ready")
    s_sin, s_half = sem("phase_sines_ready"), sem("phase_reduced")
    s_combined = sem("sequence_combined")
    v_chain = sem("fold_vector_chain")
    s_gathered = [sem(f"last_rows_gathered{b}") for b in range(2)]

    with nc.Block() as block:
        @block.sync
        def _(sp):
            sp.dma_start(w.wq, a["Wq"].rearrange("(c p) n -> p c n", p=P)).then_inc(s_small, 16)
            sp.dma_start(w.qkv2[:, :, 64:128], a["Wk"].rearrange("(c p) n -> p c n", p=P)).then_inc(s_small, 16)
            sp.dma_start(w.qkv2[:, :, 128:192], a["Wv"].rearrange("(c p) n -> p c n", p=P)).then_inc(s_small, 16)
            sp.dma_start(w.wo[0:64, 0, :], a["Wo"]).then_inc(s_small, 16)

        @block.gpsimd
        def _(pool):
            last_row = pool.to_reg(SLOTS + P - 1)
            for q in range(B):
                if q >= 2:
                    pool.wait_ge(s_combined, q - 1)
                if q == B - 1:
                    norm_roots_pool(nc, m, wave, pool, 0, range(1))
                for t in range(TB):
                    for k in range(TOPK):
                        nc.gpsimd.indirect_dma_start(
                            out=w.combined[q % 2][:, t * TOPK + k, :], out_offset=None, in_=m.expert_out,
                            in_offset=bass.IndirectOffsetOnAxis(m.slots[:, q * TB + t, k:k + 1], 0),
                            bounds_check=last_row, oob_is_err=False).then_inc(s_gathered[q % 2], 16)

        @block.scalar
        def _(act):
            act.wait_ge(s_half, 1)
            nc.scalar.activation(w.phase_sin, w.phase_turns, ACT.Sin).then_inc(s_sin, 1)
            act.wait_ge(s_half, 2)
            nc.scalar.activation(w.phase_cos, w.phase_cos, ACT.Sin, scale=-1.0, bias=w.half_pi).then_inc(s_sin, 1)
            wave_scalar_x(nc, w, f, wave, act, 0, BEGUN)

        @block.vector
        def _(dve):
            chain = Chain(dve, v_chain)

            def combine(q):
                x_tiles = [m.x[:, q * TB + t, :] for t in range(TB)]
                dve.wait_ge(s_gathered[q % 2], (q // 2 + 1) * 16 * TB * TOPK)
                for k in range(TOPK):
                    for t in range(TB):
                        chain.count(nc.vector.scalar_tensor_tensor(
                            out=x_tiles[t], in0=w.combined[q % 2][:, t * TOPK + k, :],
                            scalar=m.weights[:, q * TB + t, k:k + 1], in1=x_tiles[t], op0=ALU.mult, op1=ALU.add))
                    dve.wait_ge(v_chain, chain.links)
                dve.sem_inc(s_combined, 1)

            chain.count(nc.vector.memset(w.minus_quarter, -0.25))
            chain(nc.vector.memset(w.half_pi, PI / 2))
            dve.wait_ge(m.s_rows, 5 * 16)
            for l in range(NL):
                nc.vector.tensor_copy(w.ent_b_wide[:, l], w.ent_b[:, l, :].unsqueeze(2).broadcast_to([P, EW // P, P])
                                      ).then_inc(s_wide, 1)
            phase = w.rows[:, ROW_NAMES.index("phase00"):ROW_NAMES.index("phase00") + NL * PW, :]
            big = 12582912.0
            chain(nc.vector.tensor_scalar(w.phase_turns, phase, 0.5 / PI, big, ALU.mult, ALU.add))
            chain(nc.vector.tensor_scalar(w.phase_sin, w.phase_turns, -big, None, ALU.add))
            c1 = 6.28125
            c2 = float(np.float32(2 * np.pi - c1))
            chain(nc.vector.scalar_tensor_tensor(out=w.phase_turns, in0=w.phase_sin, scalar=-c1, in1=phase,
                                                 op0=ALU.mult, op1=ALU.add))
            chain(nc.vector.scalar_tensor_tensor(out=w.phase_turns, in0=w.phase_sin, scalar=-c2, in1=w.phase_turns,
                                                 op0=ALU.mult, op1=ALU.add))
            nc.vector.tensor_scalar(w.phase_turns, w.phase_turns, TURN_PI, -TURN_PI, ALU.min, ALU.max).then_inc(s_half, 1)
            dve.wait_ge(s_half, 1)
            nc.vector.scalar_tensor_tensor(out=w.phase_cos, in0=w.phase_turns, scalar=-1.0, in1=w.phase_turns,
                                           op0=ALU.mult, op1=ALU.max).then_inc(s_half, 1)
            dve.wait_ge(s_sin, 2)
            chain(nc.vector.tensor_tensor(w.mod, w.phase_sin, w.phase_cos, ALU.add))
            dve.wait_ge(m.s_path, 16 * (NL * PW + 2))
            for l in range(NL):
                step = 2 * l + 1
                for q in range(PW):
                    mod = w.mod[:, l * PW + q, :].unsqueeze(1).broadcast_to([P, KC, D])
                    target = w.lin[:, step] if q == 0 else w.scaled
                    chain(nc.vector.tensor_tensor(target, w.path[:, l * PW + q], mod, ALU.mult))
                chain(nc.vector.tensor_tensor(w.lin[:, step], w.lin[:, step], w.scaled, ALU.add))
                for c in range(KC):
                    part = w.lin[:, step, c, c * P:(c + 1) * P]
                    chain(nc.vector.tensor_tensor(part, part, m.ident[:, :], ALU.add))
                own = w.bias[:, 2 + step, :]
                chain(nc.vector.tensor_tensor(own, row(w, f"path_b{l}0"), w.mod[:, l * PW, :], ALU.mult))
                chain(nc.vector.tensor_tensor(w.scaled[:, 0, :], row(w, f"path_b{l}1"), w.mod[:, l * PW + 1, :],
                                              ALU.mult))
                chain(nc.vector.tensor_tensor(own, own, w.scaled[:, 0, :], ALU.add))
                step = 2 * l
                for c in range(KC):
                    dve.wait_ge(s_prod, 3 * l + c + 1)
                    chain(nc.vector.tensor_copy(w.lin[:, step, c, :], m.banks[:, 3 * l + c, 0:D]))
                    part = w.lin[:, step, c, c * P:(c + 1) * P]
                    chain(nc.vector.tensor_tensor(part, part, m.ident[:, :], ALU.add))
                dve.wait_ge(s_prod, 3 * l + 3)
                chain(nc.vector.tensor_tensor(w.bias[:, 2 + step, :], m.banks[:, 3 * l + 2, 0:D], row(w, f"ent_pb{l}"),
                                              ALU.add))
                combine(l)
            stats_all_vector(nc, m, wave, chain, BEGUN)
            chain(nc.vector.tensor_scalar(w.amp_ph[:, :, 0:D], w.amp_ph[:, :, 0:D], 0.5, None, ALU.mult))
            chain(nc.vector.tensor_scalar(w.bias[:, 0, :], row(w, "amp_b"), 0.5, None, ALU.mult))
            chain(nc.vector.tensor_copy(w.bias[:, 1, :], row(w, "ph_b")))
            for k in range(1, STEPS):
                nc.vector.tensor_copy(w.shift_wide[:, k - 1], w.shift_cols[:, k - 1, :].unsqueeze(2).broadcast_to([P, KC, P])
                                      ).then_inc(s_wide, 1)
            split_bias(nc, m, w, chain, slice(0, 2))
            for k in range(1, STEPS):
                dve.wait_ge(s_prod, 3 * NL + k)
                chain.count(nc.vector.tensor_tensor(w.bias[:, 2 + k, :], w.bias[:, 2 + k, :], m.banks[:, 4 + k, 0:D],
                                                    ALU.add))
            chain(nc.vector.tensor_scalar(w.rows[:, -2:, :], w.rows[:, -2:, :], 0.5, None, ALU.mult))
            apply_all_vector(nc, m, f, wave, dve, 0, BEGUN)
            combine(2)
            stats_all_vector(nc, m, wave, chain, range(2 * TB, 3 * TB))
            combine(3)

        @block.tensor
        def _(pe):
            pe.wait_ge(m.s_ent, 16 * 2 * NL)
            for l in range(NL):
                for c in range(KC):
                    for e in range(EW // P):
                        last = nc.tensor.matmul(m.banks[:, 3 * l + c, 0:D], w.ent_wT[:, l, e, c * P:(c + 1) * P],
                                                w.ent_pw[:, l, e, :], start=(e == 0), stop=(e == EW // P - 1))
                    last.then_inc(s_prod, 1)
                pe.wait_ge(s_wide, l + 1)
                for e in range(EW // P):
                    last = nc.tensor.matmul(m.banks[:, 3 * l + 2, 0:D], w.ent_b_wide[:, l, e, :], w.ent_pw[:, l, e, :],
                                            start=(e == 0), stop=(e == EW // P - 1))
                last.then_inc(s_prod, 1)
            for k in range(1, STEPS):
                pe.wait_ge(s_wide, NL + k)
                for c in range(KC):
                    last = nc.tensor.matmul(m.banks[:, 4 + k, 0:D], w.shift_wide[:, k - 1, c, :], w.lin[:, k, c, :],
                                            start=(c == 0), stop=(c == KC - 1))
                last.then_inc(s_prod, 1)
            wave_tensor_x(nc, m, w, f, wave, pe, 0, BEGUN)
    return w


ITEMS = STEPS * TILES
DEEP = 4
LAG = 2
BEGUN = range(TILES // 2)
REST = range(TILES // 2, TILES)


class WaveSems:

    def __init__(self, sem, name):
        self.stats = sem(f"{name}_x_variance_ready")
        self.x_rstd = sem(f"{name}_x_rstd_ready")
        self.xn = sem(f"{name}_x_normed")
        self.x_turned = sem(f"{name}_x_turned")
        self.xT = sem(f"{name}_x_T_ready")
        self.z = sem(f"{name}_z_ready")
        self.tanh = sem(f"{name}_tanh_ready")
        self.abs = sem(f"{name}_sine_argument_ready")
        self.sines = sem(f"{name}_sines_ready")
        self.u = sem(f"{name}_input_or_normed_ready")
        self.turned = sem(f"{name}_turned")
        self.uT = sem(f"{name}_turned_copied")
        self.lin = sem(f"{name}_linear_ready")
        self.square = sem(f"{name}_mean_square_ready")
        self.eps = sem(f"{name}_eps_added")
        self.rstd = sem(f"{name}_rstd_ready")
        self.shifted = sem(f"{name}_shift_added_to_x")


class WavePlaces:
    def __init__(self, m):
        area = m.w_dn
        self.u = flat(area, 0, (TILES, D))
        self.z = flat(area, 2048, (TILES, 2 * D))
        self.squares = [flat(area, 6144 + 256 * b, (D,)) for b in range(DEEP)]
        self.uT = [flat(area, 7168 + 256 * b, (KC, P)) for b in range(DEEP)]
        self.xn = flat(area, 8192, (TILES, D))
        self.p_turn = [m.banks[:, b, 0:KC * P].rearrange("p (c t) -> p c t", t=P) for b in range(DEEP)]
        self.p_lin = [m.banks[:, 4 + b, 0:D] for b in range(DEEP)]
        self.p_z = [m.banks[:, 4 + b, :] for b in range(DEEP)]


def turn_x(nc, m, f, s, eng, norms, t, banks):
    eng.wait_ge(s.xn, norms * TILES + (t + 1))
    for c in range(KC):
        last = nc.tensor.transpose(banks[t % DEEP][:, c, :], f.xn[:, t, c * P:(c + 1) * P], m.ident[:, :])
    last.then_inc(s.x_turned, 1)


def wave_tensor_x(nc, m, w, f, s, eng, ffn, tiles):
    norms = 2 * ffn

    def product_x(t):
        eng.wait_ge(s.xT, norms * TILES + (t + 1))
        if t >= DEEP:
            eng.wait_ge(s.tanh, ffn * TILES + (t - DEEP + 1))
        nc.tensor.matmul(f.p_z[t % DEEP], m.ones_b[:, :], w.bias_b[:, 0:2, :].rearrange("p a b -> p (a b)"),
                         start=True, stop=False)
        for c in range(KC):
            last = nc.tensor.matmul(f.p_z[t % DEEP], f.uT[t % DEEP][:, c, :], w.amp_ph[:, c, :],
                                    start=False, stop=(c == KC - 1))
        last.then_inc(s.z, 1)

    for p in range(tiles.start, tiles.stop + LAG):
        if p < tiles.stop:
            turn_x(nc, m, f, s, eng, norms, p, f.p_turn)
        if p - LAG >= tiles.start:
            product_x(p - LAG)


def wave_tensor(nc, m, w, f, s, eng, ffn, s_maps, tiles=range(TILES)):
    first_u = ffn * (TILES + ITEMS)
    wave_tensor_x(nc, m, w, f, s, eng, ffn, tiles)

    def turn_u(n, t):
        eng.wait_ge(s.u, n + (first_u + 1))
        for c in range(KC):
            last = nc.tensor.transpose(f.p_turn[t % DEEP][:, c, :], f.u[:, t, c * P:(c + 1) * P], m.ident[:, :])
        last.then_inc(s.turned, 1)

    def product_u(n, t, step):
        eng.wait_ge(s.uT, n + (ffn * ITEMS + 1))
        eng.wait_ge(s.u, n + (first_u + TILES - DEEP + 1))
        nc.tensor.matmul(f.p_lin[t % DEEP], m.ones_b[:, :], w.bias_b[:, step + 2, :], start=True, stop=False)
        for c in range(KC):
            last = nc.tensor.matmul(f.p_lin[t % DEEP], f.uT[t % DEEP][:, c, :], w.lin[:, step, c, :],
                                    start=False, stop=(c == KC - 1))
        last.then_inc(s.lin, 1)

    eng.wait_ge(s_maps, 1)
    in_steps(eng, [(0, turn_u), (LAG, with_turn(product_u))], ITEMS, TILES)


def wave_scalar_x(nc, w, f, s, eng, ffn, tiles):
    def copy_x(t):
        eng.wait_ge(s.x_turned, 2 * ffn * TILES + (t + 1))
        nc.scalar.copy(f.uT[t % DEEP], f.p_turn[t % DEEP]).then_inc(s.xT, 1)

    def tanh(t):
        eng.wait_ge(s.z, ffn * TILES + (t + 1))
        nc.scalar.activation(f.z[:, t, :], f.p_z[t % DEEP], ACT.Tanh).then_inc(s.tanh, 1)

    def argument(t):
        eng.wait_ge(s.tanh, ffn * TILES + (t + 1))
        nc.scalar.activation(f.z[:, t, D:2 * D], f.z[:, t, D:2 * D], ACT.Abs, bias=w.minus_quarter).then_inc(s.abs, 1)

    for p in range(tiles.start, tiles.stop + LAG + 1):
        if p in tiles:
            copy_x(p)
        if p - LAG in tiles:
            tanh(p - LAG)
        if p - LAG - 1 in tiles:
            argument(p - LAG - 1)


def wave_scalar(nc, m, w, f, s, eng, ffn, tiles=range(TILES)):
    wave_scalar_x(nc, w, f, s, eng, ffn, tiles)
    for t in range(TILES):
        eng.wait_ge(s.abs, ffn * TILES + (t + 1))
        nc.scalar.activation(f.z[:, t, D:2 * D], f.z[:, t, D:2 * D], ACT.Sin, scale=-PI, bias=w.half_pi
                             ).then_inc(s.sines, 1)

    def copy_u(n, t):
        eng.wait_ge(s.turned, n + (ffn * ITEMS + 1))
        nc.scalar.copy(f.uT[t % DEEP], f.p_turn[t % DEEP]).then_inc(s.uT, 1)

    def square(n, t):
        eng.wait_ge(s.lin, n + (ffn * ITEMS + 1))
        nc.scalar.activation(f.squares[t % DEEP], f.p_lin[t % DEEP], ACT.Square, scale=D ** -0.5,
                             accum_out=m.mv[:, t, 1:2]).then_inc(s.square, 1)

    in_steps(eng, [(0, copy_u), (LAG, square)], ITEMS, TILES)


def stats_all_vector(nc, m, s, chain, tiles):
    for t in tiles:
        chain.count(nc.vector.bn_stats(m.stats[:, t, :], m.x[:, t, :]))
    chain.engine.wait_ge(chain.sem, chain.links)
    for t in tiles:
        nc.vector.bn_aggr(m.mv[:, t, :], m.stats[:, t, :]).then_inc(s.stats, 1)


def apply_all_vector(nc, m, f, s, eng, norms, tiles=range(TILES)):
    for t in tiles:
        if t % 4 == 0:
            eng.wait_ge(s.stats, norms * TILES + t + 4)
            eng.wait_ge(s.x_rstd, norms * 2 + t // 4 + 1)
        nc.vector.tensor_scalar(f.xn[:, t, :], m.x[:, t, :], m.mv[:, t, 0:1], m.rstd[:, t:t + 1],
                                ALU.subtract, ALU.mult).then_inc(s.xn, 1)


def wave_vector(nc, m, w, f, s, eng, chain, ffn, meanwhile=None, s_out=None, tiles=range(TILES)):
    apply_all_vector(nc, m, f, s, eng, 2 * ffn, tiles)
    if meanwhile:
        meanwhile(chain)
    for t in range(TILES):
        eng.wait_ge(s.sines, ffn * TILES + (t + 1))
        nc.vector.scalar_tensor_tensor(out=f.u[:, t, :], in0=f.z[:, t, 0:D], scalar=1.0, in1=f.z[:, t, D:2 * D],
                                       op0=ALU.add, op1=ALU.mult).then_inc(s.u, 1)

    def normalise(n, t):
        eng.wait_ge(s.rstd, n + (ffn * ITEMS + 1))
        nc.vector.tensor_scalar(f.u[:, t, :], f.p_lin[t % DEEP], m.rstd[:, t:t + 1], None, ALU.mult).then_inc(s.u, 1)

    in_steps(eng, [(0, normalise)], ITEMS - TILES, TILES)
    eng.wait_ge(s.shifted, 2 * ffn + 1)
    before = (ffn + 1) * (TILES + ITEMS) - TILES
    added, read = {}, {}
    for p in range(TILES + 3):
        if p < TILES:
            eng.wait_ge(s.rstd, (ffn + 1) * ITEMS - TILES + p + 1)
            nc.vector.scalar_tensor_tensor(out=f.u[:, p, :], in0=f.p_lin[p % DEEP], scalar=m.rstd[:, p:p + 1],
                                           in1=row(w, "ln4_g1"), op0=ALU.mult, op1=ALU.mult).then_inc(s.u, 1)
        t = p - 1
        if 0 <= t < TILES:
            eng.wait_ge(s.u, before + t + 1)
            own = m.x[:, t, :]
            chain.count(nc.vector.tensor_tensor(own, own, f.u[:, t, :], ALU.add))
            added[t] = chain.links
            if s_out and t % 4 == 3:
                eng.wait_ge(chain.sem, chain.links)
                eng.sem_inc(s_out, 1)
        t = p - 2
        if not s_out and 0 <= t < TILES:
            eng.wait_ge(chain.sem, added[t])
            chain.count(nc.vector.bn_stats(m.stats[:, t, :], m.x[:, t, :]))
            read[t] = chain.links
        t = p - 3
        if not s_out and 0 <= t < TILES:
            eng.wait_ge(chain.sem, read[t])
            nc.vector.bn_aggr(m.mv[:, t, :], m.stats[:, t, :]).then_inc(s.stats, 1)


def root(nc, m, s, eng, eps_done, src, group, ready, done):
    eng.wait_ge(*ready)
    nc.gpsimd.tensor_tensor(m.var_eps[:, group], src, m.eps[:, group], ALU.add).then_inc(s.eps, 1)
    eng.wait_ge(s.eps, eps_done)
    nc.gpsimd.tensor_tensor(m.rstd[:, group], m.var_eps[:, group], m.minus_half[:, group], ALU.pow).then_inc(done, 1)


def norm_roots_pool(nc, m, s, eng, norms, halves):
    before = 2 * norms + (norms > 0) * ITEMS
    for h in halves:
        group = slice(4 * h, 4 * h + 4)
        root(nc, m, s, eng, before + h + 1, m.mv[:, group, 1], group, (s.stats, norms * TILES + 4 * h + 4), s.x_rstd)


def norm_all_pool(nc, m, s, eng, norms, vector, halves=range(2)):
    norm_roots_pool(nc, m, s, eng, norms, halves)
    eng.wait_ge(s.xn, (norms + 1) * TILES)
    nc.gpsimd.tensor_tensor(m.x[:, :, :], m.x[:, :, :], vector.unsqueeze(1).broadcast_to([P, TILES, D]), ALU.add
                            ).then_inc(s.shifted, 1)


def wave_pool(nc, m, w, s, eng, ffn, meanwhile=None, halves=range(2)):
    norm_all_pool(nc, m, s, eng, 2 * ffn, row(w, "ln4_b1"), halves)
    if meanwhile:
        meanwhile()
    before = 2 * (2 * ffn + 1) + ffn * ITEMS

    def rstd(n, t):
        root(nc, m, s, eng, n + (before + 1), m.mv[:, t, 1:2], slice(t, t + 1),
             (s.square, n + (ffn * ITEMS + 1)), s.rstd)

    in_steps(eng, [(0, rstd)], ITEMS, TILES)


def last_phase(nc, m, w, a, wave, sem):
    v_chain = sem("last_vector_chain")
    sa = AttnSems(sem, "attn2")
    s_maps = sem("step_maps_ready")
    s_pad, s_out, s_stored = sem("padding2_cleared"), sem("out_ready"), sem("out_stored")
    f = WavePlaces(m)
    area = m.w_gu[:, 0:8192]
    at = AttnPlaces(m, HKV, area, m.w_dn[:, 0:6144], flat(m.w_dn, 10240, (KC, TILES * P)), m.w_dn[:, 12288:16384],
                    w.qkv2, w.wo, w.qkv2_b)
    p_turn = [m.banks[:, 4 + b, 0:KC * P].rearrange("p (c t) -> p c t", t=P) for b in range(DEEP)]

    with nc.Block() as block:
        @block.scalar
        def _(act):
            wave_scalar(nc, m, w, f, wave, act, 0, REST)
            for t in range(TILES):
                act.wait_ge(wave.x_turned, TILES + t + 1)
                nc.scalar.copy(at.xnT[:, :, t * P:(t + 1) * P], p_turn[t % DEEP]).then_inc(wave.xT, 1)
            for t in range(TILES):
                attn_scalar_v(nc, m, sa, at, act, 0, t)
            attn_scalar(nc, m, sa, at, act, 0)
            wave_scalar(nc, m, w, f, wave, act, 1)

        @block.vector
        def _(dve):
            dve.wait_ge(w.s_small, 4 * 16)
            chain = Chain(dve, v_chain)
            stats_all_vector(nc, m, wave, chain, range(3 * TB, TILES))
            wave_vector(nc, m, w, f, wave, dve, chain, 0,
                        meanwhile=lambda chain: finish_maps(nc, m, w, dve, chain, s_maps), tiles=REST)
            dve.wait_ge(s_pad, 4)
            apply_all_vector(nc, m, f, wave, dve, 1)
            for t in range(0, TILES, 2):
                attn_vector_rope(nc, m, sa, at, dve, chain, 0, t)
            attn_vector(nc, m, sa, at, dve, chain, 0, None,
                        ahead=lambda: dve.wait_ge(wave.shifted, 2),
                        after=lambda t: stats_all_vector(nc, m, wave, chain, range(t, t + 2)))
            wave_vector(nc, m, w, f, wave, dve, chain, 1, s_out=s_out)

        @block.tensor
        def _(pe):
            wave_tensor(nc, m, w, f, wave, pe, 0, s_maps, REST)
            for t in range(TILES):
                if t >= DEEP:
                    pe.wait_ge(wave.xT, TILES + t - DEEP + 1)
                turn_x(nc, m, f, wave, pe, 1, t, p_turn)
            for t in range(TILES):
                attn_tensor_qkv(nc, m, sa, at, pe, (wave.xT, TILES + t + 1), t)
            attn_tensor(nc, m, sa, at, pe, 0)
            wave_tensor(nc, m, w, f, wave, pe, 1, s_maps)

        @block.gpsimd
        def _(pool):
            wave_pool(nc, m, w, wave, pool, 0, meanwhile=lambda: attn_padding(nc.gpsimd, at, s_pad, pool),
                      halves=range(1, 2))
            norm_all_pool(nc, m, wave, pool, 1, row(w, "bo"))
            wave_pool(nc, m, w, wave, pool, 1)

        @block.sync
        def _(sp):
            out = a["out"].rearrange("(t p) c -> p t c", p=P)
            for h in range(2):
                sp.wait_ge(s_out, h + 1)
                sp.dma_start(out[:, 4 * h:4 * h + 4, :], m.x[:, 4 * h:4 * h + 4, :]).then_inc(s_stored, 16)
            sp.wait_ge(s_stored, 32)


def build(nc, a):
    with ExitStack() as ctx:
        m = allocate(nc, ctx)

        def sem(name):
            return ctx.enter_context(nc.semaphore(name))

        m.norm, m.route, m.combine = NormSems(sem, "norm"), RouteSems(sem, "route"), CombineSems(sem, "combine")
        m.experts = ExpertSems(sem)
        m.s_ent, m.s_path, m.s_rows = (sem(f"{name}_weights_loaded") for name in ("entangling", "path", "vector"))
        first_phase(nc, m, a, sem)
        experts_phase(nc, m, a, 0)
        middle_phase(nc, m, a, sem)
        experts_phase(nc, m, a, 1)
        wave = WaveSems(sem, "wave")
        w = fold_phase(nc, m, a, wave, sem)
        last_phase(nc, m, w, a, wave, sem)



def shape_constants():
    i = np.arange(P)
    consts = np.concatenate([np.eye(P), i[:, None] < i[None, :], i[None, :] > i[:, None],
                             np.tile(np.arange(NE), (P, 1))], axis=1).astype(np.float32)
    inv_freq = (1.0 / np.float32(10000.0) ** (np.arange(0, DH, 2, dtype=np.float32) / np.float32(DH))).astype(np.float32)
    angle = np.arange(T, dtype=np.float32)[:, None] * inv_freq[None, :]
    cos, sin = np.cos(angle), np.sin(angle)
    tables = np.stack([np.concatenate([cos, cos], 1), np.concatenate([-sin, sin], 1)], 1)
    tables = np.stack([tables * DH ** -0.5, tables], 2)
    rope = tables.reshape(TB, P, 2, 2, DH).transpose(1, 0, 2, 3, 4).reshape(P, -1)
    return consts, rope.astype(np.float32)


def kernel(**inputs):
    import concourse.bacc as _bacc
    from concourse.bass_utils import run_bass_kernel_spmd as _run

    v = {k: np.asarray(x) for k, x in inputs.items()}
    consts, rope = shape_constants()
    ffn, at = "L1_ffn_", "L1_attn_"
    turn = np.concatenate([np.arange(0, DH, 2), np.arange(1, DH, 2)])
    heads_first = lambda x: x.reshape(*x.shape[:-1], -1, DH)[..., turn].reshape(x.shape)
    vectors = [v[ffn + "amp_b"], v[ffn + "ph_b"], *v[ffn + "ent_pb"], *v[ffn + "path_b"].reshape(NL * PW, D),
               *v[ffn + "phase"].reshape(NL * PW, D), v[at + "bo"], heads_first(v[at + "bq"]),
               v[ffn + "ln4_g"][-1], v[ffn + "ln4_b"][-1]]

    def columns(*names):
        return np.stack([v[ffn + n] for n in names], 1).reshape(NL, 2, KC, P).transpose(3, 0, 1, 2).reshape(P, -1)

    arrays = {
        "x": v["L0_attn_x"].reshape(TOK, D),
        "consts": consts,
        "rope": rope,
        "router": v["L0_ffn_gate_w"].T,
        "shared_gate": v["L0_ffn_shared_gate_w"].T,
        "shared_up": v["L0_ffn_shared_up_w"].T,
        "shared_down": v["L0_ffn_shared_down_w"].T,
        "gate_up": v["L0_ffn_gate_up_proj"].reshape(NE, KC, P, SHID).transpose(2, 0, 1, 3).reshape(P, -1),
        "down": v["L0_ffn_down_proj"].transpose(1, 0, 2).reshape(HID, -1),
        "qkv": v["L0_attn_w_qkv"].T,
        "proj": v["L0_attn_w_proj"].T,
        "ent_wT": v[ffn + "ent_w"].transpose(0, 2, 1),
        "ent_pw": v[ffn + "ent_pw"],
        "ent_b": v[ffn + "ent_b"].reshape(NL, EW // P, P).transpose(2, 0, 1).reshape(P, -1),
        "path_w": v[ffn + "path_w"].reshape(NL * PW, D, D),
        "amp_w": v[ffn + "amp_w"],
        "ph_w": v[ffn + "ph_w"],
        "rows": np.concatenate(vectors).reshape(1, -1),
        "gain_cols": columns("ln3_g", "ln4_g"),
        "shift_cols": columns("ln3_b", "ln4_b"),
        "kv_b": np.concatenate([heads_first(v[at + "bk"]), v[at + "bv"]]).reshape(1, -1),
        "Wq": heads_first(v[at + "Wq"]),
        "Wk": heads_first(v[at + "Wk"]),
        "Wv": v[at + "Wv"],
        "Wo": v[at + "Wo"],
    }
    nc = _bacc.Bacc("TRN2", target_bir_lowering=False, num_devices=1)
    sent, a = {}, {}
    for name, x in arrays.items():
        sent[f"in_{name}"] = np.ascontiguousarray(x)
        a[name] = nc.dram_tensor(f"in_{name}", sent[f"in_{name}"].shape, mybir.dt.from_np(x.dtype),
                                 kind="ExternalInput").ap()
    a["out"] = nc.dram_tensor("out_0", (TOK, D), F32, kind="ExternalOutput").ap()
    build(nc, a)
    r = _run(nc, [sent], core_ids=[0])
    return r.results[0]["out_0"].reshape(B, T, D)
```
